# Optimizing a Trainium2 kernel written in Bass

```python
import numpy as np
import jax
import jax.numpy as jnp

def _softmax(x, axis=-1):
    return jax.nn.softmax(x, axis=axis)

def _gelu(x):
    return jax.nn.gelu(x, approximate=True)

def _silu(x):
    return jax.nn.silu(x)

def _sigmoid(x):
    return jax.nn.sigmoid(x)

def _layernorm(x, axis=-1, eps=1e-05):
    m = jnp.mean(x, axis=axis, keepdims=True)
    v = jnp.var(x, axis=axis, keepdims=True)
    return (x - m) / jnp.sqrt(v + eps)

def _scatter_add(tgt, idx, src, axis=0):
    return tgt.at[idx].add(src)

def _segment_sum(src, seg, n):
    return jax.ops.segment_sum(src, seg, n)
kernel_name = 'mk_decoder_preln_d2_seqx_r8_31b36b'

def setup_inputs(seed: int=0):
    np.random.seed(seed)
    _w = jnp.asarray

    def _rec_inputs():
        import jax
        import jax.numpy as jnp
        _rk = jax.random.key(seed)
        x = 4.136e-05 + 0.9999 * jax.random.normal(jax.random.fold_in(_rk, 1), (2, 512, 128), jnp.float32)
        _lenS = 512 - jax.random.randint(jax.random.fold_in(_rk, 7), (2,), 0, max(1, 512 // 4) + 1, jnp.int32)
        _lenS2 = 77 - jax.random.randint(jax.random.fold_in(_rk, 8), (2,), 0, max(1, 77 // 4) + 1, jnp.int32)
        _ctx_2048P = jax.random.normal(jax.random.fold_in(_rk, 11), (2, 16, 256), jnp.float32)
        _ctx_2048c = jax.random.dirichlet(jax.random.fold_in(_rk, 511), 0.3 * jnp.ones((16,), jnp.float32), (2, 77))
        _ctx_2048t = jnp.einsum('bsk,bkd->bsd', _ctx_2048c, _ctx_2048P)
        _ctx_2048t = _ctx_2048t * jax.lax.rsqrt(jnp.mean(jnp.square(_ctx_2048t)) + 1e-12) * 0.953939
        ctx_2048 = -0.000392918 + 0.999932 * (_ctx_2048t + 0.3 * jax.random.normal(jax.random.fold_in(_rk, 611), (2, 77, 256), jnp.float32))
        _validS = jnp.arange(512)[None, :] < _lenS[:, None]
        _validS2 = jnp.arange(77)[None, :] < _lenS2[:, None]
        _causal = jnp.tril(jnp.ones((512, 512), dtype=bool))
        mask_BxS2_ik0 = jnp.where(jnp.broadcast_to(_validS2[:, :], (2, 77)), 0, 1).astype(jnp.int32)
        mask_BxS2_if0 = jnp.where(jnp.ones((2, 77), dtype=bool), 4, 0).astype(jnp.int32)
        return (x, ctx_2048, mask_BxS2_ik0, mask_BxS2_if0)
    x, ctx_2048, mask_BxS2_ik0, mask_BxS2_if0 = _rec_inputs()

    def _L0_attn_setup():
        import math
        import jax, jax.numpy as jnp
        import numpy as np
        N_HEADS = 16

        def _phi(x, rf, m):
            norms_sq = jnp.sum(x * x, axis=-1, keepdims=True)
            proj = jnp.einsum('bhtd,md->bhtm', x, rf)
            scale = jnp.exp(-norms_sq * 0.5) / math.sqrt(m)
            return jnp.concatenate([jnp.cos(proj), jnp.sin(proj)], axis=-1) * scale
        key = jax.random.key(seed)
        ks = jax.random.split(key, 6)
        B, T, D = (2, 512, 128)
        m, dh = (32, D // N_HEADS)
        x = jax.random.normal(ks[0], (B, T, D), dtype=jnp.float32)
        s = 1.0 / math.sqrt(D)
        wq = jax.random.normal(ks[1], (D, D), dtype=jnp.float32) * s
        wk = jax.random.normal(ks[2], (D, D), dtype=jnp.float32) * s
        wv = jax.random.normal(ks[3], (D, D), dtype=jnp.float32) * s
        wo = jax.random.normal(ks[4], (D, D), dtype=jnp.float32) * s
        rf = jax.random.normal(ks[5], (m, dh), dtype=jnp.float32) / math.sqrt(dh)
        return {'x': x, 'wq': wq, 'wk': wk, 'wv': wv, 'wo': wo, 'rf': rf}
    _L0_attn_all = _L0_attn_setup()
    _L0_attn_in = {k: v for k, v in _L0_attn_all.items() if k in ('wq', 'wk', 'wv', 'wo', 'rf')}
    del _L0_attn_all

    def _L0_xattn_setup():
        import jax, jax.numpy as jnp
        import numpy as np
        UNITS = 128
        NUM_HEADS = 8

        def _split_heads(x, n):
            B, S, D = x.shape
            return x.reshape(B, S, n, D // n).transpose(0, 2, 1, 3)
        key = jax.random.key(seed)
        k1, k2, k3 = jax.random.split(key, 3)
        B, S = (8, 128)
        memory = jax.random.normal(k1, (B, S, 2 * UNITS), dtype=jnp.float32)
        query = jax.random.normal(k2, (B, S, UNITS), dtype=jnp.float32)
        seq_mask = jax.random.randint(k3, (B, S), 0, 2, dtype=jnp.int32)
        b = jnp.zeros((1,), dtype=jnp.float32)
        return {'memory': memory, 'query': query, 'seq_mask': seq_mask, 'b': b}
    _L0_xattn_all = _L0_xattn_setup()
    _L0_xattn_in = {k: v for k, v in _L0_xattn_all.items() if k in ('b',)}
    del _L0_xattn_all

    def _L0_ffn_setup():
        import jax, jax.numpy as jnp
        import numpy as np
        QMAX = 127.0

        def _ste_round(v):
            return v + jax.lax.stop_gradient(jnp.round(v) - v)

        def _act_fake_quant(x, clip_factor):
            scale = jax.nn.sigmoid(clip_factor) * jnp.max(jnp.abs(x)) / QMAX
            return jnp.clip(_ste_round(x / scale), -QMAX - 1.0, QMAX) * scale

        def _weight_fake_quant(w):
            scale = jnp.max(jnp.abs(w), axis=1, keepdims=True) / QMAX
            return jnp.clip(_ste_round(w / scale), -QMAX - 1.0, QMAX) * scale
        key = jax.random.key(seed)
        k1, k2, k3, k4 = jax.random.split(key, 4)
        B, S, H, I = (8, 1024, 128, 352)
        return {'x': jax.random.normal(k1, (B, S, H), dtype=jnp.float32), 'clip_x': jnp.full((1,), 4.0, dtype=jnp.float32), 'clip_down': jnp.full((1,), 4.0, dtype=jnp.float32), 'w_gate': jax.random.normal(k2, (I, H), dtype=jnp.float32) * 0.02, 'w_up': jax.random.normal(k3, (I, H), dtype=jnp.float32) * 0.02, 'w_down': jax.random.normal(k4, (H, I), dtype=jnp.float32) * 0.02}
    _L0_ffn_all = _L0_ffn_setup()
    _L0_ffn_in = {k: v for k, v in _L0_ffn_all.items() if k in ('clip_x', 'clip_down', 'w_gate', 'w_up', 'w_down')}
    del _L0_ffn_all

    def _L1_attn_setup():
        import jax, jax.numpy as jnp
        import numpy as np
        B, S, E, H = (2, 256, 128, 16)
        key = jax.random.key(seed)
        k1, k2, k3, k4 = jax.random.split(key, 4)
        x = jax.random.normal(k1, (B, S, E), dtype=jnp.float32)
        Wq = jax.random.normal(k2, (E, E), dtype=jnp.float32) * E ** (-0.5)
        Wk = jax.random.normal(k3, (E, E), dtype=jnp.float32) * E ** (-0.5)
        Wv = jax.random.normal(k4, (E, E), dtype=jnp.float32) * E ** (-0.5)
        ln_gamma = jnp.ones((E,), dtype=jnp.float32)
        ln_beta = jnp.zeros((E,), dtype=jnp.float32)
        return {'x': x, 'Wq': Wq, 'Wk': Wk, 'Wv': Wv, 'ln_gamma': ln_gamma, 'ln_beta': ln_beta}
    _L1_attn_all = _L1_attn_setup()
    _L1_attn_in = {k: v for k, v in _L1_attn_all.items() if k in ('Wq', 'Wk', 'Wv', 'ln_gamma', 'ln_beta')}
    del _L1_attn_all

    def _L1_xattn_setup():
        import jax, jax.numpy as jnp
        import numpy as np
        B, L, P = (4, 512, 128)
        D_MODEL = 128
        D_GLOBAL = 256
        HEADDIM = 32
        EPSILON = 0.001
        RMS_EPS = 1e-05

        def rmsnorm(x, g, eps=RMS_EPS):
            var = jnp.mean(jnp.square(x), axis=-1, keepdims=True)
            return x * jax.lax.rsqrt(var + eps) * g

        def _hnet_depool(h, h_patch_full, patch_lens):
            h_patch = h_patch_full[..., :D_MODEL]
            bsz, plen = (h_patch.shape[0], h_patch.shape[1])
            seqlen = h.shape[1]
            logp = jnp.full((bsz, plen), -EPSILON, dtype=jnp.float32)
            bidx = jnp.cumsum(patch_lens, axis=1) - 1
            boundary_mask = jnp.zeros((bsz, seqlen), dtype=jnp.int32)
            boundary_mask = boundary_mask.at[jnp.arange(bsz)[:, None], bidx].set(1)
            dt = (-jnp.log(-jnp.expm1(logp))).astype(h_patch.dtype)
            x = h_patch / dt[..., None]
            n_heads = D_MODEL // HEADDIM
            A = -jnp.ones((n_heads,), dtype=jnp.float32)
            bcoef = jnp.exp(logp).astype(h_patch.dtype)
            x4 = x.reshape(bsz, plen, n_heads, HEADDIM)
            a = jnp.exp(dt[:, :, None] * A[None, None, :])
            u = (dt * bcoef)[:, :, None, None] * x4
            a_b = jnp.broadcast_to(a[..., None], u.shape)

            def comb(lft, rgt):
                aL, uL = lft
                aR, uR = rgt
                return (aL * aR, uL * aR + uR)
            _, s = jax.lax.associative_scan(comb, (a_b, u), axis=1)
            depool = s.reshape(bsz, plen, D_MODEL)
            plug = jnp.clip(jnp.cumsum(boundary_mask, axis=1) - 1, 0, plen - 1)
            depool_out = depool[jnp.arange(bsz)[:, None], plug]
            return depool_out + h
        key = jax.random.key(seed)
        k1, k2, k3, k4 = jax.random.split(key, 4)
        embeds = jax.random.normal(k1, (B, L, D_MODEL), dtype=jnp.float32)
        patch_embeds = jax.random.normal(k2, (B, P, D_GLOBAL), dtype=jnp.float32)
        patch_lens = jnp.full((B, P), L // P, dtype=jnp.int64)
        W_in = jax.random.normal(k3, (D_MODEL, D_MODEL), dtype=jnp.float32) * 0.02
        b_in = jnp.zeros((D_MODEL,), dtype=jnp.float32)
        g_res = jnp.ones((D_MODEL,), dtype=jnp.float32)
        g_init = jnp.ones((D_GLOBAL,), dtype=jnp.float32)
        return {'embeds': embeds, 'patch_embeds': patch_embeds, 'patch_lens': patch_lens, 'W_in': W_in, 'b_in': b_in, 'g_res': g_res, 'g_init': g_init}
    _L1_xattn_all = _L1_xattn_setup()
    _L1_xattn_in = {k: v for k, v in _L1_xattn_all.items() if k in ('W_in', 'b_in', 'g_res', 'g_init')}
    del _L1_xattn_all

    def _L1_ffn_setup():
        import jax, jax.numpy as jnp
        import numpy as np
        NUM_EXPERTS = 8
        CAPACITY = 512
        key = jax.random.key(seed)
        ks = jax.random.split(key, 5)
        dim, hidden = (128, 256)
        x = jax.random.normal(ks[0], (4, 512, dim), dtype=jnp.float32)
        wg = jax.random.normal(ks[1], (dim, NUM_EXPERTS), dtype=jnp.float32) * 0.02
        w1 = jax.random.normal(ks[2], (NUM_EXPERTS, dim, hidden), dtype=jnp.float32) * 0.02
        w3 = jax.random.normal(ks[3], (NUM_EXPERTS, dim, hidden), dtype=jnp.float32) * 0.02
        w2 = jax.random.normal(ks[4], (NUM_EXPERTS, hidden, dim), dtype=jnp.float32) * 0.02
        return {'x': x, 'wg': wg, 'w1': w1, 'w3': w3, 'w2': w2}
    _L1_ffn_all = _L1_ffn_setup()
    _L1_ffn_in = {k: v for k, v in _L1_ffn_all.items() if k in ('wg', 'w1', 'w3', 'w2')}
    del _L1_ffn_all
    return {'x': x, 'ctx_2048': ctx_2048, 'mask_BxS2_ik0': mask_BxS2_ik0, 'mask_BxS2_if0': mask_BxS2_if0, 'L0_attn_wq': _L0_attn_in['wq'], 'L0_attn_wk': _L0_attn_in['wk'], 'L0_attn_wv': _L0_attn_in['wv'], 'L0_attn_wo': _L0_attn_in['wo'], 'L0_attn_rf': _L0_attn_in['rf'], 'L0_xattn_b': _L0_xattn_in['b'], 'L0_ffn_clip_x': _L0_ffn_in['clip_x'], 'L0_ffn_clip_down': _L0_ffn_in['clip_down'], 'L0_ffn_w_gate': _L0_ffn_in['w_gate'], 'L0_ffn_w_up': _L0_ffn_in['w_up'], 'L0_ffn_w_down': _L0_ffn_in['w_down'], 'L1_attn_Wq': _L1_attn_in['Wq'], 'L1_attn_Wk': _L1_attn_in['Wk'], 'L1_attn_Wv': _L1_attn_in['Wv'], 'L1_attn_ln_gamma': _L1_attn_in['ln_gamma'], 'L1_attn_ln_beta': _L1_attn_in['ln_beta'], 'L1_xattn_W_in': _L1_xattn_in['W_in'], 'L1_xattn_b_in': _L1_xattn_in['b_in'], 'L1_xattn_g_res': _L1_xattn_in['g_res'], 'L1_xattn_g_init': _L1_xattn_in['g_init'], 'L1_ffn_wg': _L1_ffn_in['wg'], 'L1_ffn_w1': _L1_ffn_in['w1'], 'L1_ffn_w3': _L1_ffn_in['w3'], 'L1_ffn_w2': _L1_ffn_in['w2']}

def reference(x, ctx_2048, mask_BxS2_ik0, mask_BxS2_if0, L0_attn_wq, L0_attn_wk, L0_attn_wv, L0_attn_wo, L0_attn_rf, L0_xattn_b, L0_ffn_clip_x, L0_ffn_clip_down, L0_ffn_w_gate, L0_ffn_w_up, L0_ffn_w_down, L1_attn_Wq, L1_attn_Wk, L1_attn_Wv, L1_attn_ln_gamma, L1_attn_ln_beta, L1_xattn_W_in, L1_xattn_b_in, L1_xattn_g_res, L1_xattn_g_init, L1_ffn_wg, L1_ffn_w1, L1_ffn_w3, L1_ffn_w2):
    import jax
    import jax.numpy as jnp

    def _L0_attn_ref(x, wq, wk, wv, wo, rf):
        import math
        import jax, jax.numpy as jnp
        import numpy as np
        N_HEADS = 16

        def _phi(x, rf, m):
            norms_sq = jnp.sum(x * x, axis=-1, keepdims=True)
            proj = jnp.einsum('bhtd,md->bhtm', x, rf)
            scale = jnp.exp(-norms_sq * 0.5) / math.sqrt(m)
            return jnp.concatenate([jnp.cos(proj), jnp.sin(proj)], axis=-1) * scale
        B, T, D = x.shape
        H = N_HEADS
        Dh = D // H
        m = rf.shape[0]

        def heads(w):
            return (x @ w.T).reshape(B, T, H, Dh).transpose(0, 2, 1, 3)
        Q, K, V = (heads(wq), heads(wk), heads(wv))
        Qf = _phi(Q, rf, m)
        Kf = _phi(K, rf, m)
        KV = jnp.einsum('bhnd,bhnv->bhdv', Kf, V)
        QKV = jnp.einsum('bhnd,bhdv->bhnv', Qf, KV)
        K_sum = jnp.sum(Kf, axis=2)
        Z = jnp.maximum(jnp.einsum('bhnd,bhd->bhn', Qf, K_sum)[..., None], 1e-06)
        out = (QKV / Z).transpose(0, 2, 1, 3).reshape(B, T, D)
        return out @ wo.T

    def _L0_xattn_ref(memory, query, seq_mask, b):
        import jax, jax.numpy as jnp
        import numpy as np
        UNITS = 128
        NUM_HEADS = 8

        def _split_heads(x, n):
            B, S, D = x.shape
            return x.reshape(B, S, n, D // n).transpose(0, 2, 1, 3)
        H = NUM_HEADS
        depth = UNITS // H
        Q = _split_heads(query, H) * depth ** (-0.5)
        k_mem, v_mem = jnp.split(memory, 2, axis=2)
        K = _split_heads(k_mem, H)
        V = _split_heads(v_mem, H)
        logits = jnp.einsum('bhqd,bhkd->bhqk', Q, K) + b[0]
        mask = seq_mask.astype(jnp.float32)[:, None, None, :]
        logits = logits + -1e+30 * (1.0 - mask)
        weights = jax.nn.softmax(logits, axis=-1)
        out = jnp.einsum('bhqk,bhkd->bhqd', weights, V)
        B, _, S, _ = out.shape
        return out.transpose(0, 2, 1, 3).reshape(B, S, UNITS)

    def _L0_ffn_ref(x, clip_x, clip_down, w_gate, w_up, w_down):
        import jax, jax.numpy as jnp
        import numpy as np
        QMAX = 127.0

        def _ste_round(v):
            return v + jax.lax.stop_gradient(jnp.round(v) - v)

        def _act_fake_quant(x, clip_factor):
            scale = jax.nn.sigmoid(clip_factor) * jnp.max(jnp.abs(x)) / QMAX
            return jnp.clip(_ste_round(x / scale), -QMAX - 1.0, QMAX) * scale

        def _weight_fake_quant(w):
            scale = jnp.max(jnp.abs(w), axis=1, keepdims=True) / QMAX
            return jnp.clip(_ste_round(w / scale), -QMAX - 1.0, QMAX) * scale
        xq = _act_fake_quant(x, clip_x[0])
        gate = jnp.einsum('bsh,ih->bsi', xq, _weight_fake_quant(w_gate))
        up = jnp.einsum('bsh,ih->bsi', xq, _weight_fake_quant(w_up))
        h = _act_fake_quant(jax.nn.silu(gate) * up, clip_down[0])
        return jnp.einsum('bsi,hi->bsh', h, _weight_fake_quant(w_down))

    def _L1_attn_ref(x, Wq, Wk, Wv, ln_gamma, ln_beta):
        import jax, jax.numpy as jnp
        import numpy as np
        B, S, E, H = (2, 256, 128, 16)
        b, s, e = x.shape
        h = H
        d = e // h
        scale = e ** (-0.5)
        idx = jnp.arange(s, dtype=jnp.float32)
        dist_w = jnp.abs(idx[None, :] - idx[:, None]) / s
        q = (x @ Wq.T).reshape(b, s, h, d)
        k = (x @ Wk.T).reshape(b, s, h, d)
        v = (x @ Wv.T).reshape(b, s, h, d)
        attn = jnp.einsum('bqhd,bkhd->bhqk', q, k) * scale
        attn = attn * dist_w
        attn = jax.nn.softmax(attn, axis=-1)
        out = jnp.einsum('bhqk,bkhd->bqhd', attn, v).reshape(b, s, e)
        mu = jnp.mean(out, axis=-1, keepdims=True)
        var = jnp.var(out, axis=-1, keepdims=True)
        out = (out - mu) * jax.lax.rsqrt(var + 1e-05) * ln_gamma + ln_beta
        return out

    def _L1_xattn_ref(embeds, patch_embeds, patch_lens, W_in, b_in, g_res, g_init):
        import jax, jax.numpy as jnp
        import numpy as np
        B, L, P = (4, 512, 128)
        D_MODEL = 128
        D_GLOBAL = 256
        HEADDIM = 32
        EPSILON = 0.001
        RMS_EPS = 1e-05

        def rmsnorm(x, g, eps=RMS_EPS):
            var = jnp.mean(jnp.square(x), axis=-1, keepdims=True)
            return x * jax.lax.rsqrt(var + eps) * g

        def _hnet_depool(h, h_patch_full, patch_lens):
            h_patch = h_patch_full[..., :D_MODEL]
            bsz, plen = (h_patch.shape[0], h_patch.shape[1])
            seqlen = h.shape[1]
            logp = jnp.full((bsz, plen), -EPSILON, dtype=jnp.float32)
            bidx = jnp.cumsum(patch_lens, axis=1) - 1
            boundary_mask = jnp.zeros((bsz, seqlen), dtype=jnp.int32)
            boundary_mask = boundary_mask.at[jnp.arange(bsz)[:, None], bidx].set(1)
            dt = (-jnp.log(-jnp.expm1(logp))).astype(h_patch.dtype)
            x = h_patch / dt[..., None]
            n_heads = D_MODEL // HEADDIM
            A = -jnp.ones((n_heads,), dtype=jnp.float32)
            bcoef = jnp.exp(logp).astype(h_patch.dtype)
            x4 = x.reshape(bsz, plen, n_heads, HEADDIM)
            a = jnp.exp(dt[:, :, None] * A[None, None, :])
            u = (dt * bcoef)[:, :, None, None] * x4
            a_b = jnp.broadcast_to(a[..., None], u.shape)

            def comb(lft, rgt):
                aL, uL = lft
                aR, uR = rgt
                return (aL * aR, uL * aR + uR)
            _, s = jax.lax.associative_scan(comb, (a_b, u), axis=1)
            depool = s.reshape(bsz, plen, D_MODEL)
            plug = jnp.clip(jnp.cumsum(boundary_mask, axis=1) - 1, 0, plen - 1)
            depool_out = depool[jnp.arange(bsz)[:, None], plug]
            return depool_out + h
        h = rmsnorm(embeds, g_res)
        h = jnp.einsum('bld,ed->ble', h, W_in) + b_in
        h_patch = rmsnorm(patch_embeds, g_init)
        return _hnet_depool(h, h_patch, patch_lens)

    def _L1_ffn_ref(x, wg, w1, w3, w2):
        import jax, jax.numpy as jnp
        import numpy as np
        NUM_EXPERTS = 8
        CAPACITY = 512
        bz, slen, dim = x.shape
        xt = x.reshape(bz * slen, dim)
        scores = jax.nn.softmax(xt @ wg, axis=-1)
        top_scores, sel = jax.lax.top_k(scores.T, CAPACITY)
        token_idx = sel.reshape(-1)
        routed = xt[token_idx] * top_scores.reshape(-1, 1)
        routed = routed.reshape(NUM_EXPERTS, CAPACITY, dim)
        h = jax.nn.silu(jnp.einsum('ecd,edh->ech', routed, w1)) * jnp.einsum('ecd,edh->ech', routed, w3)
        routed_out = jnp.einsum('ech,ehd->ecd', h, w2).reshape(-1, dim)
        out = jnp.zeros_like(xt).at[token_idx].add(routed_out)
        return out.reshape(bz, slen, dim)
    x = x + _L0_attn_ref(_layernorm(x, axis=-1), L0_attn_wq, L0_attn_wk, L0_attn_wv, L0_attn_wo, L0_attn_rf)
    x = x + _L0_xattn_ref(ctx_2048, _layernorm(x, axis=-1), mask_BxS2_ik0, L0_xattn_b)
    x = x + _L0_ffn_ref(_layernorm(x, axis=-1), L0_ffn_clip_x, L0_ffn_clip_down, L0_ffn_w_gate, L0_ffn_w_up, L0_ffn_w_down)
    x = x + _L1_attn_ref(_layernorm(x, axis=-1), L1_attn_Wq, L1_attn_Wk, L1_attn_Wv, L1_attn_ln_gamma, L1_attn_ln_beta)
    x = x + _L1_xattn_ref(_layernorm(x, axis=-1), ctx_2048, mask_BxS2_if0, L1_xattn_W_in, L1_xattn_b_in, L1_xattn_g_res, L1_xattn_g_init)
    x = x + _L1_ffn_ref(_layernorm(x, axis=-1), L1_ffn_wg, L1_ffn_w1, L1_ffn_w3, L1_ffn_w2)
    return x

_drawn_inputs = setup_inputs


def setup_inputs(seed=0):
    import zlib

    import numpy as np

    out = dict(_drawn_inputs(seed))
    spreads = {'L1_attn_ln_gamma': (1.0, 0.548),
     'L1_attn_ln_beta': (0.0, 0.523),
     'L1_xattn_b_in': (0.0, 0.51),
     'L1_xattn_g_res': (1.0, 0.6),
     'L1_xattn_g_init': (1.0, 0.2)}
    factors = {'L0_ffn_w_gate': 8.0,
     'L0_ffn_w_up': 8.0,
     'L0_ffn_w_down': 8.0,
     'L1_attn_Wq': 7.509,
     'L1_attn_Wk': 7.211,
     'L1_ffn_wg': 8.0,
     'L1_ffn_w1': 8.0,
     'L1_ffn_w3': 8.0,
     'L1_ffn_w2': 8.0}
    for name, (base, spread) in spreads.items():
        noise = np.random.default_rng([zlib.crc32(name.encode()), seed]).standard_normal(out[name].shape)
        drawn = base * np.exp(spread * noise) if base else spread * noise
        out[name] = jnp.asarray(drawn.astype(out[name].dtype))
    for name, factor in factors.items():
        out[name] = (out[name] * factor).astype(out[name].dtype)
    return out
```

```python
import math
from contextlib import ExitStack

import numpy as np

import concourse.bass as bass
import concourse.mybir as mybir

ACT = mybir.ActivationFunctionType
ALU = mybir.AluOpType
AX = mybir.AxisListType
F32 = mybir.dt.float32
BF16 = mybir.dt.bfloat16
I32 = mybir.dt.int32

P = 128
B = 2
S = 512
D = 128
NT = B * S // P
TB = NT // B
H16, DH8 = 16, 8
M_RF = 32
FC = H16 * M_RF // P
HX, DX = 8, 16
SC = 77
CTX = 256
FF = 352
NFC = (FF + P - 1) // P
FFL = FF - (NFC - 1) * P
NE, HID, CAP = 8, 256, 512
EPS = 1e-5
MAGIC = 1.5 * 2.0 ** 23
QMAX = 127.0
TWO_PI = 6.2831850
DT = -math.log(-math.expm1(-0.001))
DECAY = math.exp(-DT)
BCOEF = math.exp(-0.001)
W9 = DH8 + 1
W17 = DX + 1
TERMS_Q = (0, 0, 1, 0, 2, 1)
TERMS_K = (0, 1, 0, 2, 0, 1)
NTERM = len(TERMS_Q)
KS = NTERM * DH8
SEL_J = 16
SEL_SHIFTS = (26, 22, 18, 14, 10, 6, 2, -2)

CONST = {}
_at = 0
for _name, _n in (("ident", P), ("halfpi", 1), ("eps", 1), ("iota_p", 1), ("bd16", H16), ("bd8", HX), ("bd4", 4),
                  ("rowsel", P), ("group", P), ("lmat", SC), ("tri", SC), ("ones", P),
                  ("dist", 2 * S - P), ("iota_l", S)):
    CONST[_name] = (_at, _at + _n)
    _at += _n
NCONST = _at


def constants():
    c = np.zeros((P, NCONST), np.float32)
    p = np.arange(P)

    def put(name, a):
        lo, hi = CONST[name]
        c[:a.shape[0], lo:hi] = a
    put("ident", np.eye(P))
    put("halfpi", np.full((P, 1), math.pi / 2))
    put("eps", np.full((P, 1), EPS))
    put("iota_p", p[:, None])
    put("bd16", p[:, None] // DH8 == np.arange(H16)[None])
    put("bd8", (p[:, None] // DX == np.arange(HX)[None]) * DX ** -0.5)
    put("bd4", p[:, None] // M_RF == np.arange(4)[None])
    put("rowsel", p[None] // SEL_J == np.arange(NE)[:, None])
    put("group", p[:, None] // SEL_J == p[None] // SEL_J)
    s = np.arange(SC)
    lag = s[None] - s[:, None]
    put("lmat", np.where(lag >= 0, DECAY ** np.maximum(lag, 0).astype(np.float64), 0.0))
    put("tri", lag >= 0)
    put("ones", np.ones((P, P)))
    put("dist", np.abs(p[:, None] - (np.arange(2 * S - P)[None] - (S - P))) / S * D ** -0.5)
    put("iota_l", np.tile(np.arange(S)[None], (P, 1)))
    return c


def build(nc, x_in, ctx_in, ctxkT_in, xmask_in, lens_in, wqkv0_in, wqk0_in, wo0_in, rf_in, bias0_in, clips_in,
          wgu_in, wd_in, wqkv1_in, gamma_in, beta_in, win_in, bin_in, gres_in, ginit_in,
          wg_in, w1_in, w3_in, w2_in, const_in, jbits_in, out, parts_dram):
    with ExitStack() as ctx:
        def sb(name, shape, dt=F32):
            return ctx.enter_context(nc.sbuf_tensor(name, shape, dt))

        def sem(name):
            return ctx.enter_context(nc.semaphore(name))

        psum = ctx.enter_context(nc.psum_tensor("psum", [P, 8, 512], F32))
        const = sb("const", [P, NCONST])

        def cst(name, rows=P):
            lo, hi = CONST[name]
            return const[0:rows, lo:hi]

        x = sb("x", [P, NT, D])
        y = sb("y", [P, NT, D])
        yT = sb("yT", [P, NT * P])
        tmp = sb("tmp", [P, NT, D])
        arena = sb("arena", [P, 5 * NT * P])
        stats = sb("stats", [P, NT, 6])
        mv = sb("mv", [P, NT, 2])
        std = sb("std", [P, NT])
        rstd = sb("rstd", [P, NT])
        rms = sb("rms", [P, NT])
        ident_bf = sb("ident_bf", [P, P], BF16)
        wqkv0 = sb("wqkv0", [P, 3 * D])
        wqk0 = sb("wqk0", [P, 2, D])
        wo0 = sb("wo0", [P, D])
        rf = sb("rf", [P, M_RF])
        rf_bd = sb("rf_bd", [P, H16, M_RF])
        wf = sb("wf", [P, 2, 512])
        sq = sb("sq", [P, 2, 2 * D])
        nsq = sb("nsq", [P, NT, 2 * H16])
        fscale = sb("fscale", [P, NT, 2 * H16])
        v_tok = tmp
        vext0 = sb("vext0", [P, NT, H16, W9])
        big = sb("big", [P, 16384])
        kfeat = big[:, 0:8192].rearrange("p (t s n) -> p t s n", t=NT, s=2)
        qfeat = big[:, 8192:16384].rearrange("p (c s n) -> p c s n", c=FC, s=2)
        ring = sb("ring", [P, 8, 512])
        turns, frac, fabs = ring[:, 0:2, :], ring[:, 2:5, :], ring[:, 5:8, :]
        kv_bd = sb("kv_bd", [P, B, 2 * FC, 4, W9])
        zden = sb("zden", [P, TB, H16])
        zrec = sb("zrec", [P, TB, H16])
        zfac = sb("zfac", [P, TB, H16])
        oT = yT
        ctx_sb = sb("ctx_sb", [SC, B, CTX])
        ctxkT = sb("ctxkT", [P, B, SC])
        kx_bd = sb("kx_bd", [P, B, HX, SC])
        vx = sb("vx", [SC, B, HX, W17])
        xmask_i = sb("xmask_i", [P, B * SC], I32)
        xmask_f = sb("xmask_f", [P, B * SC])
        xbias = sb("xbias", [P, B, SC])
        bias0 = sb("bias0", [P, 1])
        lx = big[:, 0:2 * HX * SC].rearrange("p (k h n) -> p k h n", k=2, h=HX)
        nmx = sb("nmx", [P, 2, HX])
        pxT = big[0:SC, 2048:2048 + 2 * HX * P].rearrange("p (k n) -> p k n", k=2)
        xrec = sb("xrec", [P, HX])
        clips = sb("clips", [1, 2])
        clipe = sb("clipe", [1, 2])
        clipf = sb("clipf", [1, 2])
        wgu = sb("wgu", [P, 2 * NFC * P + FF])
        wmax = sb("wmax", [P, 2 * NFC + 1])
        wscale = sb("wscale", [P, 2 * NFC + 1])
        winv = sb("winv", [P, 2 * NFC + 1])
        wq_bf = sb("wq_bf", [P, 2 * NFC * P + FF], BF16)
        wguT = sb("wguT", [P, 2 * NFC * P], BF16)
        wdT = sb("wdT", [P, NFC * P], BF16)
        wdrow = sb("wdrow", [1, P])
        wdscale = sb("wdscale", [P, P])
        amax = sb("amax", [P, 2])
        hmax = sb("hmax", [P, 2 * NFC])
        gmax = sb("gmax", [1, 2])
        gsc = sb("gsc", [1, 2, 2])
        act_sc = sb("act_sc", [P, 2, 2])
        iscale = sb("iscale", [P, 2 * NFC])
        xq = big[:, 4096:4608].bitcast(BF16)
        xqT = big[:, 4608:5120].bitcast(BF16)
        hf = arena[:, 0:NFC * NT * P].rearrange("p (c n) -> p c n", c=NFC)
        hq = arena[:, NFC * NT * P:].bitcast(BF16)[:, 0:NFC * NT * P].rearrange("p (c n) -> p c n", c=NFC)
        sg = sb("sg", [P, 4, 512])
        wqkv1 = sb("wqkv1", [P, 3 * D])
        heads = big[0:KS, :].bitcast(BF16).rearrange("p (w h b n) -> p w (h b n)", w=2, h=H16, b=B)
        resid = arena[:, 0:2 * NT * P].rearrange("p (w n) -> p w n", w=2)
        part = arena[:, 2 * NT * P:].bitcast(BF16).rearrange("p (w k n) -> p w k n", w=2, k=3)
        vext1 = sb("vext1", [P, TB, H16, B, W9])
        tw = sg
        tmax = sb("tmax", [P, 4])
        pT = ring[:, 0:4, :]
        oraw = vext0
        gamma = sb("gamma", [P, D])
        beta = sb("beta", [P, D])
        win = sb("win", [P, D])
        bin_row = sb("bin_row", [1, D])
        gres = sb("gres", [P, 1])
        ginit = sb("ginit", [SC, D])
        lens_i = sb("lens_i", [SC, B], I32)
        lens_f = sb("lens_f", [SC, B])
        bidx = sb("bidx", [SC, 2, B])
        bhit = arena[0:SC, 0:2 * S].rearrange("p (b n) -> p b n", b=B)
        bmask = arena[0:SC, 2 * S:3 * S]
        bcum = arena[0:SC, 3 * S:4 * S]
        onehot = sb("onehot", [SC, B, S])
        csum = sb("csum", [SC, B])
        csq = sb("csq", [SC, CTX])
        upd = sb("upd", [SC, B, D])
        depool = sb("depool", [SC, B, D])
        zeros = arena[0:SC, 4 * S:5 * S]
        wg = sb("wg", [P, NE])
        w1 = sb("w1", [P, 2, HID])
        w3 = sb("w3", [P, 2, HID])
        w2 = sb("w2", [P, 2, 2, D])
        smx = sb("smx", [P, NT])
        lg = sb("lg", [P, NT, NE])
        sc8 = sb("sc8", [P, NT, NE])
        sT = sb("sT", [NE, NT * P])
        sbc = big[:, 0:NT * P]
        selw = big[:, NT * P:4 * NT * P].rearrange("p (k n) -> p k n", k=3)
        jbits = sb("jbits", [P, len(SEL_SHIFTS)], I32)
        thr = sb("thr", [P, 1], I32)
        cand = sb("cand", [P, 1], I32)
        cnt = sb("cnt", [P, 2])
        flag = sb("flag", [P, 1], BF16)
        digit = sb("digit", [P, 1], I32)
        need = sb("need", [P, 1])
        group_bf = sb("group_bf", [P, P], BF16)
        selmask = big[:, 4 * NT * P:5 * NT * P]
        smask = sb("smask", [P, NT, NE])
        ys = big[:, 5 * NT * P:7 * NT * P].rearrange("p (k t d) -> p k t d", k=2, t=NT)
        ysT = big[:, 7 * NT * P:9 * NT * P].rearrange("p (k n) -> p k n", k=2)
        hmoe = big[:, 9 * NT * P:11 * NT * P].rearrange("p (k n) -> p k n", k=2)

        in_x = sem("in_x")
        in_names = ["const_a", "const_b", "wqkv0", "wqk0", "wo0", "rf", "ctx", "ctxkT", "xmask", "bias0", "clips", "wgu",
                    "wqkv1", "gb", "win", "lens", "wg", "jbits"]
        loaded = {n: sem("in_" + n) for n in in_names}
        var_ready, std_ready, y_ready, yT_psum, yT_ready = (sem(n) for n in ("var_ready", "std_ready", "y_ready", "yT_psum", "yT_ready"))
        VAR0 = (0, 1, 2, 3, 4, 6)
        YT0 = (0, 2, None, 4, 6, 8)
        s = {n: sem(n) for n in (
            "dve_chain act_chain pool_chain identbf_ready rfbd_ready wf_psum wf_ready qkv_psum sq_ready v_ready nsq_ready fexp_ready vext_ready "
            "proj_psum frac_ready fabs_ready feat_ready kv_psum kv_ready qkvo_psum o_ready oT_psum oT_ready wo_psum "
            "x0_ready kx_ready vx_ready xb_ready sx_psum lx_ready px_ready pxT_psum pxT_ready ox_psum ox_used x1_ready "
            "clip_exp wq_ready wT_psum wT_ready wdrow_psum wdrow_ready wdb_psum "
            "amax_ready amaxT_psum gsc_ready gscb_psum act_ready xq_ready xqT_psum xqT_ready gu_psum sg_ready hf_ready "
            "hmax_ready hmaxT_psum gsh_ready gshb_psum hq_ready down_psum x2_ready "
            "q1_psum part1_ready resid1_ready part2_ready part3_ready v1_psum vext1_ready parts_stored heads_loaded "
            "scores_psum tw_ready shifted_ready t_psum p_ready pv_done wdb_used oraw_ready lno_var lno_std x3_ready "
            "len_ready cs_psum hit_ready cnt_psum csq_ready cstd_ready upd_ready dep_psum dep_ready wing_ready onehot_ready e_psum "
            "x4_ready lg_psum lgm_ready lge_ready s_ready sT_psum sT_ready sbc_psum sbc_ready flag_ready digit_psum "
            "selmask_ready smaskT_psum smask_ready ys_ready ysT_psum ysT_ready ab_psum silu_ready h_ready "
            "w2_psum acc_done x5_ready out_done").split()}

        w_in = [sem(f"w_in{k}") for k in range(2)]


        bank = [psum[:, i, :] for i in range(8)]

        block = ctx.enter_context(nc.Block())

        @block.sync
        def _(sp):
            n_a = CONST["bd4"][1]
            sp.dma_start(x[:, 0:TB, :], x_in[0].rearrange("(t p) d -> p t d", p=P)).then_inc(in_x, 16)
            sp.dma_start(x[:, TB:NT, :], x_in[1].rearrange("(t p) d -> p t d", p=P)).then_inc(in_x, 16)
            sp.dma_start(const[:, 0:n_a], const_in[:, 0:n_a]).then_inc(loaded["const_a"], 16)
            sp.dma_start(rf[:, :], rf_in).then_inc(loaded["rf"], 16)
            sp.dma_start(wqkv0[:, :], wqkv0_in).then_inc(loaded["wqkv0"], 16)
            sp.dma_start(wqk0[:, :, :], wqk0_in).then_inc(loaded["wqk0"], 16)
            sp.dma_start(const[:, n_a:], const_in[:, n_a:]).then_inc(loaded["const_b"], 16)
            sp.dma_start(wo0[:, :], wo0_in).then_inc(loaded["wo0"], 16)
            sp.dma_start(ctxkT[:, :, :], ctxkT_in).then_inc(loaded["ctxkT"], 16)
            sp.dma_start(ctx_sb[:, :, :], ctx_in.rearrange("b s c -> s b c")).then_inc(loaded["ctx"], 16)
            sp.dma_start(xmask_i[:, :], xmask_in.rearrange("(a n) -> a n", a=1).to_broadcast([P, B * SC])).then_inc(loaded["xmask"], 16)
            sp.dma_start(bias0[:, :], bias0_in.rearrange("(a n) -> a n", a=1).to_broadcast([P, 1])).then_inc(loaded["bias0"], 16)
            sp.dma_start(clips[:, :], clips_in).then_inc(loaded["clips"], 16)
            sp.dma_start(lens_i[:, :], lens_in).then_inc(loaded["lens"], 16)
            sp.dma_start(wgu[:, 0:2 * NFC * P].rearrange("p (c n) -> p c n", n=P),
                         wgu_in.rearrange("(c p) n -> p c n", p=P)).then_inc(loaded["wgu"], 16)
            sp.dma_start(wgu[:, 2 * NFC * P:], wd_in).then_inc(loaded["wgu"], 16)
            sp.dma_start(wqkv1[:, :], wqkv1_in).then_inc(loaded["wqkv1"], 16)

            def rows(v, n, r=P):
                return v.rearrange("(a n) -> a n", a=1).to_broadcast([r, n])
            sp.dma_start(gamma[:, :], rows(gamma_in, D)).then_inc(loaded["gb"], 16)
            sp.dma_start(beta[:, :], rows(beta_in, D)).then_inc(loaded["gb"], 16)
            sp.dma_start(win[:, :], win_in).then_inc(loaded["win"], 16)
            sp.dma_start(gres[:, :], gres_in).then_inc(loaded["win"], 16)
            sp.dma_start(bin_row[:, :], rows(bin_in, D, 1)).then_inc(loaded["win"], 16)
            sp.dma_start(ginit[:, :], rows(ginit_in[0:D], D, SC)).then_inc(loaded["win"], 16)
            sp.dma_start(wg[:, :], wg_in).then_inc(loaded["wg"], 16)
            sp.dma_start(jbits[:, :], jbits_in).then_inc(loaded["jbits"], 16)

            for n in range(3):
                sp.wait_ge((s["part1_ready"], s["part2_ready"], s["part3_ready"])[n], 4)
                for w in range(2):
                    sp.dma_start(parts_dram[w, n], part[:, w, n, :]).then_inc(s["parts_stored"], 16)
            sp.wait_ge(s["parts_stored"], 6 * 16)
            for i in range(NTERM):
                for w, terms in ((0, TERMS_Q), (1, TERMS_K)):
                    sp.dma_start(heads[DH8 * i:DH8 * (i + 1), w, :].rearrange("d (h n) -> d h n", h=H16),
                                 parts_dram[w, terms[i]].rearrange("(h d) n -> d h n", h=H16)).then_inc(s["heads_loaded"], 16)
            for e in range(NE):
                if e >= 2:
                    sp.wait_ge(s["w2_psum"], 2 * (e - 1))
                sp.dma_start(w1[:, e % 2, :], w1_in[e]).then_inc(w_in[e % 2], 16)
                sp.dma_start(w3[:, e % 2, :], w3_in[e]).then_inc(w_in[e % 2], 16)
                sp.dma_start(w2[:, e % 2, :, :], w2_in[e].rearrange("(c p) d -> p c d", p=P)).then_inc(w_in[e % 2], 16)
            sp.wait_ge(s["x5_ready"], 2)
            for b in range(B):
                sp.dma_start(out[b].rearrange("(t p) d -> p t d", p=P), x[:, TB * b:TB * (b + 1), :]).then_inc(s["out_done"], 16)
            sp.wait_ge(s["out_done"], 32)

        @block.tensor
        def _(pe):
            ident = cst("ident")

            def transpose_y(i):
                for b in range(B):
                    for t in range(TB * b, TB * b + TB):
                        pe.wait_ge(y_ready, NT * i + t + 1)
                        last = pe.transpose(bank[b][:, (t % TB) * P:(t % TB + 1) * P], y[:, t, :], ident)
                    last.then_inc(yT_psum, 1)

            pe.wait_ge(loaded["const_a"], 16)
            pe.wait_ge(loaded["wqk0"], 16)
            pe.wait_ge(s["rfbd_ready"], 1)
            for w in range(2):
                pe.matmul(bank[4 + w], lhsT=wqk0[:, w, :], rhs=rf_bd[:, :, :], start=True, stop=True).then_inc(s["wf_psum"], 1)
            transpose_y(0)
            pe.wait_ge(loaded["wqkv0"], 16)
            for t in range(NT):
                if t % TB == 0:
                    pe.wait_ge(yT_ready, YT0[0] + t // TB + 1)
                if t >= 2:
                    pe.wait_ge(s["v_ready"], t - 1)
                pe.matmul(bank[2 + t % 2][:, 0:3 * D], lhsT=yT[:, t * P:(t + 1) * P], rhs=wqkv0[:, :],
                          start=True, stop=True).then_inc(s["qkv_psum"], 1)
            pe.wait_ge(s["wf_ready"], 2)
            for u in range(16):
                if u >= 4:
                    pe.wait_ge(s["frac_ready"], u - 3)
                if u < NT:
                    l, r = yT[:, u * P:(u + 1) * P], wf[:, 1, :]
                else:
                    b, c = divmod(u - NT, FC)
                    l, r = wf[:, 0, c * P:(c + 1) * P], yT[:, b * S:(b + 1) * S]
                pe.matmul(bank[4 + u % 4], lhsT=l, rhs=r, start=True, stop=True).then_inc(s["proj_psum"], 1)
            pe.wait_ge(s["vext_ready"], 2)
            for b in range(B):
                pe.wait_ge(s["feat_ready"], 2 * TB * (b + 1))
                for f in range(2):
                    for c in range(FC):
                        for t in range(TB * b, TB * b + TB):
                            last = pe.matmul(bank[2 + b][:, (f * FC + c) * 36:(f * FC + c + 1) * 36],
                                             lhsT=kfeat[:, t, f, c * P:(c + 1) * P], rhs=vext0[:, t, 4 * c:4 * c + 4, :],
                                             start=(t == TB * b), stop=(t == TB * b + TB - 1))
                last.then_inc(s["kv_psum"], 1)
            pe.wait_ge(s["frac_ready"], 16)
            for b in range(B):
                pe.wait_ge(s["kv_ready"], b + 1)
                pe.wait_ge(s["feat_ready"], 2 * (NT + FC * (b + 1)))
                if b:
                    pe.wait_ge(s["o_ready"], 1)
                for t in range(TB * b, TB * b + TB):
                    for c in range(FC):
                        for f in range(2):
                            last = pe.matmul(bank[4 + t % TB][:, c * 36:(c + 1) * 36], lhsT=qfeat[:, c, f, t * P:(t + 1) * P],
                                             rhs=kv_bd[:, b, f * FC + c, :, :], start=(f == 0), stop=(f == 1))
                last.then_inc(s["qkvo_psum"], 1)
            pe.wait_ge(loaded["wo0"], 16)
            for b in range(B):
                pe.wait_ge(s["o_ready"], b + 1)
                for t in range(TB * b, TB * b + TB):
                    last = pe.transpose(bank[b][:, (t % TB) * P:(t % TB + 1) * P], tmp[:, t, :], ident)
                last.then_inc(s["oT_psum"], 1)
            for b in range(B):
                pe.wait_ge(s["oT_ready"], b + 1)
                for t in range(TB * b, TB * b + TB):
                    last = pe.matmul(bank[2 + b][:, (t % TB) * D:(t % TB + 1) * D], lhsT=oT[:, t * P:(t + 1) * P], rhs=wo0[:, :],
                                     start=True, stop=True)
                last.then_inc(s["wo_psum"], 1)

            pe.wait_ge(loaded["const_b"], 16)
            pe.wait_ge(s["identbf_ready"], 1)
            pe.wait_ge(s["wq_ready"], 1)
            wps = bank[6].bitcast(BF16)
            for c in range(2 * NFC):
                last = pe.transpose(wps[:, c * P:(c + 1) * P], wq_bf[:, c * P:(c + 1) * P], ident_bf[:, :])
            last.then_inc(s["wT_psum"], 1)
            wps = bank[7].bitcast(BF16)
            for c in range(NFC):
                n = P if c < NFC - 1 else FFL
                at = 2 * NFC * P + c * P
                last = pe.transpose(wps[0:n, c * P:(c + 1) * P], wq_bf[:, at:at + n], ident_bf[:, :])
            last.then_inc(s["wT_psum"], 1)
            pe.wait_ge(s["wT_ready"], 2)
            pe.transpose(bank[6][0:1, 0:P], wscale[:, 2 * NFC:2 * NFC + 1], ident).then_inc(s["wdrow_psum"], 1)
            pe.wait_ge(s["wdrow_ready"], 1)
            pe.matmul(bank[7][:, 0:P], lhsT=cst("ones", 1), rhs=wdrow[:, :], start=True, stop=True).then_inc(s["wdb_psum"], 1)

            pe.wait_ge(loaded["const_b"], 16)
            pe.wait_ge(s["len_ready"], 1)
            pe.matmul(bank[6][0:SC, 0:B], lhsT=cst("tri", SC), rhs=lens_f[:, :], start=True, stop=True).then_inc(s["cs_psum"], 1)
            for b in range(B):
                pe.wait_ge(s["hit_ready"], b + 1)
                pe.matmul(bank[6 + b][0:SC, :], lhsT=cst("ones", SC)[:, 0:SC], rhs=bhit[:, b, :],
                          start=True, stop=True).then_inc(s["cnt_psum"], 1)
            pe.wait_ge(s["onehot_ready"], 2)
            pe.wait_ge(s["upd_ready"], 1)
            pe.matmul(bank[6][0:SC, 0:B * D], lhsT=cst("lmat", SC), rhs=upd[:, :, :], start=True, stop=True).then_inc(s["dep_psum"], 1)

            transpose_y(1)
            pe.wait_ge(s["kx_ready"], 1)
            pe.wait_ge(s["vx_ready"], 2)

            def x_scores(t):
                if t % TB == 0:
                    pe.wait_ge(yT_ready, YT0[1] + t // TB + 1)
                if t >= 2:
                    pe.wait_ge(s["lx_ready"], t - 1)
                for g in range(2):
                    last = pe.matmul(bank[2 + 2 * (t % 2) + g][:, 0:4 * SC], lhsT=yT[:, t * P:(t + 1) * P],
                                     rhs=kx_bd[:, t // TB, 4 * g:4 * g + 4, :], start=True, stop=True)
                last.then_inc(s["sx_psum"], 1)

            pe.wait_ge(s["dep_ready"], 1)
            x_scores(0)
            for t in range(NT):
                if t + 1 < NT:
                    x_scores(t + 1)
                pe.wait_ge(s["px_ready"], t + 1)
                if t >= 1:
                    pe.wait_ge(s["pxT_ready"], t)
                for h in range(HX):
                    last = pe.transpose(bank[6 + h // 4][0:SC, (h % 4) * P:(h % 4 + 1) * P], lx[:, t % 2, h, :], ident)
                last.then_inc(s["pxT_psum"], 1)
                pe.wait_ge(s["pxT_ready"], t + 1)
                if t >= 2:
                    pe.wait_ge(s["ox_used"], t - 1)
                if t == 0:
                    pe.wait_ge(yT_ready, YT0[1] + 2)
                for h in range(HX):
                    last = pe.matmul(bank[t % 2][:, h * W17:(h + 1) * W17], lhsT=pxT[:, t % 2, h * P:(h + 1) * P],
                                     rhs=vx[:, t // TB, h, :], start=True, stop=True)
                last.then_inc(s["ox_psum"], 1)

            pe.wait_ge(s["amax_ready"], 1)
            pe.transpose(bank[2][0:1, 0:P], amax[:, 0:1], ident).then_inc(s["amaxT_psum"], 1)
            pe.wait_ge(s["gsc_ready"], 1)
            pe.matmul(bank[3][:, 0:2], lhsT=cst("ones", 1), rhs=gsc[:, 0, :], start=True, stop=True).then_inc(s["gscb_psum"], 1)
            xps = bank[4].bitcast(BF16)
            pe.wait_ge(s["xq_ready"], 1)
            for t in range(NT):
                last = pe.transpose(xps[:, t * P:(t + 1) * P], xq[:, t * P:(t + 1) * P], ident_bf[:, :])
            last.then_inc(s["xqT_psum"], 1)
            pe.wait_ge(s["xqT_ready"], 1)
            pe.wait_ge(s["act_ready"], 1)
            for u in range(2 * NFC):
                c, b = divmod(u, 2)
                if u >= 3:
                    pe.wait_ge(s["hf_ready"], u - 2)
                for w in range(2):
                    last = pe.matmul(bank[2 + 2 * (u % 3) + w], lhsT=wguT[:, (w * NFC + c) * P:(w * NFC + c + 1) * P],
                                     rhs=xqT[:, b * S:(b + 1) * S], start=True, stop=True)
                last.then_inc(s["gu_psum"], 1)
            pe.wait_ge(s["hmax_ready"], 1)
            pe.transpose(bank[0][0:1, 0:P], amax[:, 1:2], ident).then_inc(s["hmaxT_psum"], 1)
            pe.wait_ge(s["gsh_ready"], 1)
            pe.matmul(bank[1][:, 0:2], lhsT=cst("ones", 1), rhs=gsc[:, 1, :], start=True, stop=True).then_inc(s["gshb_psum"], 1)
            pe.wait_ge(s["hq_ready"], NFC)
            for b in range(B):
                for t in range(TB * b, TB * b + TB):
                    for c in range(NFC):
                        n = P if c < NFC - 1 else FFL
                        last = pe.matmul(bank[2 + b][:, (t % TB) * D:(t % TB + 1) * D], lhsT=hq[0:n, c, t * P:(t + 1) * P],
                                         rhs=wdT[0:n, c * P:(c + 1) * P], start=(c == 0), stop=(c == NFC - 1))
                last.then_inc(s["down_psum"], 1)

            transpose_y(3)
            pe.wait_ge(loaded["wqkv1"], 16)
            for b in range(B):
                pe.wait_ge(yT_ready, YT0[3] + b + 1)
                for w in range(2):
                    pe.matmul(bank[2 + 2 * b + w], lhsT=wqkv1[:, w * D:(w + 1) * D], rhs=yT[:, b * S:(b + 1) * S],
                              start=True, stop=True).then_inc(s["q1_psum"], 1)
            for b in range(B):
                for t in range(TB * b, TB * b + TB):
                    last = pe.matmul(bank[6 + b][:, (t % TB) * D:(t % TB + 1) * D], lhsT=yT[:, t * P:(t + 1) * P],
                                     rhs=wqkv1[:, 2 * D:3 * D], start=True, stop=True)
                last.then_inc(s["v1_psum"], 1)
            pe.wait_ge(s["heads_loaded"], 2 * NTERM * 16)
            pe.wait_ge(s["vext1_ready"], 3)

            def scores(h, j, first):
                b, q = divmod(j, 4)
                if not (first and j < 4):
                    pe.wait_ge(s["tw_ready"], 8 * h + j - 3)
                at = h * (B * S) + b * S
                pe.matmul(bank[j % 4], lhsT=heads[:, 0, bass.ds(at + q * P, P)], rhs=heads[:, 1, bass.ds(at, S)],
                          start=True, stop=True).then_inc(s["scores_psum"], 1)

            def turn(h, j, first):
                pe.wait_ge(s["shifted_ready"], 8 * h + j + 1)
                if not (first and j < 2):
                    pe.wait_ge(s["p_ready"], 8 * h + j - 1)
                for k in range(4):
                    last = pe.transpose(bank[4 + j % 2][:, k * P:(k + 1) * P], tw[:, j % 4, k * P:(k + 1) * P], ident)
                last.then_inc(s["t_psum"], 1)

            def values(h, j, first):
                b, q = divmod(j, 4)
                pe.wait_ge(s["p_ready"], 8 * h + j + 1)
                if q == 0 and not first:
                    pe.wait_ge(s["oraw_ready"], 2 * h + b - 1)
                for k in range(4):
                    last = pe.matmul(bank[6 + b][:, q * W9:(q + 1) * W9], lhsT=pT[:, j % 4, k * P:(k + 1) * P],
                                     rhs=vext1[:, k, :, b, :][:, bass.ds(h, 1), :],
                                     start=(k == 0), stop=(k == 3))
                last.then_inc(s["pv_done"], 1)

            def head(h, first=False, final=False):
                for j in range(8):
                    if j + 2 < 8:
                        scores(h, j + 2, first)
                    elif not final:
                        scores(h + 1, j + 2 - 8, False)
                    turn(h, j, first)
                    if j >= 1:
                        values(h, j - 1, first)
                    elif not first:
                        values(h - 1, 7, False)
            scores(0, 0, True)
            scores(0, 1, True)
            head(0, first=True)
            for h in range(1, H16 - 1):
                head(h)
            head(H16 - 1, final=True)
            values(H16 - 1, 7, False)

            pe.wait_ge(s["oraw_ready"], 2 * H16)
            transpose_y(4)
            pe.wait_ge(s["dep_ready"], 1)
            pe.wait_ge(s["wing_ready"], 1)
            for b in range(B):
                pe.wait_ge(yT_ready, YT0[4] + b + 1)
                for t in range(TB * b, TB * b + TB):
                    o = bank[2 + b][:, (t % TB) * D:(t % TB + 1) * D]
                    pe.matmul(o, lhsT=yT[:, t * P:(t + 1) * P], rhs=win[:, :], start=True, stop=False)
                    pe.matmul(o, lhsT=cst("ones", 1), rhs=bin_row[:, :], start=False, stop=False)
                    last = pe.matmul(o, lhsT=onehot[:, b, (t % TB) * P:(t % TB + 1) * P], rhs=depool[:, b, :],
                                     start=False, stop=True)
                last.then_inc(s["e_psum"], 1)

            transpose_y(5)
            pe.wait_ge(loaded["wg"], 16)
            for t in range(NT):
                if t % TB == 0:
                    pe.wait_ge(yT_ready, YT0[5] + t // TB + 1)
                last = pe.matmul(bank[2][:, t * NE:(t + 1) * NE], lhsT=yT[:, t * P:(t + 1) * P], rhs=wg[:, :],
                                 start=True, stop=True)
            last.then_inc(s["lg_psum"], 1)
            pe.wait_ge(s["s_ready"], 1)
            for t in range(NT):
                last = pe.transpose(bank[3 + t // TB][0:NE, (t % TB) * P:(t % TB + 1) * P], sc8[:, t, :], ident)
            last.then_inc(s["sT_psum"], 1)
            pe.wait_ge(s["sT_ready"], 1)
            for b in range(B):
                last = pe.matmul(bank[5 + b], lhsT=cst("rowsel", NE), rhs=sT[:, b * S:(b + 1) * S], start=True, stop=True)
            last.then_inc(s["sbc_psum"], 1)
            for r in range(len(SEL_SHIFTS) + 1):
                pe.wait_ge(s["flag_ready"], r + 1)
                pe.matmul(bank[7][:, r:r + 1], lhsT=group_bf[:, :], rhs=flag[:, :], start=True, stop=True).then_inc(s["digit_psum"], 1)
                if r == len(SEL_SHIFTS) - 1:
                    break
            pe.wait_ge(s["selmask_ready"], 1)
            for t in range(NT):
                last = pe.transpose(bank[3 + t // TB][:, (t % TB) * P:(t % TB + 1) * P], selmask[:, t * P:(t + 1) * P], ident)
            last.then_inc(s["smaskT_psum"], 1)

            pe.wait_ge(s["smask_ready"], 1)
            for e in range(NE):
                pe.wait_ge(w_in[e % 2], 48 * (e // 2 + 1))
                pe.wait_ge(s["ys_ready"], e + 1)
                if e >= 1:
                    pe.wait_ge(s["acc_done"], 2 * e)
                for b in range(B):
                    if e >= 1:
                        pe.wait_ge(s["ysT_ready"], 2 * e - 1 + b)
                    for t in range(TB * b, TB * b + TB):
                        last = pe.transpose(bank[b][:, (t % TB) * P:(t % TB + 1) * P], ys[:, e % 2, t, :], ident)
                    last.then_inc(s["ysT_psum"], 1)
                for u in range(4):
                    c, b = divmod(u, 2)
                    g = 4 * e + u
                    pe.wait_ge(s["ysT_ready"], 2 * e + b + 1)
                    if g >= 2:
                        pe.wait_ge(s["h_ready"], g - 1)
                    for w, ww in enumerate((w1, w3)):
                        last = pe.matmul(bank[2 + 2 * (u % 2) + w], lhsT=ww[:, e % 2, c * P:(c + 1) * P],
                                         rhs=ysT[:, e % 2, b * S:(b + 1) * S], start=True, stop=True)
                    last.then_inc(s["ab_psum"], 1)
                pe.wait_ge(s["h_ready"], 4 * e + 4)
                for b in range(B):
                    for t in range(TB * b, TB * b + TB):
                        for c in range(2):
                            last = pe.matmul(bank[6 + b][:, (t % TB) * D:(t % TB + 1) * D], lhsT=hmoe[:, c, t * P:(t + 1) * P],
                                             rhs=w2[:, e % 2, c, :], start=(c == 0), stop=(c == 1))
                    last.then_inc(s["w2_psum"], 1)

        @block.scalar
        def _(act):
            links = [0]

            def link(ins):
                links[0] += 1
                ins.then_inc(s["act_chain"], 1)
                act.wait_ge(s["act_chain"], links[0])

            def copy(o, i):
                return act.activation(o, i, ACT.Copy)

            def norm(i, turn=True):
                act.wait_ge(var_ready, VAR0[i] + 1)
                if i == 0:
                    act.wait_ge(loaded["const_a"], 16)
                act.activation(std[:, :], mv[:, :, 1], ACT.Sqrt, bias=cst("eps")).then_inc(std_ready, 1)
                if turn:
                    for b in range(B):
                        act.wait_ge(yT_psum, YT0[i] + b + 1)
                        copy(yT[:, b * S:(b + 1) * S], bank[b]).then_inc(yT_ready, 1)

            for w in range(2):
                act.wait_ge(s["wf_psum"], w + 1)
                copy(wf[:, w, :], bank[4 + w]).then_inc(s["wf_ready"], 1)
            norm(0)
            for t in range(NT):
                act.wait_ge(s["qkv_psum"], t + 1)
                if t >= 2:
                    act.wait_ge(s["nsq_ready"], t - 1)
                act.activation(sq[:, t % 2, :], bank[2 + t % 2][:, 0:2 * D], ACT.Square).then_inc(s["sq_ready"], 1)
                copy(v_tok[:, t, :], bank[2 + t % 2][:, 2 * D:3 * D]).then_inc(s["v_ready"], 1)
            act.wait_ge(s["nsq_ready"], NT)
            act.activation(fscale[:, :, :], nsq[:, :, :], ACT.Exp, scale=-0.5).then_inc(s["fexp_ready"], 1)
            for u in range(16):
                act.wait_ge(s["fabs_ready"], u + 1)
                if u < NT:
                    o = [kfeat[:, u, f, :] for f in range(2)]
                else:
                    b, c = divmod(u - NT, FC)
                    o = [qfeat[:, c, f, b * S:(b + 1) * S] for f in range(2)]
                act.activation(o[0], frac[:, u % 3, :], ACT.Sin, scale=TWO_PI).then_inc(s["feat_ready"], 1)
                act.activation(o[1], fabs[:, u % 3, :], ACT.Sin, scale=-TWO_PI, bias=cst("halfpi")).then_inc(s["feat_ready"], 1)
            for b in range(B):
                act.wait_ge(s["oT_psum"], b + 1)
                copy(oT[:, b * S:(b + 1) * S], bank[b]).then_inc(s["oT_ready"], 1)

            act.wait_ge(loaded["clips"], 16)
            act.activation(clipe[:, :], clips[:, :], ACT.Exp, scale=-1.0).then_inc(s["clip_exp"], 1)
            act.wait_ge(s["wT_psum"], 1)
            copy(wguT[:, :], bank[6].bitcast(BF16)[:, 0:2 * NFC * P]).then_inc(s["wT_ready"], 1)
            act.wait_ge(s["wT_psum"], 2)
            wps = bank[7].bitcast(BF16)
            copy(wdT[:, 0:(NFC - 1) * P], wps[:, 0:(NFC - 1) * P])
            copy(wdT[0:FFL, (NFC - 1) * P:NFC * P], wps[0:FFL, (NFC - 1) * P:NFC * P]).then_inc(s["wT_ready"], 1)
            act.wait_ge(loaded["ctx"], 16)
            for b in range(B):
                act.activation(csq[:, :], ctx_sb[:, b, :], ACT.Square, accum_out=csum[:, b:b + 1]).then_inc(s["csq_ready"], 1)
                act.wait_ge(s["csq_ready"], b + 1)
            act.activation(csum[:, :], csum[:, :], ACT.Sqrt, scale=1.0 / CTX, bias=cst("eps", SC)).then_inc(s["cstd_ready"], 1)

            norm(1)
            for t in range(NT):
                act.wait_ge(s["lx_ready"], t + 1)
                act.activation(lx[:, t % 2, :, :], lx[:, t % 2, :, :], ACT.Exp).then_inc(s["px_ready"], 1)
                act.wait_ge(s["pxT_psum"], t + 1)
                if t >= 2:
                    act.wait_ge(s["ox_psum"], t - 1)
                copy(pxT[:, t % 2, :].rearrange("p (a n) -> p a n", a=2), psum[0:SC, 6:8, :]).then_inc(s["pxT_ready"], 1)

            norm(2, turn=False)
            act.wait_ge(s["xqT_psum"], 1)
            copy(xqT[:, :], bank[4].bitcast(BF16)).then_inc(s["xqT_ready"], 1)
            act.wait_ge(s["act_ready"], 2)
            for u in range(2 * NFC):
                c, b = divmod(u, 2)
                act.wait_ge(s["gu_psum"], u + 1)
                if u >= 4:
                    act.wait_ge(s["hf_ready"], u - 3)
                act.activation(sg[:, u % 4, :], bank[2 + 2 * (u % 3)], ACT.Silu, scale=iscale[:, c:c + 1]).then_inc(s["sg_ready"], 1)

            norm(3)
            for n in range(4):
                b, w = divmod(n, 2)
                act.wait_ge(s["q1_psum"], n + 1)
                copy(part[:, w, 0, b * S:(b + 1) * S], bank[2 + n]).then_inc(s["part1_ready"], 1)
            for n in range(4):
                b, w = divmod(n, 2)
                act.wait_ge(s["resid1_ready"], n + 1)
                copy(part[:, w, 1, b * S:(b + 1) * S], resid[:, w, b * S:(b + 1) * S]).then_inc(s["part2_ready"], 1)
            act.wait_ge(s["vext1_ready"], 1)
            for b in range(B):
                act.wait_ge(s["v1_psum"], b + 1)
                copy(vext1[:, :, :, b, 0:DH8], bank[6 + b].rearrange("p (t h d) -> p t h d", t=TB, h=H16)).then_inc(s["vext1_ready"], 1)

            def evacuate(h, b):
                act.wait_ge(s["pv_done"], 8 * h + 4 * b + 4)
                copy(oraw[:, TB * b:TB * (b + 1), :, :][:, :, bass.ds(h, 1), :],
                     bank[6 + b][:, 0:TB * W9].rearrange("p (t a d) -> p t a d", t=TB, a=1)).then_inc(s["oraw_ready"], 1)

            def head(h, first=False):
                for j in range(8):
                    act.wait_ge(s["t_psum"], 8 * h + j + 1)
                    if not (first and j < 4):
                        act.wait_ge(s["pv_done"], 8 * h + j - 3)
                    act.activation(pT[:, j % 4, :], bank[4 + j % 2], ACT.Exp).then_inc(s["p_ready"], 1)
                    if j == 1 and not first:
                        evacuate(h - 1, 1)
                    if j == 5:
                        evacuate(h, 0)
            head(0, first=True)
            for h in range(1, H16):
                head(h)
            evacuate(H16 - 1, 1)
            act.wait_ge(s["lno_var"], 1)
            act.activation(std[:, :], mv[:, :, 1], ACT.Sqrt, bias=cst("eps")).then_inc(s["lno_std"], 1)

            act.wait_ge(var_ready, VAR0[4] + 1)
            act.activation(std[:, :], mv[:, :, 1], ACT.Sqrt, bias=cst("eps")).then_inc(std_ready, 1)
            act.wait_ge(var_ready, VAR0[4] + 2)
            act.activation(rms[:, :], rms[:, :], ACT.Sqrt, bias=cst("eps")).then_inc(std_ready, 1)
            for b in range(B):
                act.wait_ge(yT_psum, YT0[4] + b + 1)
                copy(yT[:, b * S:(b + 1) * S], bank[b]).then_inc(yT_ready, 1)

            norm(5)
            act.wait_ge(s["lgm_ready"], 1)
            act.activation(lg[:, :, :], lg[:, :, :], ACT.Exp).then_inc(s["lge_ready"], 1)
            act.wait_ge(s["sT_psum"], 1)
            copy(sT[:, :].rearrange("p (a n) -> p a n", a=2), psum[0:NE, 3:5, :]).then_inc(s["sT_ready"], 1)
            act.wait_ge(s["sbc_psum"], 1)
            copy(sbc[:, :].rearrange("p (a n) -> p a n", a=2), psum[:, 5:7, :]).then_inc(s["sbc_ready"], 1)
            for e in range(NE):
                for b in range(B):
                    act.wait_ge(s["ysT_psum"], 2 * e + b + 1)
                    copy(ysT[:, e % 2, b * S:(b + 1) * S], bank[b]).then_inc(s["ysT_ready"], 1)
                for u in range(4):
                    g = 4 * e + u
                    act.wait_ge(s["ab_psum"], g + 1)
                    if g >= 4:
                        act.wait_ge(s["h_ready"], g - 3)
                    act.activation(sg[:, u, :], bank[2 + 2 * (u % 2)], ACT.Silu).then_inc(s["silu_ready"], 1)

        @block.gpsimd
        def _(pool):
            links = [0]

            def link(ins):
                links[0] += 1
                ins.then_inc(s["pool_chain"], 1)
                pool.wait_ge(s["pool_chain"], links[0])

            pool.wait_ge(loaded["const_a"], 16)
            pool.wait_ge(loaded["ctxkT"], 16)
            for b in range(B):
                ins = pool.tensor_tensor(kx_bd[:, b, :, :], ctxkT[:, b, :].unsqueeze(1).to_broadcast([P, HX, SC]),
                                         cst("bd8").unsqueeze(2).to_broadcast([P, HX, SC]), ALU.mult)
            ins.then_inc(s["kx_ready"], 1)
            pool.wait_ge(loaded["ctx"], 16)
            pool.memset(vx[:, :, :, :], 1.0).then_inc(s["vx_ready"], 1)
            pool.wait_ge(s["vx_ready"], 1)
            pool.tensor_copy(vx[:, :, :, 0:DX], ctx_sb[:, :, D:2 * D].rearrange("p b (h d) -> p b h d", h=HX)).then_inc(s["vx_ready"], 1)
            pool.memset(vext1[:, :, :, :, :], 1.0).then_inc(s["vext1_ready"], 1)

            def head(h):
                for j in range(8):
                    pool.wait_ge(s["tw_ready"], 8 * h + j + 1)
                    pool.tensor_scalar(tw[:, j % 4, :], tw[:, j % 4, :], tmax[:, j % 4:j % 4 + 1], None,
                                       ALU.subtract).then_inc(s["shifted_ready"], 1)
            for h in range(H16):
                head(h)
            pool.wait_ge(s["s_ready"], 1)
            for e in range(NE):
                if e >= 2:
                    pool.wait_ge(s["ysT_psum"], 2 * (e - 1))
                pool.tensor_tensor(ys[:, e % 2, :, :], y[:, :, :], sc8[:, :, e:e + 1].to_broadcast([P, NT, D]),
                                   ALU.mult).then_inc(s["ys_ready"], 1)

        @block.vector
        def _(dve):
            links = [0]

            def link(ins):
                links[0] += 1
                ins.then_inc(s["dve_chain"], 1)
                dve.wait_ge(s["dve_chain"], links[0])

            def moments(src):
                for t in range(NT):
                    last = dve.bn_stats(stats[:, t, :], src[:, t, :])
                link(last)
                for t in range(NT):
                    last = dve.bn_aggr(mv[:, t, :], stats[:, t, :])
                return last

            def norm(i):
                moments(x).then_inc(var_ready, 1)
                dve.wait_ge(std_ready, VAR0[i] + 1)
                link(dve.reciprocal(rstd[:, :], std[:, :]))
                for t in range(NT):
                    dve.tensor_scalar(y[:, t, :], x[:, t, :], mv[:, t, 0:1], rstd[:, t:t + 1], ALU.subtract,
                                      ALU.mult).then_inc(y_ready, 1)

            def quantise(dst, src, inv):
                if inv is not None:
                    link(dve.tensor_scalar(src, src, inv, QMAX, ALU.mult, ALU.min))
                else:
                    link(dve.tensor_scalar(src, src, QMAX, None, ALU.min))
                link(dve.tensor_scalar(src, src, -QMAX - 1.0, MAGIC, ALU.max, ALU.add))
                return dve.tensor_scalar(dst, src, MAGIC, None, ALU.subtract)

            dve.wait_ge(loaded["const_a"], 16)
            dve.wait_ge(loaded["rf"], 16)
            dve.scalar_tensor_tensor(rf_bd[:, :, :], rf[:, :].unsqueeze(1).to_broadcast([P, H16, M_RF]), 1.0 / (2 * math.pi),
                                     cst("bd16").unsqueeze(2).to_broadcast([P, H16, M_RF]), ALU.mult, ALU.mult).then_inc(s["rfbd_ready"], 1)
            dve.tensor_copy(ident_bf[:, :], cst("ident")).then_inc(s["identbf_ready"], 1)
            dve.wait_ge(in_x, 32)
            norm(0)
            for t in range(NT):
                dve.wait_ge(s["sq_ready"], t + 1)
                dve.tensor_reduce(nsq[:, t, :], sq[:, t % 2, :].rearrange("p (h d) -> p h d", d=DH8), AX.X, ALU.add).then_inc(s["nsq_ready"], 1)
            dve.wait_ge(s["fexp_ready"], 1)
            link(dve.tensor_scalar(fscale[:, :, :], fscale[:, :, :], M_RF ** -0.5, None, ALU.mult))
            dve.wait_ge(s["v_ready"], NT)
            k_sc = fscale[:, :, H16:2 * H16]
            dve.tensor_tensor(vext0[:, :, :, 0:DH8], v_tok[:, :, :].rearrange("p t (h d) -> p t h d", h=H16),
                              k_sc.unsqueeze(3).to_broadcast([P, NT, H16, DH8]), ALU.mult).then_inc(s["vext_ready"], 1)
            dve.tensor_copy(vext0[:, :, :, DH8:W9], k_sc.unsqueeze(3)).then_inc(s["vext_ready"], 1)

            def kv(b):
                dve.wait_ge(s["kv_psum"], b + 1)
                dve.tensor_tensor(kv_bd[:, b, :, :, :], bank[2 + b][:, 0:2 * FC * 36].rearrange("p (c g d) -> p c g d", g=4, d=W9),
                                  cst("bd4").unsqueeze(1).unsqueeze(3).to_broadcast([P, 2 * FC, 4, W9]), ALU.mult).then_inc(s["kv_ready"], 1)

            for u in range(16):
                dve.wait_ge(s["proj_psum"], u + 1)
                if u >= 3:
                    dve.wait_ge(s["feat_ready"], 2 * (u - 2))
                link(dve.tensor_scalar(turns[:, u % 2, :], bank[4 + u % 4], MAGIC, MAGIC, ALU.add, ALU.subtract))
                dve.tensor_tensor(frac[:, u % 3, :], bank[4 + u % 4], turns[:, u % 2, :], ALU.subtract).then_inc(s["frac_ready"], 1)
                dve.wait_ge(s["frac_ready"], u + 1)
                dve.tensor_scalar(fabs[:, u % 3, :].bitcast(I32), frac[:, u % 3, :].bitcast(I32), 0x7FFFFFFF, None,
                                  ALU.bitwise_and).then_inc(s["fabs_ready"], 1)
            for b in range(B):
                kv(b)
            for b in range(B):
                dve.wait_ge(s["qkvo_psum"], b + 1)
                q_sc = fscale[:, TB * b:TB * (b + 1), 0:H16]
                sums = psum[:, 4:8, 0:H16 * W9].rearrange("p t (h d) -> p t h d", d=W9)
                link(dve.tensor_tensor(zden[:, :, :].unsqueeze(3), sums[:, :, :, DH8:W9], q_sc.unsqueeze(3), ALU.mult))
                link(dve.tensor_scalar(zden[:, :, :], zden[:, :, :], 1e-6, None, ALU.max))
                link(dve.reciprocal(zrec[:, :, :], zden[:, :, :]))
                link(dve.tensor_tensor(zfac[:, :, :], zrec[:, :, :], q_sc, ALU.mult))
                dve.tensor_tensor(tmp[:, TB * b:TB * (b + 1), :].rearrange("p t (h d) -> p t h d", h=H16), sums[:, :, :, 0:DH8],
                                  zfac[:, :, :].unsqueeze(3).to_broadcast([P, TB, H16, DH8]), ALU.mult).then_inc(s["o_ready"], 1)

            def add_psum(b, first_bank, done):
                xs = x[:, TB * b:TB * (b + 1), :]
                dve.tensor_tensor(xs, xs, bank[first_bank + b].rearrange("p (t d) -> p t d", t=TB), ALU.add).then_inc(done, 1)
            for b in range(B):
                dve.wait_ge(s["wo_psum"], b + 1)
                add_psum(b, 2, s["x0_ready"])

            dve.wait_ge(loaded["const_b"], 16)
            nw = 2 * NFC * P
            dve.wait_ge(loaded["wgu"], 32)
            dve.tensor_reduce(wmax[:, 0:2 * NFC], wgu[:, 0:nw].rearrange("p (c n) -> p c n", n=P), AX.X, ALU.max, apply_absolute_value=True)
            link(dve.tensor_reduce(wmax[:, 2 * NFC:], wgu[:, nw:], AX.X, ALU.max, apply_absolute_value=True))
            link(dve.tensor_scalar(wscale[:, :], wmax[:, :], 1.0 / QMAX, None, ALU.mult))
            link(dve.reciprocal(winv[:, :], wscale[:, :]))
            dve.tensor_tensor(wgu[:, 0:nw].rearrange("p (c n) -> p c n", n=P), wgu[:, 0:nw].rearrange("p (c n) -> p c n", n=P),
                              winv[:, 0:2 * NFC].unsqueeze(2).to_broadcast([P, 2 * NFC, P]), ALU.mult)
            link(dve.tensor_scalar(wgu[:, nw:], wgu[:, nw:], winv[:, 2 * NFC:], None, ALU.mult))
            quantise(wq_bf[:, :], wgu[:, :], None).then_inc(s["wq_ready"], 1)
            dve.wait_ge(s["wdrow_psum"], 1)
            dve.tensor_copy(wdrow[:, :], bank[6][0:1, 0:P]).then_inc(s["wdrow_ready"], 1)
            dve.wait_ge(s["wdb_psum"], 1)
            dve.tensor_copy(wdscale[:, :], bank[7][:, 0:P]).then_inc(s["wdb_used"], 1)
            dve.wait_ge(s["clip_exp"], 1)
            link(dve.tensor_scalar(clipf[:, :], clipe[:, :], 1.0, None, ALU.add))
            link(dve.reciprocal(clipf[:, :], clipf[:, :]))

            dve.wait_ge(loaded["lens"], 16)
            dve.wait_ge(loaded["const_b"], 16)
            dve.wait_ge(loaded["win"], 64)
            dve.tensor_copy(lens_f[:, :], lens_i[:, :]).then_inc(s["len_ready"], 1)
            dve.wait_ge(s["cs_psum"], 1)
            dve.tensor_scalar(bidx[:, 0, :], bank[6][0:SC, 0:B], -1.0, None, ALU.add)
            link(dve.tensor_scalar(bidx[:, 1, :], bank[6][0:SC, 0:B], S - 1.0, None, ALU.add))
            link(dve.memset(zeros[:, :], 0.0))
            for b in range(B):
                link(dve.tensor_scalar(bhit[:, b, :], cst("iota_l", SC), bidx[:, 0, b:b + 1], None, ALU.is_equal))
                dve.scalar_tensor_tensor(bhit[:, b, :], cst("iota_l", SC), bidx[:, 1, b:b + 1], bhit[:, b, :], ALU.is_equal,
                                         ALU.add).then_inc(s["hit_ready"], 1)
            for b in range(B):
                dve.wait_ge(s["cnt_psum"], b + 1)
                link(dve.tensor_scalar(bmask[:, :], bank[6 + b][0:SC, :], 1.0, None, ALU.min))
                link(dve.tensor_tensor_scan(bcum[:, :], bmask[:, :], zeros[:, :], 0.0, ALU.add, ALU.add))
                link(dve.tensor_scalar(bcum[:, :], bcum[:, :], -1.0, 0.0, ALU.add, ALU.max))
                link(dve.tensor_scalar(bcum[:, :], bcum[:, :], SC - 1.0, None, ALU.min))
                dve.tensor_scalar(onehot[:, b, :], bcum[:, :], cst("iota_p", SC), None, ALU.is_equal).then_inc(s["onehot_ready"], 1)
            dve.wait_ge(s["cstd_ready"], 1)
            link(dve.reciprocal(csum[:, :], csum[:, :]))
            for b in range(B):
                link(dve.tensor_scalar(upd[:, b, :], ctx_sb[:, b, 0:D], csum[:, b:b + 1], BCOEF, ALU.mult, ALU.mult))
                last = dve.tensor_tensor(upd[:, b, :], upd[:, b, :], ginit[:, :], ALU.mult)
            last.then_inc(s["upd_ready"], 1)
            dve.wait_ge(s["dep_psum"], 1)
            dve.tensor_copy(depool[:, :, :], bank[6][0:SC, 0:B * D].rearrange("p (b d) -> p b d", b=B)).then_inc(s["dep_ready"], 1)
            dve.tensor_scalar(win[:, :], win[:, :], gres[:, 0:1], None, ALU.mult).then_inc(s["wing_ready"], 1)

            dve.wait_ge(loaded["xmask"], 16)
            dve.wait_ge(loaded["bias0"], 16)
            link(dve.tensor_copy(xmask_f[:, :], xmask_i[:, :]))
            link(dve.tensor_scalar(xmask_f[:, :], xmask_f[:, :], 1.0, 1e30, ALU.subtract, ALU.mult))
            link(dve.tensor_scalar(xbias[:, :, :].rearrange("p b n -> p (b n)"), xmask_f[:, :], bias0[:, 0:1], None, ALU.add))
            dve.wait_ge(s["x0_ready"], 2)
            norm(1)

            def x_out(t):
                dve.wait_ge(s["ox_psum"], t + 1)
                o = bank[t % 2][:, 0:HX * W17].rearrange("p (h d) -> p h d", d=W17)
                link(dve.reciprocal(xrec[:, :].unsqueeze(2), o[:, :, DX:W17]))
                dve.tensor_tensor(tmp[:, t, :].rearrange("p (h d) -> p h d", h=HX), o[:, :, 0:DX],
                                  xrec[:, :].unsqueeze(2).to_broadcast([P, HX, DX]), ALU.mult).then_inc(s["ox_used"], 1)
                dve.wait_ge(s["ox_used"], t + 1)
                ins = dve.tensor_tensor(x[:, t, :], x[:, t, :], tmp[:, t, :], ALU.add)
                if t % TB == TB - 1:
                    ins.then_inc(s["x1_ready"], 1)

            for t in range(NT):
                dve.wait_ge(s["sx_psum"], t + 1)
                if t >= 2:
                    dve.wait_ge(s["pxT_psum"], t - 1)
                l = lx[:, t % 2, :, :]
                b0 = 2 + 2 * (t % 2)
                link(dve.tensor_tensor(l.rearrange("p (g h) n -> p g h n", g=2),
                                       psum[:, b0:b0 + 2, 0:4 * SC].rearrange("p g (h n) -> p g h n", n=SC),
                                       xbias[:, t // TB, :].unsqueeze(1).unsqueeze(1).to_broadcast([P, 2, 4, SC]), ALU.add))
                link(dve.tensor_reduce(nmx[:, t % 2, :], l, AX.X, ALU.max, negate=True))
                dve.tensor_tensor(l, l, nmx[:, t % 2, :].unsqueeze(2).to_broadcast([P, HX, SC]), ALU.add).then_inc(s["lx_ready"], 1)
                if t >= 1:
                    x_out(t - 1)
            x_out(NT - 1)

            dve.wait_ge(s["x1_ready"], 2)
            norm(2)

            def scale_of(k, src_bank, ready):
                link(dve.tensor_reduce(gmax[:, k:k + 1], bank[src_bank][0:1, 0:P], AX.X, ALU.max))
                link(dve.tensor_scalar(gsc[:, k, 0:1], gmax[:, k:k + 1], clipf[:, k:k + 1], 1.0 / QMAX, ALU.mult, ALU.mult))
                dve.reciprocal(gsc[:, k, 1:2], gsc[:, k, 0:1]).then_inc(ready, 1)
            dve.wait_ge(y_ready, 3 * NT)
            dve.tensor_reduce(amax[:, 0:1], y[:, :, :], AX.XY, ALU.max, apply_absolute_value=True).then_inc(s["amax_ready"], 1)
            dve.wait_ge(s["amaxT_psum"], 1)
            scale_of(0, 2, s["gsc_ready"])
            dve.wait_ge(s["gscb_psum"], 1)
            dve.tensor_copy(act_sc[:, 0, :], bank[3][:, 0:2]).then_inc(s["act_ready"], 1)
            dve.wait_ge(s["act_ready"], 1)
            dve.tensor_scalar(iscale[:, :], wscale[:, 0:2 * NFC], act_sc[:, 0, 0:1], None, ALU.mult).then_inc(s["act_ready"], 1)
            quantise(xq[:, :], y[:, :, :].rearrange("p t d -> p (t d)"), act_sc[:, 0, 1:2]).then_inc(s["xq_ready"], 1)
            dve.wait_ge(s["act_ready"], 2)
            for u in range(2 * NFC):
                c, b = divmod(u, 2)
                dve.wait_ge(s["sg_ready"], u + 1)
                h = hf[:, c, b * S:(b + 1) * S]
                dve.scalar_tensor_tensor(h, bank[3 + 2 * (u % 3)], iscale[:, NFC + c:NFC + c + 1], sg[:, u % 4, :], ALU.mult,
                                         ALU.mult).then_inc(s["hf_ready"], 1)
                dve.wait_ge(s["hf_ready"], u + 1)
                last = dve.tensor_reduce(hmax[:, u:u + 1], h, AX.X, ALU.max, apply_absolute_value=True)
            link(last)
            dve.tensor_reduce(amax[:, 1:2], hmax[:, :], AX.X, ALU.max).then_inc(s["hmax_ready"], 1)
            dve.wait_ge(s["hmaxT_psum"], 1)
            scale_of(1, 0, s["gsh_ready"])
            dve.wait_ge(s["gshb_psum"], 1)
            link(dve.tensor_copy(act_sc[:, 1, :], bank[1][:, 0:2]))
            for c in range(NFC):
                quantise(hq[:, c, :], hf[:, c, :], act_sc[:, 1, 1:2]).then_inc(s["hq_ready"], 1)
            for b in range(B):
                dve.wait_ge(s["down_psum"], b + 1)
                ts_ = tmp[:, TB * b:TB * (b + 1), :]
                xs = x[:, TB * b:TB * (b + 1), :]
                link(dve.scalar_tensor_tensor(ts_, bank[2 + b].rearrange("p (t d) -> p t d", t=TB), act_sc[:, 1, 0:1],
                                              wdscale[:, :].unsqueeze(1).to_broadcast([P, TB, D]), ALU.mult, ALU.mult))
                dve.tensor_tensor(xs, xs, ts_, ALU.add).then_inc(s["x2_ready"], 1)

            dve.wait_ge(s["x2_ready"], 2)
            norm(3)
            for n in range(4):
                b, w = divmod(n, 2)
                dve.wait_ge(s["part1_ready"], n + 1)
                h = slice(b * S, (b + 1) * S)
                dve.tensor_tensor(resid[:, w, h], bank[2 + n], part[:, w, 0, h], ALU.subtract).then_inc(s["resid1_ready"], 1)
            for n in range(4):
                b, w = divmod(n, 2)
                dve.wait_ge(s["part2_ready"], n + 1)
                h = slice(b * S, (b + 1) * S)
                dve.tensor_tensor(part[:, w, 2, h], resid[:, w, h], part[:, w, 1, h], ALU.subtract).then_inc(s["part3_ready"], 1)

            def head(h, first=False):
                for j in range(8):
                    dve.wait_ge(s["scores_psum"], 8 * h + j + 1)
                    at = (S - P) - (j % 4) * P
                    dve.tensor_tensor_reduce(out=tw[:, j % 4, :], in0=bank[j % 4], in1=cst("dist")[:, at:at + S], scale=1.0,
                                             scalar=-3.0e38, op0=ALU.mult, op1=ALU.max,
                                             accum_out=tmax[:, j % 4:j % 4 + 1]).then_inc(s["tw_ready"], 1)
            head(0, first=True)
            for h in range(1, H16):
                head(h)
            dve.wait_ge(s["oraw_ready"], 2 * H16)
            link(dve.reciprocal(nsq[:, :, 0:H16].unsqueeze(3), oraw[:, :, :, DH8:W9]))
            link(dve.tensor_tensor(tmp[:, :, :].rearrange("p t (h d) -> p t h d", h=H16), oraw[:, :, :, 0:DH8],
                                   nsq[:, :, 0:H16].unsqueeze(3).to_broadcast([P, NT, H16, DH8]), ALU.mult))
            moments(tmp).then_inc(s["lno_var"], 1)
            dve.wait_ge(s["lno_std"], 1)
            link(dve.reciprocal(rstd[:, :], std[:, :]))
            for t in range(NT):
                last = dve.tensor_scalar(tmp[:, t, :], tmp[:, t, :], mv[:, t, 0:1], rstd[:, t:t + 1], ALU.subtract, ALU.mult)
            link(last)
            dve.wait_ge(loaded["gb"], 32)
            link(dve.tensor_tensor(tmp[:, :, :], tmp[:, :, :], gamma[:, :].unsqueeze(1).to_broadcast([P, NT, D]), ALU.mult))
            link(dve.tensor_tensor(tmp[:, :, :], tmp[:, :, :], beta[:, :].unsqueeze(1).to_broadcast([P, NT, D]), ALU.add))
            dve.tensor_tensor(x[:, :, :], x[:, :, :], tmp[:, :, :], ALU.add).then_inc(s["x3_ready"], 2)

            dve.wait_ge(s["x3_ready"], 2)
            moments(x).then_inc(var_ready, 1)
            dve.wait_ge(std_ready, VAR0[4] + 1)
            link(dve.reciprocal(rstd[:, :], std[:, :]))
            link(dve.tensor_tensor(rms[:, :], rstd[:, :], rstd[:, :], ALU.mult))
            dve.tensor_tensor(rms[:, :], rms[:, :], mv[:, :, 1], ALU.mult).then_inc(var_ready, 1)
            dve.wait_ge(std_ready, VAR0[4] + 2)
            link(dve.reciprocal(rms[:, :], rms[:, :]))
            link(dve.tensor_tensor(rstd[:, :], rstd[:, :], rms[:, :], ALU.mult))
            for t in range(NT):
                dve.tensor_scalar(y[:, t, :], x[:, t, :], mv[:, t, 0:1], rstd[:, t:t + 1], ALU.subtract,
                                  ALU.mult).then_inc(y_ready, 1)
            for b in range(B):
                dve.wait_ge(s["e_psum"], b + 1)
                add_psum(b, 2, s["x4_ready"])

            dve.wait_ge(s["x4_ready"], 2)
            norm(5)
            dve.tensor_copy(group_bf[:, :], cst("group"))
            dve.wait_ge(s["lg_psum"], 1)
            lgp = bank[2][:, 0:NT * NE].rearrange("p (t e) -> p t e", e=NE)
            link(dve.tensor_reduce(smx[:, :], lgp, AX.X, ALU.max))
            dve.tensor_tensor(lg[:, :, :], lgp, smx[:, :].unsqueeze(2).to_broadcast([P, NT, NE]), ALU.subtract).then_inc(s["lgm_ready"], 1)
            dve.wait_ge(s["lge_ready"], 1)
            link(dve.tensor_reduce(smx[:, :], lg[:, :, :], AX.X, ALU.add))
            link(dve.reciprocal(smx[:, :], smx[:, :]))
            dve.tensor_tensor(sc8[:, :, :], lg[:, :, :], smx[:, :].unsqueeze(2).to_broadcast([P, NT, NE]), ALU.mult).then_inc(s["s_ready"], 1)
            dve.wait_ge(s["sbc_ready"], 1)
            dve.wait_ge(loaded["jbits"], 16)
            link(dve.memset(thr[:, :], 0))
            for r, sh in enumerate(SEL_SHIFTS):
                link(dve.tensor_tensor(cand[:, :], thr[:, :], jbits[:, r:r + 1], ALU.bitwise_or))
                link(dve.tensor_scalar(selw[:, 0, :], sbc[:, :], cand[:, :].bitcast(F32), None, ALU.is_ge, ALU.add, accum_out=cnt[:, 0:1]))
                dve.tensor_scalar(flag[:, :], cnt[:, 0:1], float(CAP), None, ALU.is_ge).then_inc(s["flag_ready"], 1)
                dve.wait_ge(s["digit_psum"], r + 1)
                if sh >= 0:
                    link(dve.tensor_scalar(digit[:, :], bank[7][:, r:r + 1], -1.0, None, ALU.add))
                    link(dve.tensor_scalar(digit[:, :], digit[:, :], sh, None, ALU.logical_shift_left))
                else:
                    link(dve.tensor_scalar(digit[:, :], bank[7][:, r:r + 1], 2.0 ** sh, -1.0, ALU.mult, ALU.add))
                link(dve.tensor_tensor(thr[:, :], thr[:, :], digit[:, :], ALU.bitwise_or))
            tf = thr[:, :].bitcast(F32)
            link(dve.tensor_scalar(selw[:, 0, :], sbc[:, :], tf, None, ALU.is_gt, ALU.add, accum_out=cnt[:, 1:2]))
            link(dve.tensor_scalar(need[:, :], cnt[:, 1:2], -1.0, float(CAP), ALU.mult, ALU.add))
            link(dve.tensor_scalar(selw[:, 1, :], sbc[:, :], tf, None, ALU.is_equal))
            link(dve.tensor_tensor_scan(selw[:, 2, :], selw[:, 1, :], selw[:, 1, :], 0.0, ALU.add, ALU.max))
            link(dve.scalar_tensor_tensor(selw[:, 1, :], selw[:, 2, :], need[:, 0:1], selw[:, 1, :], ALU.is_le, ALU.mult))
            dve.tensor_tensor(selmask[:, :], selw[:, 0, :], selw[:, 1, :], ALU.add).then_inc(s["selmask_ready"], 1)
            dve.wait_ge(s["smaskT_psum"], 1)
            dve.tensor_copy(smask[:, :, :].rearrange("p (a t) e -> p a t e", a=2),
                            psum[:, 3:5, :].rearrange("p a (t e j) -> p a t e j", e=NE, j=SEL_J)[:, :, :, :, 0]).then_inc(s["smask_ready"], 1)
            dve.wait_ge(s["smask_ready"], 1)
            for e in range(NE):
                for u in range(4):
                    c, b = divmod(u, 2)
                    g = 4 * e + u
                    dve.wait_ge(s["silu_ready"], g + 1)
                    if u == 0 and e >= 1:
                        dve.wait_ge(s["w2_psum"], 2 * e)
                    dve.tensor_tensor(hmoe[:, c, b * S:(b + 1) * S], bank[3 + 2 * (u % 2)], sg[:, u, :], ALU.mult).then_inc(s["h_ready"], 1)
                for b in range(B):
                    dve.wait_ge(s["w2_psum"], 2 * e + b + 1)
                    if b == 0 and e >= 1:
                        dve.wait_ge(s["acc_done"], 2 * e)
                    for t in range(TB * b, TB * b + TB):
                        ins = dve.scalar_tensor_tensor(x[:, t, :], bank[6 + b][:, (t % TB) * D:(t % TB + 1) * D], smask[:, t, e:e + 1],
                                                       x[:, t, :], ALU.mult, ALU.add)
                    ins.then_inc(s["acc_done"], 1)
            dve.wait_ge(s["acc_done"], 2 * NE)
            dve.sem_inc(s["x5_ready"], 2)


def kernel(**inputs):
    a = {k: np.asarray(v) for k, v in inputs.items()}
    import concourse.bacc as bacc
    from concourse.bass_utils import run_bass_kernel_spmd

    def pad_rows(w):
        return np.concatenate([w, w[:NFC * P - FF]], axis=0)
    jb = np.zeros((P, len(SEL_SHIFTS)), np.int32)
    for r, sh in enumerate(SEL_SHIFTS):
        j = np.arange(P) % SEL_J
        jb[:, r] = j << sh if sh >= 0 else j >> -sh
    data = {
        "x": a["x"],
        "ctx": a["ctx_2048"],
        "ctxkT": a["ctx_2048"][:, :, :D].transpose(2, 0, 1),
        "xmask": a["mask_BxS2_ik0"].reshape(-1),
        "lens": a["mask_BxS2_if0"].T,
        "wqkv0": np.concatenate([a["L0_attn_wq"].T, a["L0_attn_wk"].T, a["L0_attn_wv"].T], axis=1),
        "wqk0": np.stack([a["L0_attn_wq"], a["L0_attn_wk"]], axis=1),
        "wo0": a["L0_attn_wo"].T,
        "rf": np.tile(a["L0_attn_rf"].T, (H16, 1)),
        "bias0": a["L0_xattn_b"],
        "clips": np.stack([a["L0_ffn_clip_x"], a["L0_ffn_clip_down"]], axis=1),
        "wgu": np.concatenate([pad_rows(a["L0_ffn_w_gate"]), pad_rows(a["L0_ffn_w_up"])], axis=0),
        "wd": a["L0_ffn_w_down"],
        "wqkv1": np.concatenate([a["L1_attn_Wq"].T, a["L1_attn_Wk"].T, a["L1_attn_Wv"].T], axis=1),
        "gamma": a["L1_attn_ln_gamma"],
        "beta": a["L1_attn_ln_beta"],
        "win": a["L1_xattn_W_in"].T,
        "bin": a["L1_xattn_b_in"],
        "gres": a["L1_xattn_g_res"][:, None],
        "ginit": a["L1_xattn_g_init"],
        "wg": a["L1_ffn_wg"],
        "w1": a["L1_ffn_w1"],
        "w3": a["L1_ffn_w3"],
        "w2": a["L1_ffn_w2"],
        "const": constants(),
        "jbits": jb,
    }
    nc = bacc.Bacc("TRN2", target_bir_lowering=False, num_devices=1)
    arrays, args = {}, []
    for name, v in data.items():
        v = np.ascontiguousarray(v)
        arrays["in_" + name] = v
        args.append(nc.dram_tensor("in_" + name, v.shape, mybir.dt.from_np(v.dtype), kind="ExternalInput").ap())
    res = nc.dram_tensor("out_x", (B, S, D), F32, kind="ExternalOutput").ap()
    parts = nc.dram_tensor("qk_parts", (2, 3, P, NT * P), BF16, kind="Internal").ap()
    build(nc, *args, res, parts)
    r = run_bass_kernel_spmd(nc, [arrays], core_ids=[0])
    return r.results[0]["out_x"]
```

```python
import math
from contextlib import ExitStack

import numpy as np

import concourse.bass as bass
import concourse.mybir as mybir

ACT = mybir.ActivationFunctionType
ALU = mybir.AluOpType
AX = mybir.AxisListType
F32 = mybir.dt.float32
BF16 = mybir.dt.bfloat16
I32 = mybir.dt.int32

P = 128
B = 2
S = 512
D = 128
NT = B * S // P
TB = NT // B
H16, DH8 = 16, 8
M_RF = 32
FC = H16 * M_RF // P
HX, DX = 8, 16
SC = 77
CTX = 256
FF = 352
NFC = (FF + P - 1) // P
FFL = FF - (NFC - 1) * P
NE, HID, CAP = 8, 256, 512
EPS = 1e-5
MAGIC = 1.5 * 2.0 ** 23
QMAX = 127.0
TWO_PI = 6.2831850
DT = -math.log(-math.expm1(-0.001))
DECAY = math.exp(-DT)
BCOEF = math.exp(-0.001)
W9 = DH8 + 1
W17 = DX + 1
TERM_RUNS = ((0, 3, 0, 0, 0, 1), (3, 2, 1, 0, 0, 1), (5, 1, 2, 0, 0, 1))
NTERM = 6
KS = NTERM * DH8
HP = H16 // 2
NPAIR = B * HP
NPSTEP = 8
W18 = 2 * W9
POOL_STEPS = (0, 3, 6)


def shifted_before(i, by_pool):
    return sum(((n % NPSTEP) in POOL_STEPS) == by_pool for n in range(i))

SEL_J = 16
SEL_SHIFTS = (26, 22, 18, 14, 10, 6, 2, -2)

CONST = {}
_at = 0
for _name, _n in (("ident", P), ("halfpi", 1), ("eps", 1), ("iota_p", 1), ("bd16", H16), ("bd8", HX), ("bd4", 4),
                  ("rowsel", P), ("group", P), ("lmat", SC), ("tri", SC), ("ones", P),
                  ("fold", W18), ("dist", 2 * S - P), ("iota_l", S)):
    CONST[_name] = (_at, _at + _n)
    _at += _n
NCONST = _at


def constants():
    c = np.zeros((P, NCONST), np.float32)
    p = np.arange(P)

    def put(name, a):
        lo, hi = CONST[name]
        c[:a.shape[0], lo:hi] = a
    put("ident", np.eye(P))
    put("halfpi", np.full((P, 1), math.pi / 2))
    put("eps", np.full((P, 1), EPS))
    put("iota_p", p[:, None])
    put("bd16", p[:, None] // DH8 == np.arange(H16)[None])
    put("bd8", (p[:, None] // DX == np.arange(HX)[None]) * DX ** -0.5)
    put("bd4", p[:, None] // M_RF == np.arange(4)[None])
    put("rowsel", p[None] // SEL_J == np.arange(NE)[:, None])
    put("group", p[:, None] // SEL_J == p[None] // SEL_J)
    put("fold", (p[:, None] % 32) == np.arange(W18)[None])
    s = np.arange(SC)
    lag = s[None] - s[:, None]
    put("lmat", np.where(lag >= 0, DECAY ** np.maximum(lag, 0).astype(np.float64), 0.0))
    put("tri", lag >= 0)
    put("ones", np.ones((P, P)))
    put("dist", np.abs(p[:, None] - (np.arange(2 * S - P)[None] - (S - P))) / S * D ** -0.5)
    put("iota_l", np.tile(np.arange(S)[None], (P, 1)))
    return c


def build(nc, x_in, ctx_in, ctxkT_in, xmask_in, lens_in, wqkv0_in, wqk0_in, wo0_in, rf_in, bias0_in, clips_in,
          wgu_in, wd_in, wqkv1_in, gamma_in, beta_in, win_in, bin_in, gres_in, ginit_in,
          wg_in, w1_in, w3_in, w2_in, const_in, jbits_in, out, parts_dram):
    with ExitStack() as ctx:
        def sb(name, shape, dt=F32):
            return ctx.enter_context(nc.sbuf_tensor(name, shape, dt))

        def sem(name):
            return ctx.enter_context(nc.semaphore(name))

        psum = ctx.enter_context(nc.psum_tensor("psum", [P, 8, 512], F32))
        const = sb("const", [P, NCONST])

        def cst(name, rows=P):
            lo, hi = CONST[name]
            return const[0:rows, lo:hi]

        x = sb("x", [P, NT, D])
        y = sb("y", [P, NT, D])
        yT = sb("yT", [P, NT * P])
        tmp = sb("tmp", [P, NT, D])
        arena = sb("arena", [P, 5 * NT * P])
        stats = sb("stats", [P, NT, 6])
        mv = sb("mv", [P, NT, 2])
        std = sb("std", [P, NT])
        rstd = sb("rstd", [P, NT])
        rms = sb("rms", [P, NT])
        ident_bf = sb("ident_bf", [P, P], BF16)
        wqkv0 = sb("wqkv0", [P, 3 * D])
        wqk0 = sb("wqk0", [P, 2, D])
        wo0 = sb("wo0", [P, D])
        rf = sb("rf", [P, M_RF])
        rf_bd = sb("rf_bd", [P, H16, M_RF])
        wf = sb("wf", [P, 2, 512])
        sq = sb("sq", [P, 2, 2 * D])
        nsq = sb("nsq", [P, NT, 2 * H16])
        fscale = sb("fscale", [P, NT, 2 * H16])
        v_tok = tmp
        vext0 = sb("vext0", [P, NT, H16, W9])
        big = sb("big", [P, 16384])
        kfeat = big[:, 0:8192].rearrange("p (t s n) -> p t s n", t=NT, s=2)
        qfeat = big[:, 8192:16384].rearrange("p (c s n) -> p c s n", c=FC, s=2)
        ring = sb("ring", [P, 8, 512])
        turns, frac, fabs = ring[:, 0:2, :], ring[:, 2:5, :], ring[:, 5:8, :]
        sg = sb("sg", [P, 4, 512])
        kv_bd = sg[:, 0:2, :].rearrange("p a n -> p (a n)")[:, 0:B * 2 * FC * 4 * W9].rearrange("p (b c g d) -> p b c g d", b=B, c=2 * FC, g=4)
        zden = sb("zden", [P, TB, H16])
        zrec = sb("zrec", [P, TB, H16])
        zfac = sb("zfac", [P, TB, H16])
        oT = yT
        ctx_sb = sb("ctx_sb", [SC, B, CTX])
        ctxkT = sb("ctxkT", [P, B, SC])
        kx_bd = sb("kx_bd", [P, B, HX, SC])
        vx = sb("vx", [SC, B, HX, W17])
        xmask_i = sb("xmask_i", [P, B * SC], I32)
        xmask_f = sb("xmask_f", [P, B * SC])
        xbias = sb("xbias", [P, B, SC])
        bias0 = sb("bias0", [P, 1])
        lx = big[:, 0:2 * HX * SC].rearrange("p (k h n) -> p k h n", k=2, h=HX)
        nmx = sb("nmx", [P, 2, HX])
        pxT = big[0:SC, 2048:2048 + 2 * HX * P].rearrange("p (k n) -> p k n", k=2)
        xrec = sb("xrec", [P, HX])
        clips = sb("clips", [1, 2])
        clipe = sb("clipe", [1, 2])
        clipf = sb("clipf", [1, 2])
        wgu = sb("wgu", [P, 2 * NFC * P + FF])
        wmax = sb("wmax", [P, 2 * NFC + 1])
        wscale = sb("wscale", [P, 2 * NFC + 1])
        winv = sb("winv", [P, 2 * NFC + 1])
        wq_bf = sb("wq_bf", [P, 2 * NFC * P + FF], BF16)
        wguT = sb("wguT", [P, 2 * NFC * P], BF16)
        wdT = sb("wdT", [P, NFC * P], BF16)
        wdrow = sb("wdrow", [1, P])
        wdscale = sb("wdscale", [P, P])
        amax = sb("amax", [P, 2])
        hmax = sb("hmax", [P, 2 * NFC])
        gmax = sb("gmax", [1, 2])
        gsc = sb("gsc", [1, 2, 2])
        act_sc = sb("act_sc", [P, 2, 2])
        iscale = sb("iscale", [P, 2 * NFC])
        xq = big[:, 4096:4608].bitcast(BF16)
        xqT = big[:, 4608:5120].bitcast(BF16)
        hf = arena[:, 0:NFC * NT * P].rearrange("p (c n) -> p c n", c=NFC)
        hq = arena[:, NFC * NT * P:].bitcast(BF16)[:, 0:NFC * NT * P].rearrange("p (c n) -> p c n", c=NFC)
        wqkv1 = sb("wqkv1", [P, 3 * D])
        heads = big[:, 0:8192].bitcast(BF16).rearrange("p (w h n) -> p w h n", w=2, h=HP)
        pT = big[:, 8192:16384].rearrange("p (s h k n) -> p s h k n", s=2, h=2, k=4)
        resid = arena[:, 0:2 * NT * P].rearrange("p (w n) -> p w n", w=2)
        part = arena[:, 2 * NT * P:].bitcast(BF16).rearrange("p (w k n) -> p w k n", w=2, k=3)
        vpad = sb("vpad", [P, NT, H16, 32])
        tw = ring
        oT1 = sg[:, 0:2, :]
        tmax = sb("tmax", [P, 8])
        oraw = vext0
        gamma = sb("gamma", [P, D])
        beta = sb("beta", [P, D])
        win = sb("win", [P, D])
        bin_row = sb("bin_row", [1, D])
        gres = sb("gres", [P, 1])
        ginit = sb("ginit", [SC, D])
        lens_i = sb("lens_i", [SC, B], I32)
        lens_f = sb("lens_f", [SC, B])
        bidx = sb("bidx", [SC, 2, B])
        bhit = arena[0:SC, 0:2 * S].rearrange("p (b n) -> p b n", b=B)
        bmask = arena[0:SC, 2 * S:3 * S]
        bcum = arena[0:SC, 3 * S:4 * S]
        onehot = sb("onehot", [SC, B, S])
        csum = sb("csum", [SC, B])
        csq = sb("csq", [SC, CTX])
        upd = sb("upd", [SC, B, D])
        depool = sb("depool", [SC, B, D])
        zeros = arena[0:SC, 4 * S:5 * S]
        wg = sb("wg", [P, NE])
        w1 = sb("w1", [P, 2, HID])
        w3 = sb("w3", [P, 2, HID])
        w2 = sb("w2", [P, 2, 2, D])
        smx = sb("smx", [P, NT])
        lg = sb("lg", [P, NT, NE])
        sc8 = sb("sc8", [P, NT, NE])
        sT = big[0:NE, 11 * NT * P:12 * NT * P]
        sbc = big[:, 0:NT * P]
        selw = big[:, NT * P:4 * NT * P].rearrange("p (k n) -> p k n", k=3)
        jbits = sb("jbits", [P, len(SEL_SHIFTS)], I32)
        thr = sb("thr", [P, 1], I32)
        cand = sb("cand", [P, 1], I32)
        cnt = sb("cnt", [P, 2])
        flag = sb("flag", [P, 1], BF16)
        digit = sb("digit", [P, 1], I32)
        need = sb("need", [P, 1])
        group_bf = sb("group_bf", [P, P], BF16)
        selmask = big[:, 4 * NT * P:5 * NT * P]
        smask = sb("smask", [P, NT, NE])
        ys = big[:, 5 * NT * P:7 * NT * P].rearrange("p (k t d) -> p k t d", k=2, t=NT)
        ysT = big[:, 7 * NT * P:9 * NT * P].rearrange("p (k n) -> p k n", k=2)
        hmoe = big[:, 9 * NT * P:11 * NT * P].rearrange("p (k n) -> p k n", k=2)

        in_x = sem("in_x")
        in_names = ["const_a", "const_b", "wqkv0", "wqk0", "wo0", "rf", "ctx", "ctxkT", "xmask", "bias0", "clips", "wgu",
                    "wqkv1", "gb", "win", "lens", "wg", "jbits"]
        loaded = {n: sem("in_" + n) for n in in_names}
        var_ready, std_ready, y_ready, yT_psum, yT_ready = (sem(n) for n in ("var_ready", "std_ready", "y_ready", "yT_psum", "yT_ready"))
        VAR0 = (0, 1, 2, 3, 4, 6)
        YT0 = (0, 2, None, 4, 6, 8)
        s = {n: sem(n) for n in (
            "dve_chain act_chain pool_chain identbf_ready rfbd_ready wf_psum wf_ready qkv_psum sq_ready v_ready nsq_ready fexp_ready vext_ready "
            "proj_psum frac_ready fabs_ready feat_ready kv_psum kv_ready qkvo_psum o_ready oT_psum oT_ready wo_psum "
            "x0_ready kx_ready vx_ready xb_ready sx_psum lx_ready px_ready pxT_psum pxT_ready ox_psum ox_used x1_ready "
            "clip_exp wq_ready wT_psum wT_ready wdrow_psum wdrow_ready wdb_psum "
            "amax_ready amaxT_psum gsc_ready gscb_psum act_ready xq_ready xqT_psum xqT_ready gu_psum sg_ready hf_ready "
            "hmax_ready hmaxT_psum gsh_ready gshb_psum hq_ready down_psum x2_ready "
            "q1_psum part1_ready resid1_ready part2_ready part3_ready v1_psum vpad_ready parts_stored heads_loaded "
            "scores_psum tw_ready shifted_pool shifted_dve oT1_ready o_psum t_psum p_ready pv_done wdb_used oraw_ready lno_var lno_std x3_ready "
            "len_ready cs_psum hit_ready cnt_psum csq_ready cstd_ready upd_ready dep_psum dep_ready wing_ready onehot_ready e_psum "
            "x4_ready lg_psum lgm_ready lge_ready s_ready sT_psum sT_ready sbc_psum sbc_ready flag_ready digit_psum "
            "selmask_ready smaskT_psum smask_ready ys_ready ysT_psum ysT_ready ab_psum silu_ready h_ready "
            "w2_psum acc_done x5_ready out_done").split()}

        w_in = [sem(f"w_in{k}") for k in range(2)]


        bank = [psum[:, i, :] for i in range(8)]

        block = ctx.enter_context(nc.Block())

        @block.sync
        def _(sp):
            n_a = CONST["bd4"][1]
            sp.dma_start(x[:, 0:TB, :], x_in[0].rearrange("(t p) d -> p t d", p=P)).then_inc(in_x, 16)
            sp.dma_start(x[:, TB:NT, :], x_in[1].rearrange("(t p) d -> p t d", p=P)).then_inc(in_x, 16)
            sp.dma_start(const[:, 0:n_a], const_in[:, 0:n_a]).then_inc(loaded["const_a"], 16)
            sp.dma_start(rf[:, :], rf_in).then_inc(loaded["rf"], 16)
            sp.dma_start(wqkv0[:, :], wqkv0_in).then_inc(loaded["wqkv0"], 16)
            sp.dma_start(wqk0[:, :, :], wqk0_in).then_inc(loaded["wqk0"], 16)
            sp.dma_start(const[:, n_a:], const_in[:, n_a:]).then_inc(loaded["const_b"], 16)
            sp.dma_start(wo0[:, :], wo0_in).then_inc(loaded["wo0"], 16)
            sp.dma_start(ctxkT[:, :, :], ctxkT_in).then_inc(loaded["ctxkT"], 16)
            sp.dma_start(ctx_sb[:, :, :], ctx_in.rearrange("b s c -> s b c")).then_inc(loaded["ctx"], 16)
            sp.dma_start(xmask_i[:, :], xmask_in.rearrange("(a n) -> a n", a=1).to_broadcast([P, B * SC])).then_inc(loaded["xmask"], 16)
            sp.dma_start(bias0[:, :], bias0_in.rearrange("(a n) -> a n", a=1).to_broadcast([P, 1])).then_inc(loaded["bias0"], 16)
            sp.dma_start(clips[:, :], clips_in).then_inc(loaded["clips"], 16)
            sp.dma_start(lens_i[:, :], lens_in).then_inc(loaded["lens"], 16)
            sp.dma_start(wgu[:, 0:2 * NFC * P].rearrange("p (c n) -> p c n", n=P),
                         wgu_in.rearrange("(c p) n -> p c n", p=P)).then_inc(loaded["wgu"], 16)
            sp.dma_start(wgu[:, 2 * NFC * P:], wd_in).then_inc(loaded["wgu"], 16)
            sp.dma_start(wqkv1[:, :], wqkv1_in).then_inc(loaded["wqkv1"], 16)

            def rows(v, n, r=P):
                return v.rearrange("(a n) -> a n", a=1).to_broadcast([r, n])
            sp.dma_start(gamma[:, :], rows(gamma_in, D)).then_inc(loaded["gb"], 16)
            sp.dma_start(beta[:, :], rows(beta_in, D)).then_inc(loaded["gb"], 16)
            sp.dma_start(win[:, :], win_in).then_inc(loaded["win"], 16)
            sp.dma_start(gres[:, :], gres_in).then_inc(loaded["win"], 16)
            sp.dma_start(bin_row[:, :], rows(bin_in, D, 1)).then_inc(loaded["win"], 16)
            sp.dma_start(ginit[:, :], rows(ginit_in[0:D], D, SC)).then_inc(loaded["win"], 16)
            sp.dma_start(wg[:, :], wg_in).then_inc(loaded["wg"], 16)
            sp.dma_start(jbits[:, :], jbits_in).then_inc(loaded["jbits"], 16)

            for n in range(3):
                sp.wait_ge((s["part1_ready"], s["part2_ready"], s["part3_ready"])[n], 4)
                for w in range(2):
                    sp.dma_start(parts_dram[w, n], part[:, w, n, :]).then_inc(s["parts_stored"], 16)
            sp.wait_ge(s["parts_stored"], 6 * 16)
            for par in range(2):
                for t0, n, q0, qs, k0, ks in TERM_RUNS:
                    for w, (p0, ps) in enumerate(((q0, qs), (k0, ks))):
                        for i in range(n):
                            src = parts_dram[w, p0 + i * ps].rearrange("(h a d) n -> a d h n", h=HP, a=2)[par]
                            at = 64 * par + DH8 * (t0 + i)
                            sp.dma_start(heads[at:at + DH8, w, :, :], src).then_inc(s["heads_loaded"], 16)
            for e in range(NE):
                if e >= 2:
                    sp.wait_ge(s["w2_psum"], 2 * (e - 1))
                sp.dma_start(w1[:, e % 2, :], w1_in[e]).then_inc(w_in[e % 2], 16)
                sp.dma_start(w3[:, e % 2, :], w3_in[e]).then_inc(w_in[e % 2], 16)
                sp.dma_start(w2[:, e % 2, :, :], w2_in[e].rearrange("(c p) d -> p c d", p=P)).then_inc(w_in[e % 2], 16)
            sp.wait_ge(s["x5_ready"], 2)
            for b in range(B):
                sp.dma_start(out[b].rearrange("(t p) d -> p t d", p=P), x[:, TB * b:TB * (b + 1), :]).then_inc(s["out_done"], 16)
            sp.wait_ge(s["out_done"], 32)

        @block.tensor
        def _(pe):
            ident = cst("ident")

            def transpose_y(i):
                for b in range(B):
                    for t in range(TB * b, TB * b + TB):
                        pe.wait_ge(y_ready, NT * i + t + 1)
                        last = pe.transpose(bank[b][:, (t % TB) * P:(t % TB + 1) * P], y[:, t, :], ident)
                    last.then_inc(yT_psum, 1)

            pe.wait_ge(loaded["const_a"], 16)
            pe.wait_ge(loaded["wqk0"], 16)
            pe.wait_ge(s["rfbd_ready"], 1)
            for w in range(2):
                pe.matmul(bank[4 + w], lhsT=wqk0[:, w, :], rhs=rf_bd[:, :, :], start=True, stop=True).then_inc(s["wf_psum"], 1)
            transpose_y(0)
            pe.wait_ge(loaded["wqkv0"], 16)
            for t in range(NT):
                if t % TB == 0:
                    pe.wait_ge(yT_ready, YT0[0] + t // TB + 1)
                if t >= 2:
                    pe.wait_ge(s["v_ready"], t - 1)
                pe.matmul(bank[2 + t % 2][:, 0:3 * D], lhsT=yT[:, t * P:(t + 1) * P], rhs=wqkv0[:, :],
                          start=True, stop=True).then_inc(s["qkv_psum"], 1)
            pe.wait_ge(s["wf_ready"], 2)
            for u in range(16):
                if u >= 4:
                    pe.wait_ge(s["frac_ready"], u - 3)
                if u < NT:
                    l, r = yT[:, u * P:(u + 1) * P], wf[:, 1, :]
                else:
                    b, c = divmod(u - NT, FC)
                    l, r = wf[:, 0, c * P:(c + 1) * P], yT[:, b * S:(b + 1) * S]
                pe.matmul(bank[4 + u % 4], lhsT=l, rhs=r, start=True, stop=True).then_inc(s["proj_psum"], 1)
            pe.wait_ge(s["vext_ready"], 2)
            for b in range(B):
                pe.wait_ge(s["feat_ready"], 2 * TB * (b + 1))
                for f in range(2):
                    for c in range(FC):
                        for t in range(TB * b, TB * b + TB):
                            last = pe.matmul(bank[2 + b][:, (f * FC + c) * 36:(f * FC + c + 1) * 36],
                                             lhsT=kfeat[:, t, f, c * P:(c + 1) * P], rhs=vext0[:, t, 4 * c:4 * c + 4, :],
                                             start=(t == TB * b), stop=(t == TB * b + TB - 1))
                last.then_inc(s["kv_psum"], 1)
            pe.wait_ge(s["frac_ready"], 16)
            for b in range(B):
                pe.wait_ge(s["kv_ready"], b + 1)
                pe.wait_ge(s["feat_ready"], 2 * (NT + FC * (b + 1)))
                if b:
                    pe.wait_ge(s["o_ready"], 1)
                for t in range(TB * b, TB * b + TB):
                    for c in range(FC):
                        for f in range(2):
                            last = pe.matmul(bank[4 + t % TB][:, c * 36:(c + 1) * 36], lhsT=qfeat[:, c, f, t * P:(t + 1) * P],
                                             rhs=kv_bd[:, b, f * FC + c, :, :], start=(f == 0), stop=(f == 1))
                last.then_inc(s["qkvo_psum"], 1)
            pe.wait_ge(loaded["wo0"], 16)
            for b in range(B):
                pe.wait_ge(s["o_ready"], b + 1)
                for t in range(TB * b, TB * b + TB):
                    last = pe.transpose(bank[b][:, (t % TB) * P:(t % TB + 1) * P], tmp[:, t, :], ident)
                last.then_inc(s["oT_psum"], 1)
            for b in range(B):
                pe.wait_ge(s["oT_ready"], b + 1)
                for t in range(TB * b, TB * b + TB):
                    last = pe.matmul(bank[2 + b][:, (t % TB) * D:(t % TB + 1) * D], lhsT=oT[:, t * P:(t + 1) * P], rhs=wo0[:, :],
                                     start=True, stop=True)
                last.then_inc(s["wo_psum"], 1)

            pe.wait_ge(loaded["const_b"], 16)
            pe.wait_ge(s["identbf_ready"], 1)
            pe.wait_ge(s["wq_ready"], 1)
            wps = bank[6].bitcast(BF16)
            for c in range(2 * NFC):
                last = pe.transpose(wps[:, c * P:(c + 1) * P], wq_bf[:, c * P:(c + 1) * P], ident_bf[:, :])
            last.then_inc(s["wT_psum"], 1)
            wps = bank[7].bitcast(BF16)
            for c in range(NFC):
                n = P if c < NFC - 1 else FFL
                at = 2 * NFC * P + c * P
                last = pe.transpose(wps[0:n, c * P:(c + 1) * P], wq_bf[:, at:at + n], ident_bf[:, :])
            last.then_inc(s["wT_psum"], 1)
            pe.wait_ge(s["wT_ready"], 2)
            pe.transpose(bank[6][0:1, 0:P], wscale[:, 2 * NFC:2 * NFC + 1], ident).then_inc(s["wdrow_psum"], 1)
            pe.wait_ge(s["wdrow_ready"], 1)
            pe.matmul(bank[7][:, 0:P], lhsT=cst("ones", 1), rhs=wdrow[:, :], start=True, stop=True).then_inc(s["wdb_psum"], 1)

            pe.wait_ge(loaded["const_b"], 16)
            pe.wait_ge(s["len_ready"], 1)
            pe.matmul(bank[6][0:SC, 0:B], lhsT=cst("tri", SC), rhs=lens_f[:, :], start=True, stop=True).then_inc(s["cs_psum"], 1)
            for b in range(B):
                pe.wait_ge(s["hit_ready"], b + 1)
                pe.matmul(bank[6 + b][0:SC, :], lhsT=cst("ones", SC)[:, 0:SC], rhs=bhit[:, b, :],
                          start=True, stop=True).then_inc(s["cnt_psum"], 1)
            pe.wait_ge(s["onehot_ready"], 2)
            pe.wait_ge(s["upd_ready"], 1)
            pe.matmul(bank[6][0:SC, 0:B * D], lhsT=cst("lmat", SC), rhs=upd[:, :, :], start=True, stop=True).then_inc(s["dep_psum"], 1)

            transpose_y(1)
            pe.wait_ge(s["kx_ready"], 1)
            pe.wait_ge(s["vx_ready"], 2)

            def x_scores(t):
                if t % TB == 0:
                    pe.wait_ge(yT_ready, YT0[1] + t // TB + 1)
                if t >= 2:
                    pe.wait_ge(s["lx_ready"], t - 1)
                for g in range(2):
                    last = pe.matmul(bank[2 + 2 * (t % 2) + g][:, 0:4 * SC], lhsT=yT[:, t * P:(t + 1) * P],
                                     rhs=kx_bd[:, t // TB, 4 * g:4 * g + 4, :], start=True, stop=True)
                last.then_inc(s["sx_psum"], 1)

            pe.wait_ge(s["dep_ready"], 1)
            x_scores(0)
            for t in range(NT):
                if t + 1 < NT:
                    x_scores(t + 1)
                pe.wait_ge(s["px_ready"], t + 1)
                if t >= 1:
                    pe.wait_ge(s["pxT_ready"], t)
                for h in range(HX):
                    last = pe.transpose(bank[6 + h // 4][0:SC, (h % 4) * P:(h % 4 + 1) * P], lx[:, t % 2, h, :], ident)
                last.then_inc(s["pxT_psum"], 1)
                pe.wait_ge(s["pxT_ready"], t + 1)
                if t >= 2:
                    pe.wait_ge(s["ox_used"], t - 1)
                if t == 0:
                    pe.wait_ge(yT_ready, YT0[1] + 2)
                for h in range(HX):
                    last = pe.matmul(bank[t % 2][:, h * W17:(h + 1) * W17], lhsT=pxT[:, t % 2, h * P:(h + 1) * P],
                                     rhs=vx[:, t // TB, h, :], start=True, stop=True)
                last.then_inc(s["ox_psum"], 1)

            pe.wait_ge(s["amax_ready"], 1)
            pe.transpose(bank[2][0:1, 0:P], amax[:, 0:1], ident).then_inc(s["amaxT_psum"], 1)
            pe.wait_ge(s["gsc_ready"], 1)
            pe.matmul(bank[3][:, 0:2], lhsT=cst("ones", 1), rhs=gsc[:, 0, :], start=True, stop=True).then_inc(s["gscb_psum"], 1)
            xps = bank[4].bitcast(BF16)
            pe.wait_ge(s["xq_ready"], 1)
            for t in range(NT):
                last = pe.transpose(xps[:, t * P:(t + 1) * P], xq[:, t * P:(t + 1) * P], ident_bf[:, :])
            last.then_inc(s["xqT_psum"], 1)
            pe.wait_ge(s["xqT_ready"], 1)
            pe.wait_ge(s["act_ready"], 1)
            for u in range(2 * NFC):
                c, b = divmod(u, 2)
                if u >= 3:
                    pe.wait_ge(s["hf_ready"], u - 2)
                for w in range(2):
                    last = pe.matmul(bank[2 + 2 * (u % 3) + w], lhsT=wguT[:, (w * NFC + c) * P:(w * NFC + c + 1) * P],
                                     rhs=xqT[:, b * S:(b + 1) * S], start=True, stop=True)
                last.then_inc(s["gu_psum"], 1)
            pe.wait_ge(s["hmax_ready"], 1)
            pe.transpose(bank[0][0:1, 0:P], amax[:, 1:2], ident).then_inc(s["hmaxT_psum"], 1)
            pe.wait_ge(s["gsh_ready"], 1)
            pe.matmul(bank[1][:, 0:2], lhsT=cst("ones", 1), rhs=gsc[:, 1, :], start=True, stop=True).then_inc(s["gshb_psum"], 1)
            pe.wait_ge(s["hq_ready"], NFC)
            for b in range(B):
                for t in range(TB * b, TB * b + TB):
                    for c in range(NFC):
                        n = P if c < NFC - 1 else FFL
                        last = pe.matmul(bank[2 + b][:, (t % TB) * D:(t % TB + 1) * D], lhsT=hq[0:n, c, t * P:(t + 1) * P],
                                         rhs=wdT[0:n, c * P:(c + 1) * P], start=(c == 0), stop=(c == NFC - 1))
                last.then_inc(s["down_psum"], 1)

            transpose_y(3)
            pe.wait_ge(loaded["wqkv1"], 16)
            for b in range(B):
                pe.wait_ge(yT_ready, YT0[3] + b + 1)
                for w in range(2):
                    pe.matmul(bank[2 + 2 * b + w], lhsT=wqkv1[:, w * D:(w + 1) * D], rhs=yT[:, b * S:(b + 1) * S],
                              start=True, stop=True).then_inc(s["q1_psum"], 1)
            for b in range(B):
                for t in range(TB * b, TB * b + TB):
                    last = pe.matmul(bank[6 + b][:, (t % TB) * D:(t % TB + 1) * D], lhsT=yT[:, t * P:(t + 1) * P],
                                     rhs=wqkv1[:, 2 * D:3 * D], start=True, stop=True)
                last.then_inc(s["v1_psum"], 1)
            pe.wait_ge(s["heads_loaded"], 2 * 2 * NTERM * 16)
            pe.wait_ge(s["vpad_ready"], 4)

            def scores(i):
                if i >= 4:
                    pe.wait_ge(s["tw_ready"], i - 2)
                pair, q = i // NPSTEP, (i % NPSTEP) // 2
                b, hp = divmod(pair, HP)
                for a in range(2):
                    rows = slice(64 * a, 64 * a + KS)
                    pe.matmul(bank[(i + a) % 4], lhsT=heads[rows, 0, hp, b * S + q * P:b * S + (q + 1) * P],
                              rhs=heads[rows, 1, hp, b * S:(b + 1) * S], start=True, stop=True).then_inc(s["scores_psum"], 1)

            def turn(i):
                by_pool = i % NPSTEP in POOL_STEPS
                pe.wait_ge(s["shifted_pool"] if by_pool else s["shifted_dve"], shifted_before(i, by_pool) + 1)
                if i >= 2:
                    pe.wait_ge(s["p_ready"], i - 1)
                for k in range(4):
                    last = pe.transpose(bank[4 + i % 2][:, k * P:(k + 1) * P], tw[:, i % 8, k * P:(k + 1) * P], ident)
                last.then_inc(s["t_psum"], 1)

            def values(pair, a):
                b, hp = divmod(pair, HP)
                pe.wait_ge(s["p_ready"], NPSTEP * pair + NPSTEP - 1 + a)
                if a == 0 and pair >= 2:
                    pe.wait_ge(s["oraw_ready"], pair - 1)
                for k in range(4):
                    last = pe.matmul(bank[6 + pair % 2][32 * k:32 * k + 32, :], lhsT=vpad[:, b * TB + k, 2 * hp + a, :],
                                     rhs=pT[:, pair % 2, a, k, :], start=(a == 0), stop=(a == 1), tile_position=(0, 32 * k))
                last.then_inc(s["pv_done"], 1)

            def fold(pair):
                pe.wait_ge(s["oT1_ready"], pair + 1)
                for q in range(4):
                    last = pe.matmul(bank[6 + pair % 2][:, q * W18:(q + 1) * W18], lhsT=oT1[:, pair % 2, q * P:(q + 1) * P],
                                     rhs=cst("fold"), start=True, stop=True)
                last.then_inc(s["o_psum"], 1)

            scores(0)
            scores(2)
            for i in range(0, NPSTEP * NPAIR, 2):
                pair, q = i // NPSTEP, (i % NPSTEP) // 2
                if i + 4 < NPSTEP * NPAIR:
                    scores(i + 4)
                turn(i)
                turn(i + 1)
                if pair >= 1 and q < 2:
                    values(pair - 1, q)
                if pair >= 1 and q == 3:
                    fold(pair - 1)
            values(NPAIR - 1, 0)
            values(NPAIR - 1, 1)
            fold(NPAIR - 1)

            pe.wait_ge(s["oraw_ready"], NPAIR)
            transpose_y(4)
            pe.wait_ge(s["dep_ready"], 1)
            pe.wait_ge(s["wing_ready"], 1)
            for b in range(B):
                pe.wait_ge(yT_ready, YT0[4] + b + 1)
                for t in range(TB * b, TB * b + TB):
                    o = bank[2 + b][:, (t % TB) * D:(t % TB + 1) * D]
                    pe.matmul(o, lhsT=yT[:, t * P:(t + 1) * P], rhs=win[:, :], start=True, stop=False)
                    pe.matmul(o, lhsT=cst("ones", 1), rhs=bin_row[:, :], start=False, stop=False)
                    last = pe.matmul(o, lhsT=onehot[:, b, (t % TB) * P:(t % TB + 1) * P], rhs=depool[:, b, :],
                                     start=False, stop=True)
                last.then_inc(s["e_psum"], 1)

            transpose_y(5)
            pe.wait_ge(loaded["wg"], 16)
            for t in range(NT):
                if t % TB == 0:
                    pe.wait_ge(yT_ready, YT0[5] + t // TB + 1)
                last = pe.matmul(bank[2][:, t * NE:(t + 1) * NE], lhsT=yT[:, t * P:(t + 1) * P], rhs=wg[:, :],
                                 start=True, stop=True)
            last.then_inc(s["lg_psum"], 1)
            pe.wait_ge(s["s_ready"], 1)
            for t in range(NT):
                last = pe.transpose(bank[3 + t // TB][0:NE, (t % TB) * P:(t % TB + 1) * P], sc8[:, t, :], ident)
            last.then_inc(s["sT_psum"], 1)
            pe.wait_ge(s["sT_ready"], 1)
            for b in range(B):
                last = pe.matmul(bank[5 + b], lhsT=cst("rowsel", NE), rhs=sT[:, b * S:(b + 1) * S], start=True, stop=True)
            last.then_inc(s["sbc_psum"], 1)
            for r in range(len(SEL_SHIFTS) + 1):
                pe.wait_ge(s["flag_ready"], r + 1)
                pe.matmul(bank[7][:, r:r + 1], lhsT=group_bf[:, :], rhs=flag[:, :], start=True, stop=True).then_inc(s["digit_psum"], 1)
                if r == len(SEL_SHIFTS) - 1:
                    break
            pe.wait_ge(s["selmask_ready"], 1)
            for t in range(NT):
                last = pe.transpose(bank[3 + t // TB][:, (t % TB) * P:(t % TB + 1) * P], selmask[:, t * P:(t + 1) * P], ident)
            last.then_inc(s["smaskT_psum"], 1)

            pe.wait_ge(s["smask_ready"], 1)
            for e in range(NE):
                pe.wait_ge(w_in[e % 2], 48 * (e // 2 + 1))
                pe.wait_ge(s["ys_ready"], e + 1)
                if e >= 1:
                    pe.wait_ge(s["acc_done"], 2 * e)
                for b in range(B):
                    if e >= 1:
                        pe.wait_ge(s["ysT_ready"], 2 * e - 1 + b)
                    for t in range(TB * b, TB * b + TB):
                        last = pe.transpose(bank[b][:, (t % TB) * P:(t % TB + 1) * P], ys[:, e % 2, t, :], ident)
                    last.then_inc(s["ysT_psum"], 1)
                for u in range(4):
                    c, b = divmod(u, 2)
                    g = 4 * e + u
                    pe.wait_ge(s["ysT_ready"], 2 * e + b + 1)
                    if g >= 2:
                        pe.wait_ge(s["h_ready"], g - 1)
                    for w, ww in enumerate((w1, w3)):
                        last = pe.matmul(bank[2 + 2 * (u % 2) + w], lhsT=ww[:, e % 2, c * P:(c + 1) * P],
                                         rhs=ysT[:, e % 2, b * S:(b + 1) * S], start=True, stop=True)
                    last.then_inc(s["ab_psum"], 1)
                pe.wait_ge(s["h_ready"], 4 * e + 4)
                for b in range(B):
                    for t in range(TB * b, TB * b + TB):
                        for c in range(2):
                            last = pe.matmul(bank[6 + b][:, (t % TB) * D:(t % TB + 1) * D], lhsT=hmoe[:, c, t * P:(t + 1) * P],
                                             rhs=w2[:, e % 2, c, :], start=(c == 0), stop=(c == 1))
                    last.then_inc(s["w2_psum"], 1)

        @block.scalar
        def _(act):
            links = [0]

            def link(ins):
                links[0] += 1
                ins.then_inc(s["act_chain"], 1)
                act.wait_ge(s["act_chain"], links[0])

            def copy(o, i):
                return act.activation(o, i, ACT.Copy)

            def norm(i, turn=True):
                act.wait_ge(var_ready, VAR0[i] + 1)
                if i == 0:
                    act.wait_ge(loaded["const_a"], 16)
                act.activation(std[:, :], mv[:, :, 1], ACT.Sqrt, bias=cst("eps")).then_inc(std_ready, 1)
                if turn:
                    for b in range(B):
                        act.wait_ge(yT_psum, YT0[i] + b + 1)
                        copy(yT[:, b * S:(b + 1) * S], bank[b]).then_inc(yT_ready, 1)

            for w in range(2):
                act.wait_ge(s["wf_psum"], w + 1)
                copy(wf[:, w, :], bank[4 + w]).then_inc(s["wf_ready"], 1)
            norm(0)
            for t in range(NT):
                act.wait_ge(s["qkv_psum"], t + 1)
                if t >= 2:
                    act.wait_ge(s["nsq_ready"], t - 1)
                act.activation(sq[:, t % 2, :], bank[2 + t % 2][:, 0:2 * D], ACT.Square).then_inc(s["sq_ready"], 1)
                copy(v_tok[:, t, :], bank[2 + t % 2][:, 2 * D:3 * D]).then_inc(s["v_ready"], 1)
            act.wait_ge(s["nsq_ready"], NT)
            act.activation(fscale[:, :, :], nsq[:, :, :], ACT.Exp, scale=-0.5).then_inc(s["fexp_ready"], 1)
            for u in range(16):
                act.wait_ge(s["fabs_ready"], u + 1)
                if u < NT:
                    o = [kfeat[:, u, f, :] for f in range(2)]
                else:
                    b, c = divmod(u - NT, FC)
                    o = [qfeat[:, c, f, b * S:(b + 1) * S] for f in range(2)]
                act.activation(o[0], frac[:, u % 3, :], ACT.Sin, scale=TWO_PI).then_inc(s["feat_ready"], 1)
                act.activation(o[1], fabs[:, u % 3, :], ACT.Sin, scale=-TWO_PI, bias=cst("halfpi")).then_inc(s["feat_ready"], 1)
            for b in range(B):
                act.wait_ge(s["oT_psum"], b + 1)
                copy(oT[:, b * S:(b + 1) * S], bank[b]).then_inc(s["oT_ready"], 1)

            act.wait_ge(loaded["clips"], 16)
            act.activation(clipe[:, :], clips[:, :], ACT.Exp, scale=-1.0).then_inc(s["clip_exp"], 1)
            act.wait_ge(s["wT_psum"], 1)
            copy(wguT[:, :], bank[6].bitcast(BF16)[:, 0:2 * NFC * P]).then_inc(s["wT_ready"], 1)
            act.wait_ge(s["wT_psum"], 2)
            wps = bank[7].bitcast(BF16)
            copy(wdT[:, 0:(NFC - 1) * P], wps[:, 0:(NFC - 1) * P])
            copy(wdT[0:FFL, (NFC - 1) * P:NFC * P], wps[0:FFL, (NFC - 1) * P:NFC * P]).then_inc(s["wT_ready"], 1)
            act.wait_ge(loaded["ctx"], 16)
            for b in range(B):
                act.activation(csq[:, :], ctx_sb[:, b, :], ACT.Square, accum_out=csum[:, b:b + 1]).then_inc(s["csq_ready"], 1)
                act.wait_ge(s["csq_ready"], b + 1)
            act.activation(csum[:, :], csum[:, :], ACT.Sqrt, scale=1.0 / CTX, bias=cst("eps", SC)).then_inc(s["cstd_ready"], 1)

            norm(1)
            for t in range(NT):
                act.wait_ge(s["lx_ready"], t + 1)
                act.activation(lx[:, t % 2, :, :], lx[:, t % 2, :, :], ACT.Exp).then_inc(s["px_ready"], 1)
                act.wait_ge(s["pxT_psum"], t + 1)
                if t >= 2:
                    act.wait_ge(s["ox_psum"], t - 1)
                copy(pxT[:, t % 2, :].rearrange("p (a n) -> p a n", a=2), psum[0:SC, 6:8, :]).then_inc(s["pxT_ready"], 1)

            norm(2, turn=False)
            act.wait_ge(s["xqT_psum"], 1)
            copy(xqT[:, :], bank[4].bitcast(BF16)).then_inc(s["xqT_ready"], 1)
            act.wait_ge(s["act_ready"], 2)
            for u in range(2 * NFC):
                c, b = divmod(u, 2)
                act.wait_ge(s["gu_psum"], u + 1)
                if u >= 4:
                    act.wait_ge(s["hf_ready"], u - 3)
                act.activation(sg[:, u % 4, :], bank[2 + 2 * (u % 3)], ACT.Silu, scale=iscale[:, c:c + 1]).then_inc(s["sg_ready"], 1)

            norm(3)
            for n in range(4):
                b, w = divmod(n, 2)
                act.wait_ge(s["q1_psum"], n + 1)
                copy(part[:, w, 0, b * S:(b + 1) * S], bank[2 + n]).then_inc(s["part1_ready"], 1)
            for n in range(4):
                b, w = divmod(n, 2)
                act.wait_ge(s["resid1_ready"], n + 1)
                copy(part[:, w, 1, b * S:(b + 1) * S], resid[:, w, b * S:(b + 1) * S]).then_inc(s["part2_ready"], 1)
            act.wait_ge(s["vpad_ready"], 2)
            for b in range(B):
                act.wait_ge(s["v1_psum"], b + 1)
                v = bank[6 + b].rearrange("p (t h a d) -> p (t h) a d", t=TB, h=HP, a=2)
                dst = vpad[:, b * TB:(b + 1) * TB, :, :].rearrange("p t (h a) c -> p (t h) a c", a=2)
                copy(dst[:, :, 0, 0:DH8], v[:, :, 0, :])
                copy(dst[:, :, 1, W9:W9 + DH8], v[:, :, 1, :]).then_inc(s["vpad_ready"], 1)

            for i in range(NPSTEP * NPAIR + NPSTEP):
                pair, j = divmod(i, NPSTEP)
                if pair < NPAIR:
                    act.wait_ge(s["t_psum"], i + 1)
                    if pair >= 2:
                        act.wait_ge(s["pv_done"], 2 * (pair - 2) + 1 + i % 2)
                    act.activation(pT[:, pair % 2, i % 2, :, (j // 2) * P:(j // 2 + 1) * P],
                                   bank[4 + i % 2].rearrange("p (k n) -> p k n", k=4), ACT.Exp).then_inc(s["p_ready"], 1)
                if pair >= 1 and j == 4:
                    act.wait_ge(s["pv_done"], 2 * pair)
                    copy(oT1[:, (pair - 1) % 2, :], bank[6 + (pair - 1) % 2]).then_inc(s["oT1_ready"], 1)
                if pair >= 1 and j == 7:
                    b, hp = divmod(pair - 1, HP)
                    act.wait_ge(s["o_psum"], pair)
                    copy(oraw[:, TB * b:TB * (b + 1), 2 * hp:2 * hp + 2, :].rearrange("p t h d -> p t (h d)"),
                         bank[6 + (pair - 1) % 2][:, 0:TB * W18].rearrange("p (t d) -> p t d", t=TB)).then_inc(s["oraw_ready"], 1)
            act.wait_ge(s["lno_var"], 1)
            act.activation(std[:, :], mv[:, :, 1], ACT.Sqrt, bias=cst("eps")).then_inc(s["lno_std"], 1)

            act.wait_ge(var_ready, VAR0[4] + 1)
            act.activation(std[:, :], mv[:, :, 1], ACT.Sqrt, bias=cst("eps")).then_inc(std_ready, 1)
            act.wait_ge(var_ready, VAR0[4] + 2)
            act.activation(rms[:, :], rms[:, :], ACT.Sqrt, bias=cst("eps")).then_inc(std_ready, 1)
            for b in range(B):
                act.wait_ge(yT_psum, YT0[4] + b + 1)
                copy(yT[:, b * S:(b + 1) * S], bank[b]).then_inc(yT_ready, 1)

            norm(5)
            act.wait_ge(s["lgm_ready"], 1)
            act.activation(lg[:, :, :], lg[:, :, :], ACT.Exp).then_inc(s["lge_ready"], 1)
            act.wait_ge(s["sT_psum"], 1)
            copy(sT[:, :].rearrange("p (a n) -> p a n", a=2), psum[0:NE, 3:5, :]).then_inc(s["sT_ready"], 1)
            act.wait_ge(s["sbc_psum"], 1)
            copy(sbc[:, :].rearrange("p (a n) -> p a n", a=2), psum[:, 5:7, :]).then_inc(s["sbc_ready"], 1)
            for e in range(NE):
                for b in range(B):
                    act.wait_ge(s["ysT_psum"], 2 * e + b + 1)
                    copy(ysT[:, e % 2, b * S:(b + 1) * S], bank[b]).then_inc(s["ysT_ready"], 1)
                for u in range(4):
                    g = 4 * e + u
                    act.wait_ge(s["ab_psum"], g + 1)
                    if g >= 4:
                        act.wait_ge(s["h_ready"], g - 3)
                    act.activation(sg[:, u, :], bank[2 + 2 * (u % 2)], ACT.Silu).then_inc(s["silu_ready"], 1)

        @block.gpsimd
        def _(pool):
            links = [0]

            def link(ins):
                links[0] += 1
                ins.then_inc(s["pool_chain"], 1)
                pool.wait_ge(s["pool_chain"], links[0])

            pool.wait_ge(loaded["const_a"], 16)
            pool.wait_ge(loaded["ctxkT"], 16)
            for b in range(B):
                ins = pool.tensor_tensor(kx_bd[:, b, :, :], ctxkT[:, b, :].unsqueeze(1).to_broadcast([P, HX, SC]),
                                         cst("bd8").unsqueeze(2).to_broadcast([P, HX, SC]), ALU.mult)
            ins.then_inc(s["kx_ready"], 1)
            pool.wait_ge(loaded["ctx"], 16)
            pool.memset(vx[:, :, :, :], 1.0).then_inc(s["vx_ready"], 1)
            pool.wait_ge(s["vx_ready"], 1)
            pool.tensor_copy(vx[:, :, :, 0:DX], ctx_sb[:, :, D:2 * D].rearrange("p b (h d) -> p b h d", h=HX)).then_inc(s["vx_ready"], 1)
            pool.memset(vpad[:, :, :, :], 0.0).then_inc(s["vpad_ready"], 1)
            pool.wait_ge(s["vpad_ready"], 1)
            ones = vpad[:, :, :, :].rearrange("p t (h a) c -> p (t h) a c", a=2)
            pool.memset(ones[:, :, 0, DH8:W9], 1.0)
            pool.memset(ones[:, :, 1, W9 + DH8:W18], 1.0).then_inc(s["vpad_ready"], 1)
            for i in range(NPSTEP * NPAIR):
                if i % NPSTEP not in POOL_STEPS:
                    continue
                pool.wait_ge(s["tw_ready"], i + 1)
                pool.tensor_scalar(tw[:, i % 8, :], tw[:, i % 8, :], tmax[:, i % 8:i % 8 + 1], None,
                                   ALU.subtract).then_inc(s["shifted_pool"], 1)
            pool.wait_ge(s["s_ready"], 1)
            for e in range(NE):
                if e >= 2:
                    pool.wait_ge(s["ysT_psum"], 2 * (e - 1))
                pool.tensor_tensor(ys[:, e % 2, :, :], y[:, :, :], sc8[:, :, e:e + 1].to_broadcast([P, NT, D]),
                                   ALU.mult).then_inc(s["ys_ready"], 1)

        @block.vector
        def _(dve):
            links = [0]

            def link(ins):
                links[0] += 1
                ins.then_inc(s["dve_chain"], 1)
                dve.wait_ge(s["dve_chain"], links[0])

            def moments(src):
                for t in range(NT):
                    last = dve.bn_stats(stats[:, t, :], src[:, t, :])
                link(last)
                for t in range(NT):
                    last = dve.bn_aggr(mv[:, t, :], stats[:, t, :])
                return last

            def norm(i):
                moments(x).then_inc(var_ready, 1)
                dve.wait_ge(std_ready, VAR0[i] + 1)
                link(dve.reciprocal(rstd[:, :], std[:, :]))
                for t in range(NT):
                    dve.tensor_scalar(y[:, t, :], x[:, t, :], mv[:, t, 0:1], rstd[:, t:t + 1], ALU.subtract,
                                      ALU.mult).then_inc(y_ready, 1)

            def quantise(dst, src, inv):
                if inv is not None:
                    link(dve.tensor_scalar(src, src, inv, QMAX, ALU.mult, ALU.min))
                else:
                    link(dve.tensor_scalar(src, src, QMAX, None, ALU.min))
                link(dve.tensor_scalar(src, src, -QMAX - 1.0, MAGIC, ALU.max, ALU.add))
                return dve.tensor_scalar(dst, src, MAGIC, None, ALU.subtract)

            dve.wait_ge(loaded["const_a"], 16)
            dve.wait_ge(loaded["rf"], 16)
            dve.scalar_tensor_tensor(rf_bd[:, :, :], rf[:, :].unsqueeze(1).to_broadcast([P, H16, M_RF]), 1.0 / (2 * math.pi),
                                     cst("bd16").unsqueeze(2).to_broadcast([P, H16, M_RF]), ALU.mult, ALU.mult).then_inc(s["rfbd_ready"], 1)
            dve.tensor_copy(ident_bf[:, :], cst("ident")).then_inc(s["identbf_ready"], 1)
            dve.wait_ge(in_x, 32)
            norm(0)
            for t in range(NT):
                dve.wait_ge(s["sq_ready"], t + 1)
                dve.tensor_reduce(nsq[:, t, :], sq[:, t % 2, :].rearrange("p (h d) -> p h d", d=DH8), AX.X, ALU.add).then_inc(s["nsq_ready"], 1)
            dve.wait_ge(s["fexp_ready"], 1)
            link(dve.tensor_scalar(fscale[:, :, :], fscale[:, :, :], M_RF ** -0.5, None, ALU.mult))
            dve.wait_ge(s["v_ready"], NT)
            k_sc = fscale[:, :, H16:2 * H16]
            dve.tensor_tensor(vext0[:, :, :, 0:DH8], v_tok[:, :, :].rearrange("p t (h d) -> p t h d", h=H16),
                              k_sc.unsqueeze(3).to_broadcast([P, NT, H16, DH8]), ALU.mult).then_inc(s["vext_ready"], 1)
            dve.tensor_copy(vext0[:, :, :, DH8:W9], k_sc.unsqueeze(3)).then_inc(s["vext_ready"], 1)

            def kv(b):
                dve.wait_ge(s["kv_psum"], b + 1)
                dve.tensor_tensor(kv_bd[:, b, :, :, :], bank[2 + b][:, 0:2 * FC * 36].rearrange("p (c g d) -> p c g d", g=4, d=W9),
                                  cst("bd4").unsqueeze(1).unsqueeze(3).to_broadcast([P, 2 * FC, 4, W9]), ALU.mult).then_inc(s["kv_ready"], 1)

            for u in range(16):
                dve.wait_ge(s["proj_psum"], u + 1)
                if u >= 3:
                    dve.wait_ge(s["feat_ready"], 2 * (u - 2))
                link(dve.tensor_scalar(turns[:, u % 2, :], bank[4 + u % 4], MAGIC, MAGIC, ALU.add, ALU.subtract))
                dve.tensor_tensor(frac[:, u % 3, :], bank[4 + u % 4], turns[:, u % 2, :], ALU.subtract).then_inc(s["frac_ready"], 1)
                dve.wait_ge(s["frac_ready"], u + 1)
                dve.tensor_scalar(fabs[:, u % 3, :].bitcast(I32), frac[:, u % 3, :].bitcast(I32), 0x7FFFFFFF, None,
                                  ALU.bitwise_and).then_inc(s["fabs_ready"], 1)
            for b in range(B):
                kv(b)
            for b in range(B):
                dve.wait_ge(s["qkvo_psum"], b + 1)
                q_sc = fscale[:, TB * b:TB * (b + 1), 0:H16]
                sums = psum[:, 4:8, 0:H16 * W9].rearrange("p t (h d) -> p t h d", d=W9)
                link(dve.tensor_tensor(zden[:, :, :].unsqueeze(3), sums[:, :, :, DH8:W9], q_sc.unsqueeze(3), ALU.mult))
                link(dve.tensor_scalar(zden[:, :, :], zden[:, :, :], 1e-6, None, ALU.max))
                link(dve.reciprocal(zrec[:, :, :], zden[:, :, :]))
                link(dve.tensor_tensor(zfac[:, :, :], zrec[:, :, :], q_sc, ALU.mult))
                dve.tensor_tensor(tmp[:, TB * b:TB * (b + 1), :].rearrange("p t (h d) -> p t h d", h=H16), sums[:, :, :, 0:DH8],
                                  zfac[:, :, :].unsqueeze(3).to_broadcast([P, TB, H16, DH8]), ALU.mult).then_inc(s["o_ready"], 1)

            def add_psum(b, first_bank, done):
                xs = x[:, TB * b:TB * (b + 1), :]
                dve.tensor_tensor(xs, xs, bank[first_bank + b].rearrange("p (t d) -> p t d", t=TB), ALU.add).then_inc(done, 1)
            for b in range(B):
                dve.wait_ge(s["wo_psum"], b + 1)
                add_psum(b, 2, s["x0_ready"])

            dve.wait_ge(loaded["const_b"], 16)
            nw = 2 * NFC * P
            dve.wait_ge(loaded["wgu"], 32)
            dve.tensor_reduce(wmax[:, 0:2 * NFC], wgu[:, 0:nw].rearrange("p (c n) -> p c n", n=P), AX.X, ALU.max, apply_absolute_value=True)
            link(dve.tensor_reduce(wmax[:, 2 * NFC:], wgu[:, nw:], AX.X, ALU.max, apply_absolute_value=True))
            link(dve.tensor_scalar(wscale[:, :], wmax[:, :], 1.0 / QMAX, None, ALU.mult))
            link(dve.reciprocal(winv[:, :], wscale[:, :]))
            dve.tensor_tensor(wgu[:, 0:nw].rearrange("p (c n) -> p c n", n=P), wgu[:, 0:nw].rearrange("p (c n) -> p c n", n=P),
                              winv[:, 0:2 * NFC].unsqueeze(2).to_broadcast([P, 2 * NFC, P]), ALU.mult)
            link(dve.tensor_scalar(wgu[:, nw:], wgu[:, nw:], winv[:, 2 * NFC:], None, ALU.mult))
            quantise(wq_bf[:, :], wgu[:, :], None).then_inc(s["wq_ready"], 1)
            dve.wait_ge(s["wdrow_psum"], 1)
            dve.tensor_copy(wdrow[:, :], bank[6][0:1, 0:P]).then_inc(s["wdrow_ready"], 1)
            dve.wait_ge(s["wdb_psum"], 1)
            dve.tensor_copy(wdscale[:, :], bank[7][:, 0:P]).then_inc(s["wdb_used"], 1)
            dve.wait_ge(s["clip_exp"], 1)
            link(dve.tensor_scalar(clipf[:, :], clipe[:, :], 1.0, None, ALU.add))
            link(dve.reciprocal(clipf[:, :], clipf[:, :]))

            dve.wait_ge(loaded["lens"], 16)
            dve.wait_ge(loaded["const_b"], 16)
            dve.wait_ge(loaded["win"], 64)
            dve.tensor_copy(lens_f[:, :], lens_i[:, :]).then_inc(s["len_ready"], 1)
            dve.wait_ge(s["cs_psum"], 1)
            dve.tensor_scalar(bidx[:, 0, :], bank[6][0:SC, 0:B], -1.0, None, ALU.add)
            link(dve.tensor_scalar(bidx[:, 1, :], bank[6][0:SC, 0:B], S - 1.0, None, ALU.add))
            link(dve.memset(zeros[:, :], 0.0))
            for b in range(B):
                link(dve.tensor_scalar(bhit[:, b, :], cst("iota_l", SC), bidx[:, 0, b:b + 1], None, ALU.is_equal))
                dve.scalar_tensor_tensor(bhit[:, b, :], cst("iota_l", SC), bidx[:, 1, b:b + 1], bhit[:, b, :], ALU.is_equal,
                                         ALU.add).then_inc(s["hit_ready"], 1)
            for b in range(B):
                dve.wait_ge(s["cnt_psum"], b + 1)
                link(dve.tensor_scalar(bmask[:, :], bank[6 + b][0:SC, :], 1.0, None, ALU.min))
                link(dve.tensor_tensor_scan(bcum[:, :], bmask[:, :], zeros[:, :], 0.0, ALU.add, ALU.add))
                link(dve.tensor_scalar(bcum[:, :], bcum[:, :], -1.0, 0.0, ALU.add, ALU.max))
                link(dve.tensor_scalar(bcum[:, :], bcum[:, :], SC - 1.0, None, ALU.min))
                dve.tensor_scalar(onehot[:, b, :], bcum[:, :], cst("iota_p", SC), None, ALU.is_equal).then_inc(s["onehot_ready"], 1)
            dve.wait_ge(s["cstd_ready"], 1)
            link(dve.reciprocal(csum[:, :], csum[:, :]))
            for b in range(B):
                link(dve.tensor_scalar(upd[:, b, :], ctx_sb[:, b, 0:D], csum[:, b:b + 1], BCOEF, ALU.mult, ALU.mult))
                last = dve.tensor_tensor(upd[:, b, :], upd[:, b, :], ginit[:, :], ALU.mult)
            last.then_inc(s["upd_ready"], 1)
            dve.wait_ge(s["dep_psum"], 1)
            dve.tensor_copy(depool[:, :, :], bank[6][0:SC, 0:B * D].rearrange("p (b d) -> p b d", b=B)).then_inc(s["dep_ready"], 1)
            dve.tensor_scalar(win[:, :], win[:, :], gres[:, 0:1], None, ALU.mult).then_inc(s["wing_ready"], 1)

            dve.wait_ge(loaded["xmask"], 16)
            dve.wait_ge(loaded["bias0"], 16)
            link(dve.tensor_copy(xmask_f[:, :], xmask_i[:, :]))
            link(dve.tensor_scalar(xmask_f[:, :], xmask_f[:, :], 1.0, 1e30, ALU.subtract, ALU.mult))
            link(dve.tensor_scalar(xbias[:, :, :].rearrange("p b n -> p (b n)"), xmask_f[:, :], bias0[:, 0:1], None, ALU.add))
            dve.wait_ge(s["x0_ready"], 2)
            norm(1)

            def x_out(t):
                dve.wait_ge(s["ox_psum"], t + 1)
                o = bank[t % 2][:, 0:HX * W17].rearrange("p (h d) -> p h d", d=W17)
                link(dve.reciprocal(xrec[:, :].unsqueeze(2), o[:, :, DX:W17]))
                dve.tensor_tensor(tmp[:, t, :].rearrange("p (h d) -> p h d", h=HX), o[:, :, 0:DX],
                                  xrec[:, :].unsqueeze(2).to_broadcast([P, HX, DX]), ALU.mult).then_inc(s["ox_used"], 1)
                dve.wait_ge(s["ox_used"], t + 1)
                ins = dve.tensor_tensor(x[:, t, :], x[:, t, :], tmp[:, t, :], ALU.add)
                if t % TB == TB - 1:
                    ins.then_inc(s["x1_ready"], 1)

            for t in range(NT):
                dve.wait_ge(s["sx_psum"], t + 1)
                if t >= 2:
                    dve.wait_ge(s["pxT_psum"], t - 1)
                l = lx[:, t % 2, :, :]
                b0 = 2 + 2 * (t % 2)
                link(dve.tensor_tensor(l.rearrange("p (g h) n -> p g h n", g=2),
                                       psum[:, b0:b0 + 2, 0:4 * SC].rearrange("p g (h n) -> p g h n", n=SC),
                                       xbias[:, t // TB, :].unsqueeze(1).unsqueeze(1).to_broadcast([P, 2, 4, SC]), ALU.add))
                link(dve.tensor_reduce(nmx[:, t % 2, :], l, AX.X, ALU.max, negate=True))
                dve.tensor_tensor(l, l, nmx[:, t % 2, :].unsqueeze(2).to_broadcast([P, HX, SC]), ALU.add).then_inc(s["lx_ready"], 1)
                if t >= 1:
                    x_out(t - 1)
            x_out(NT - 1)

            dve.wait_ge(s["x1_ready"], 2)
            norm(2)

            def scale_of(k, src_bank, ready):
                link(dve.tensor_reduce(gmax[:, k:k + 1], bank[src_bank][0:1, 0:P], AX.X, ALU.max))
                link(dve.tensor_scalar(gsc[:, k, 0:1], gmax[:, k:k + 1], clipf[:, k:k + 1], 1.0 / QMAX, ALU.mult, ALU.mult))
                dve.reciprocal(gsc[:, k, 1:2], gsc[:, k, 0:1]).then_inc(ready, 1)
            dve.wait_ge(y_ready, 3 * NT)
            dve.tensor_reduce(amax[:, 0:1], y[:, :, :], AX.XY, ALU.max, apply_absolute_value=True).then_inc(s["amax_ready"], 1)
            dve.wait_ge(s["amaxT_psum"], 1)
            scale_of(0, 2, s["gsc_ready"])
            dve.wait_ge(s["gscb_psum"], 1)
            dve.tensor_copy(act_sc[:, 0, :], bank[3][:, 0:2]).then_inc(s["act_ready"], 1)
            dve.wait_ge(s["act_ready"], 1)
            dve.tensor_scalar(iscale[:, :], wscale[:, 0:2 * NFC], act_sc[:, 0, 0:1], None, ALU.mult).then_inc(s["act_ready"], 1)
            quantise(xq[:, :], y[:, :, :].rearrange("p t d -> p (t d)"), act_sc[:, 0, 1:2]).then_inc(s["xq_ready"], 1)
            dve.wait_ge(s["act_ready"], 2)
            for u in range(2 * NFC):
                c, b = divmod(u, 2)
                dve.wait_ge(s["sg_ready"], u + 1)
                h = hf[:, c, b * S:(b + 1) * S]
                dve.scalar_tensor_tensor(h, bank[3 + 2 * (u % 3)], iscale[:, NFC + c:NFC + c + 1], sg[:, u % 4, :], ALU.mult,
                                         ALU.mult).then_inc(s["hf_ready"], 1)
                dve.wait_ge(s["hf_ready"], u + 1)
                last = dve.tensor_reduce(hmax[:, u:u + 1], h, AX.X, ALU.max, apply_absolute_value=True)
            link(last)
            dve.tensor_reduce(amax[:, 1:2], hmax[:, :], AX.X, ALU.max).then_inc(s["hmax_ready"], 1)
            dve.wait_ge(s["hmaxT_psum"], 1)
            scale_of(1, 0, s["gsh_ready"])
            dve.wait_ge(s["gshb_psum"], 1)
            link(dve.tensor_copy(act_sc[:, 1, :], bank[1][:, 0:2]))
            for c in range(NFC):
                quantise(hq[:, c, :], hf[:, c, :], act_sc[:, 1, 1:2]).then_inc(s["hq_ready"], 1)
            for b in range(B):
                dve.wait_ge(s["down_psum"], b + 1)
                ts_ = tmp[:, TB * b:TB * (b + 1), :]
                xs = x[:, TB * b:TB * (b + 1), :]
                link(dve.scalar_tensor_tensor(ts_, bank[2 + b].rearrange("p (t d) -> p t d", t=TB), act_sc[:, 1, 0:1],
                                              wdscale[:, :].unsqueeze(1).to_broadcast([P, TB, D]), ALU.mult, ALU.mult))
                dve.tensor_tensor(xs, xs, ts_, ALU.add).then_inc(s["x2_ready"], 1)

            dve.wait_ge(s["x2_ready"], 2)
            norm(3)
            for n in range(4):
                b, w = divmod(n, 2)
                dve.wait_ge(s["part1_ready"], n + 1)
                h = slice(b * S, (b + 1) * S)
                dve.tensor_tensor(resid[:, w, h], bank[2 + n], part[:, w, 0, h], ALU.subtract).then_inc(s["resid1_ready"], 1)
            for n in range(4):
                b, w = divmod(n, 2)
                dve.wait_ge(s["part2_ready"], n + 1)
                h = slice(b * S, (b + 1) * S)
                dve.tensor_tensor(part[:, w, 2, h], resid[:, w, h], part[:, w, 1, h], ALU.subtract).then_inc(s["part3_ready"], 1)

            dve.wait_ge(loaded["const_b"], 16)
            for i in range(NPSTEP * NPAIR + 1):
                if i < NPSTEP * NPAIR:
                    dve.wait_ge(s["scores_psum"], i + 1)
                    if i >= 8:
                        dve.wait_ge(s["t_psum"], i - 7)
                    at = (S - P) - ((i % NPSTEP) // 2) * P
                    dve.tensor_tensor_reduce(out=tw[:, i % 8, :], in0=bank[i % 4], in1=cst("dist")[:, at:at + S], scale=1.0,
                                             scalar=-3.0e38, op0=ALU.mult, op1=ALU.max,
                                             accum_out=tmax[:, i % 8:i % 8 + 1]).then_inc(s["tw_ready"], 1)
                if i >= 1 and (i - 1) % NPSTEP not in POOL_STEPS:
                    o = (i - 1) % 8
                    dve.wait_ge(s["tw_ready"], i)
                    dve.tensor_scalar(tw[:, o, :], tw[:, o, :], tmax[:, o:o + 1], None, ALU.subtract).then_inc(s["shifted_dve"], 1)
            dve.wait_ge(s["oraw_ready"], NPAIR)
            link(dve.reciprocal(nsq[:, :, 0:H16].unsqueeze(3), oraw[:, :, :, DH8:W9]))
            link(dve.tensor_tensor(tmp[:, :, :].rearrange("p t (h d) -> p t h d", h=H16), oraw[:, :, :, 0:DH8],
                                   nsq[:, :, 0:H16].unsqueeze(3).to_broadcast([P, NT, H16, DH8]), ALU.mult))
            moments(tmp).then_inc(s["lno_var"], 1)
            dve.wait_ge(s["lno_std"], 1)
            link(dve.reciprocal(rstd[:, :], std[:, :]))
            for t in range(NT):
                last = dve.tensor_scalar(tmp[:, t, :], tmp[:, t, :], mv[:, t, 0:1], rstd[:, t:t + 1], ALU.subtract, ALU.mult)
            link(last)
            dve.wait_ge(loaded["gb"], 32)
            link(dve.tensor_tensor(tmp[:, :, :], tmp[:, :, :], gamma[:, :].unsqueeze(1).to_broadcast([P, NT, D]), ALU.mult))
            link(dve.tensor_tensor(tmp[:, :, :], tmp[:, :, :], beta[:, :].unsqueeze(1).to_broadcast([P, NT, D]), ALU.add))
            dve.tensor_tensor(x[:, :, :], x[:, :, :], tmp[:, :, :], ALU.add).then_inc(s["x3_ready"], 2)

            dve.wait_ge(s["x3_ready"], 2)
            moments(x).then_inc(var_ready, 1)
            dve.wait_ge(std_ready, VAR0[4] + 1)
            link(dve.reciprocal(rstd[:, :], std[:, :]))
            link(dve.tensor_tensor(rms[:, :], rstd[:, :], rstd[:, :], ALU.mult))
            dve.tensor_tensor(rms[:, :], rms[:, :], mv[:, :, 1], ALU.mult).then_inc(var_ready, 1)
            dve.wait_ge(std_ready, VAR0[4] + 2)
            link(dve.reciprocal(rms[:, :], rms[:, :]))
            link(dve.tensor_tensor(rstd[:, :], rstd[:, :], rms[:, :], ALU.mult))
            for t in range(NT):
                dve.tensor_scalar(y[:, t, :], x[:, t, :], mv[:, t, 0:1], rstd[:, t:t + 1], ALU.subtract,
                                  ALU.mult).then_inc(y_ready, 1)
            for b in range(B):
                dve.wait_ge(s["e_psum"], b + 1)
                add_psum(b, 2, s["x4_ready"])

            dve.wait_ge(s["x4_ready"], 2)
            norm(5)
            dve.tensor_copy(group_bf[:, :], cst("group"))
            dve.wait_ge(s["lg_psum"], 1)
            lgp = bank[2][:, 0:NT * NE].rearrange("p (t e) -> p t e", e=NE)
            link(dve.tensor_reduce(smx[:, :], lgp, AX.X, ALU.max))
            dve.tensor_tensor(lg[:, :, :], lgp, smx[:, :].unsqueeze(2).to_broadcast([P, NT, NE]), ALU.subtract).then_inc(s["lgm_ready"], 1)
            dve.wait_ge(s["lge_ready"], 1)
            link(dve.tensor_reduce(smx[:, :], lg[:, :, :], AX.X, ALU.add))
            link(dve.reciprocal(smx[:, :], smx[:, :]))
            dve.tensor_tensor(sc8[:, :, :], lg[:, :, :], smx[:, :].unsqueeze(2).to_broadcast([P, NT, NE]), ALU.mult).then_inc(s["s_ready"], 1)
            dve.wait_ge(s["sbc_ready"], 1)
            dve.wait_ge(loaded["jbits"], 16)
            link(dve.memset(thr[:, :], 0))
            for r, sh in enumerate(SEL_SHIFTS):
                link(dve.tensor_tensor(cand[:, :], thr[:, :], jbits[:, r:r + 1], ALU.bitwise_or))
                link(dve.tensor_scalar(selw[:, 0, :], sbc[:, :], cand[:, :].bitcast(F32), None, ALU.is_ge, ALU.add, accum_out=cnt[:, 0:1]))
                dve.tensor_scalar(flag[:, :], cnt[:, 0:1], float(CAP), None, ALU.is_ge).then_inc(s["flag_ready"], 1)
                dve.wait_ge(s["digit_psum"], r + 1)
                if sh >= 0:
                    link(dve.tensor_scalar(digit[:, :], bank[7][:, r:r + 1], -1.0, None, ALU.add))
                    link(dve.tensor_scalar(digit[:, :], digit[:, :], sh, None, ALU.logical_shift_left))
                else:
                    link(dve.tensor_scalar(digit[:, :], bank[7][:, r:r + 1], 2.0 ** sh, -1.0, ALU.mult, ALU.add))
                link(dve.tensor_tensor(thr[:, :], thr[:, :], digit[:, :], ALU.bitwise_or))
            tf = thr[:, :].bitcast(F32)
            link(dve.tensor_scalar(selw[:, 0, :], sbc[:, :], tf, None, ALU.is_gt, ALU.add, accum_out=cnt[:, 1:2]))
            link(dve.tensor_scalar(need[:, :], cnt[:, 1:2], -1.0, float(CAP), ALU.mult, ALU.add))
            link(dve.tensor_scalar(selw[:, 1, :], sbc[:, :], tf, None, ALU.is_equal))
            link(dve.tensor_tensor_scan(selw[:, 2, :], selw[:, 1, :], selw[:, 1, :], 0.0, ALU.add, ALU.max))
            link(dve.scalar_tensor_tensor(selw[:, 1, :], selw[:, 2, :], need[:, 0:1], selw[:, 1, :], ALU.is_le, ALU.mult))
            dve.tensor_tensor(selmask[:, :], selw[:, 0, :], selw[:, 1, :], ALU.add).then_inc(s["selmask_ready"], 1)
            dve.wait_ge(s["smaskT_psum"], 1)
            dve.tensor_copy(smask[:, :, :].rearrange("p (a t) e -> p a t e", a=2),
                            psum[:, 3:5, :].rearrange("p a (t e j) -> p a t e j", e=NE, j=SEL_J)[:, :, :, :, 0]).then_inc(s["smask_ready"], 1)
            dve.wait_ge(s["smask_ready"], 1)
            for e in range(NE):
                for u in range(4):
                    c, b = divmod(u, 2)
                    g = 4 * e + u
                    dve.wait_ge(s["silu_ready"], g + 1)
                    if u == 0 and e >= 1:
                        dve.wait_ge(s["w2_psum"], 2 * e)
                    dve.tensor_tensor(hmoe[:, c, b * S:(b + 1) * S], bank[3 + 2 * (u % 2)], sg[:, u, :], ALU.mult).then_inc(s["h_ready"], 1)
                for b in range(B):
                    dve.wait_ge(s["w2_psum"], 2 * e + b + 1)
                    if b == 0 and e >= 1:
                        dve.wait_ge(s["acc_done"], 2 * e)
                    for t in range(TB * b, TB * b + TB):
                        ins = dve.scalar_tensor_tensor(x[:, t, :], bank[6 + b][:, (t % TB) * D:(t % TB + 1) * D], smask[:, t, e:e + 1],
                                                       x[:, t, :], ALU.mult, ALU.add)
                    ins.then_inc(s["acc_done"], 1)
            dve.wait_ge(s["acc_done"], 2 * NE)
            dve.sem_inc(s["x5_ready"], 2)


def kernel(**inputs):
    a = {k: np.asarray(v) for k, v in inputs.items()}
    import concourse.bacc as bacc
    from concourse.bass_utils import run_bass_kernel_spmd

    def pad_rows(w):
        return np.concatenate([w, w[:NFC * P - FF]], axis=0)
    jb = np.zeros((P, len(SEL_SHIFTS)), np.int32)
    for r, sh in enumerate(SEL_SHIFTS):
        j = np.arange(P) % SEL_J
        jb[:, r] = j << sh if sh >= 0 else j >> -sh
    data = {
        "x": a["x"],
        "ctx": a["ctx_2048"],
        "ctxkT": a["ctx_2048"][:, :, :D].transpose(2, 0, 1),
        "xmask": a["mask_BxS2_ik0"].reshape(-1),
        "lens": a["mask_BxS2_if0"].T,
        "wqkv0": np.concatenate([a["L0_attn_wq"].T, a["L0_attn_wk"].T, a["L0_attn_wv"].T], axis=1),
        "wqk0": np.stack([a["L0_attn_wq"], a["L0_attn_wk"]], axis=1),
        "wo0": a["L0_attn_wo"].T,
        "rf": np.tile(a["L0_attn_rf"].T, (H16, 1)),
        "bias0": a["L0_xattn_b"],
        "clips": np.stack([a["L0_ffn_clip_x"], a["L0_ffn_clip_down"]], axis=1),
        "wgu": np.concatenate([pad_rows(a["L0_ffn_w_gate"]), pad_rows(a["L0_ffn_w_up"])], axis=0),
        "wd": a["L0_ffn_w_down"],
        "wqkv1": np.concatenate([a["L1_attn_Wq"].T, a["L1_attn_Wk"].T, a["L1_attn_Wv"].T], axis=1),
        "gamma": a["L1_attn_ln_gamma"],
        "beta": a["L1_attn_ln_beta"],
        "win": a["L1_xattn_W_in"].T,
        "bin": a["L1_xattn_b_in"],
        "gres": a["L1_xattn_g_res"][:, None],
        "ginit": a["L1_xattn_g_init"],
        "wg": a["L1_ffn_wg"],
        "w1": a["L1_ffn_w1"],
        "w3": a["L1_ffn_w3"],
        "w2": a["L1_ffn_w2"],
        "const": constants(),
        "jbits": jb,
    }
    nc = bacc.Bacc("TRN2", target_bir_lowering=False, num_devices=1)
    arrays, args = {}, []
    for name, v in data.items():
        v = np.ascontiguousarray(v)
        arrays["in_" + name] = v
        args.append(nc.dram_tensor("in_" + name, v.shape, mybir.dt.from_np(v.dtype), kind="ExternalInput").ap())
    res = nc.dram_tensor("out_x", (B, S, D), F32, kind="ExternalOutput").ap()
    parts = nc.dram_tensor("qk_parts", (2, 3, P, NT * P), BF16, kind="Internal").ap()
    build(nc, *args, res, parts)
    r = run_bass_kernel_spmd(nc, [arrays], core_ids=[0])
    return r.results[0]["out_x"]
```

```python
import math
from contextlib import ExitStack

import numpy as np

import concourse.bass as bass
import concourse.mybir as mybir

ACT = mybir.ActivationFunctionType
ALU = mybir.AluOpType
AX = mybir.AxisListType
F32 = mybir.dt.float32
BF16 = mybir.dt.bfloat16
I32 = mybir.dt.int32

P = 128
B = 2
S = 512
D = 128
NT = B * S // P
TB = NT // B
H16, DH8 = 16, 8
M_RF = 32
FC = H16 * M_RF // P
HX, DX = 8, 16
SC = 77
CTX = 256
FF = 352
NFC = (FF + P - 1) // P
FFL = FF - (NFC - 1) * P
NE, HID, CAP = 8, 256, 512
EPS = 1e-5
MAGIC = 1.5 * 2.0 ** 23
QMAX = 127.0
TWO_PI = 6.2831850
DT = -math.log(-math.expm1(-0.001))
DECAY = math.exp(-DT)
BCOEF = math.exp(-0.001)
W9 = DH8 + 1
W17 = DX + 1
TERM_RUNS = ((0, 3, 0, 0), (3, 2, 1, 0), (5, 1, 2, 0))
HEADS_BY_POOL = ((0, 0, 0),)
NTERM = 6
KS = NTERM * DH8
HP = H16 // 2
NPAIR = B * HP
NPSTEP = 8
W18 = 2 * W9
POOL_STEPS = (0, 3, 6)


def shifted_before(i, by_pool):
    return sum(((n % NPSTEP) in POOL_STEPS) == by_pool for n in range(i))

SEL_J = 16
SEL_SHIFTS = (26, 22, 18, 14, 10, 6, 2, -2)

CONST = {}
_at = 0
for _name, _n in (("ident", P), ("halfpi", 1), ("eps", 1), ("eps2", 1), ("iota_p", 1), ("bd16", H16), ("bd8", HX), ("bd4", 4),
                  ("group", P), ("lmat", SC), ("tri", SC), ("ones", P),
                  ("fold", W18), ("dist", 2 * S - P), ("iota_l", S)):
    CONST[_name] = (_at, _at + _n)
    _at += _n
NCONST = _at


def constants():
    c = np.zeros((P, NCONST), np.float32)
    p = np.arange(P)

    def put(name, a):
        lo, hi = CONST[name]
        c[:a.shape[0], lo:hi] = a
    put("ident", np.eye(P))
    put("halfpi", np.full((P, 1), math.pi / 2))
    put("eps", np.full((P, 1), EPS))
    put("eps2", np.full((P, 1), EPS * EPS))
    put("iota_p", p[:, None])
    put("bd16", p[:, None] // DH8 == np.arange(H16)[None])
    put("bd8", (p[:, None] // DX == np.arange(HX)[None]) * DX ** -0.5)
    put("bd4", p[:, None] // M_RF == np.arange(4)[None])
    put("group", p[:, None] // SEL_J == p[None] // SEL_J)
    put("fold", (p[:, None] % 32) == np.arange(W18)[None])
    s = np.arange(SC)
    lag = s[None] - s[:, None]
    put("lmat", np.where(lag >= 0, DECAY ** np.maximum(lag, 0).astype(np.float64), 0.0))
    put("tri", lag >= 0)
    put("ones", np.ones((P, P)))
    put("dist", np.abs(p[:, None] - (np.arange(2 * S - P)[None] - (S - P))) / S * D ** -0.5)
    put("iota_l", np.tile(np.arange(S)[None], (P, 1)))
    return c


def build(nc, x_in, ctx_in, ctxkT_in, xmask_in, lens_in, wqkv0_in, wqk0_in, wo0_in, rf_in, bias0_in, clips_in,
          wgu_in, wd_in, wqkv1_in, gamma_in, beta_in, win_in, bin_in, gres_in, ginit_in,
          wg_in, w1_in, w3_in, w2_in, const_in, jbits_in, out, parts_dram):
    with ExitStack() as ctx:
        def sb(name, shape, dt=F32):
            return ctx.enter_context(nc.sbuf_tensor(name, shape, dt))

        def sem(name):
            return ctx.enter_context(nc.semaphore(name))

        psum = ctx.enter_context(nc.psum_tensor("psum", [P, 8, 512], F32))
        const = sb("const", [P, NCONST])

        def cst(name, rows=P):
            lo, hi = CONST[name]
            return const[0:rows, lo:hi]

        x = sb("x", [P, NT, D])
        y = sb("y", [P, NT, D])
        yT = sb("yT", [P, NT * P])
        tmp = sb("tmp", [P, NT, D])
        arena = sb("arena", [P, 5 * NT * P])
        stats = sb("stats", [P, NT, 6])
        mv = sb("mv", [P, NT, 2])
        std = sb("std", [P, NT])
        rstd = sb("rstd", [P, NT])
        ident_bf = sb("ident_bf", [P, P], BF16)
        wqkv0 = sb("wqkv0", [P, 3 * D])
        wqk0 = sb("wqk0", [P, 2, D])
        wo0 = sb("wo0", [P, D])
        rf = sb("rf", [P, M_RF])
        rf_bd = sb("rf_bd", [P, H16, M_RF])
        wf = sb("wf", [P, 2, 512])
        sq = sb("sq", [P, 2, 2 * D])
        nsq = sb("nsq", [P, NT, 2 * H16])
        fscale = sb("fscale", [P, NT, 2 * H16])
        v_tok = tmp
        vext0 = sb("vext0", [P, NT, H16, W9])
        big = sb("big", [P, 16384])
        kfeat = big[:, 0:8192].rearrange("p (t s n) -> p t s n", t=NT, s=2)
        qfeat = big[:, 8192:16384].rearrange("p (c s n) -> p c s n", c=FC, s=2)
        ring = sb("ring", [P, 8, 512])
        turns, frac, fabs = ring[:, 0:2, :], ring[:, 2:5, :], ring[:, 5:8, :]
        sg = sb("sg", [P, 4, 512])
        kv_bd = sg[:, 0:2, :].rearrange("p a n -> p (a n)")[:, 0:B * 2 * FC * 4 * W9].rearrange("p (b c g d) -> p b c g d", b=B, c=2 * FC, g=4)
        zden = sb("zden", [P, TB, H16])
        zrec = sb("zrec", [P, TB, H16])
        zfac = sb("zfac", [P, TB, H16])
        oT = yT
        ctx_sb = sb("ctx_sb", [SC, B, CTX])
        ctxkT = sb("ctxkT", [P, B, SC])
        kx_bd = sb("kx_bd", [P, B, HX, SC])
        vx = sb("vx", [SC, B, HX, 32])
        oxs = big[:, 5120:5632].rearrange("p (k n) -> p k n", k=2)
        xmask_i = sb("xmask_i", [P, B * SC], I32)
        xmask_f = sb("xmask_f", [P, B * SC])
        xbias = sb("xbias", [P, B, SC])
        bias0 = sb("bias0", [P, 1])
        lx = big[:, 0:3 * HX * SC].rearrange("p (k h n) -> p k h n", k=3, h=HX)
        nmx = sb("nmx", [P, 3, HX])
        pxT = big[0:SC, 2048:2048 + 2 * HX * P].rearrange("p (k n) -> p k n", k=2)
        xrec = sb("xrec", [P, HX])
        clips = sb("clips", [1, 2])
        clipe = sb("clipe", [1, 2])
        clipf = sb("clipf", [1, 2])
        wgu = sb("wgu", [P, 2 * NFC * P + FF])
        wmax = sb("wmax", [P, 2 * NFC + 1])
        wscale = sb("wscale", [P, 2 * NFC + 1])
        winv = sb("winv", [P, 2 * NFC + 1])
        wq_bf = sb("wq_bf", [P, 2 * NFC * P + FF], BF16)
        wguT = sb("wguT", [P, 2 * NFC * P], BF16)
        wdT = sb("wdT", [P, NFC * P], BF16)
        wdrow = sb("wdrow", [1, P])
        wdscale = sb("wdscale", [P, P])
        amax = sb("amax", [P, 2])
        hmax = sb("hmax", [P, 2 * NFC])
        gmax = sb("gmax", [1, 2])
        gsc = sb("gsc", [1, 2, 2])
        act_sc = sb("act_sc", [P, 2, 2])
        iscale = sb("iscale", [P, 2 * NFC])
        xq = big[:, 4096:4608].bitcast(BF16)
        xqT = big[:, 4608:5120].bitcast(BF16)
        hf = arena[:, 0:NFC * NT * P].rearrange("p (c n) -> p c n", c=NFC)
        hq = arena[:, NFC * NT * P:].bitcast(BF16)[:, 0:NFC * NT * P].rearrange("p (c n) -> p c n", c=NFC)
        wqkv1 = sb("wqkv1", [P, 3 * D])
        heads = big[:, 0:8192].bitcast(BF16).rearrange("p (b w h n) -> p b w h n", b=B, w=2, h=HP)
        pT = big[:, 8192:16384].rearrange("p (s h k n) -> p s h k n", s=2, h=2, k=4)
        resid = arena[:, 0:2 * NT * P].rearrange("p (w n) -> p w n", w=2)
        part = arena[:, 2 * NT * P:].bitcast(BF16).rearrange("p (w k n) -> p w k n", w=2, k=3)
        vpad = sb("vpad", [P, NT, H16, 32])
        tw = ring
        oT1 = sg[:, 0:2, :]
        tmax = sb("tmax", [P, 8])
        gamma = sb("gamma", [P, D])
        beta = sb("beta", [P, D])
        win = sb("win", [P, D])
        bin_row = sg[0:1, 2, :]
        gres = sb("gres", [P, 1])
        ginit = sb("ginit", [SC, D])
        lens_i = sb("lens_i", [SC, B], I32)
        lens_f = sb("lens_f", [SC, B])
        bidx = sb("bidx", [SC, 2, B])
        bhit = arena[0:SC, 0:S].bitcast(BF16).rearrange("p (b n) -> p b n", b=B)
        ones_bf = sb("ones_bf", [SC, SC], BF16)
        bmask = arena[0:SC, 2 * S:3 * S]
        bcum = arena[0:SC, 3 * S:4 * S]
        onehot = sb("onehot", [SC, B, S])
        csum = sb("csum", [SC, B])
        csq = sg[0:SC, 3, 0:CTX]
        upd = sb("upd", [SC, B, D])
        depool = sb("depool", [SC, B, D])
        zeros = arena[0:SC, 4 * S:5 * S]
        wg = sb("wg", [P, NE])
        w1 = arena[:, 0:NE * HID].rearrange("p (e n) -> p e n", e=NE)
        w3 = arena[:, NE * HID:2 * NE * HID].rearrange("p (e n) -> p e n", e=NE)
        w2 = sb("w2", [P, NE, 2, D])
        smx = sb("smx", [P, NT])
        lg = sb("lg", [P, NT, NE])
        sc8 = sb("sc8", [P, NT, NE])
        sc16 = big[:, 15 * NT * P:16 * NT * P].rearrange("p (t n) -> p t n", t=NT)
        sbc = big[:, 0:NT * P]
        selw = big[:, NT * P:4 * NT * P].rearrange("p (k n) -> p k n", k=3)
        jbits = sb("jbits", [P, len(SEL_SHIFTS)], I32)
        thr = sb("thr", [P, 1], I32)
        cand = sb("cand", [P, 1], I32)
        cnt = sb("cnt", [P, 2])
        flag = sb("flag", [P, 1], BF16)
        digit = sb("digit", [P, 1], I32)
        need = sb("need", [P, 1])
        group_bf = sb("group_bf", [P, P], BF16)
        selmask = big[:, 4 * NT * P:5 * NT * P]
        smask = sb("smask", [P, NT, NE])
        ys = big[:, 5 * NT * P:7 * NT * P].rearrange("p (k t d) -> p k t d", k=2, t=NT)
        ysT = big[:, 7 * NT * P:9 * NT * P].rearrange("p (k n) -> p k n", k=2)
        hmoe = big[:, 9 * NT * P:15 * NT * P].rearrange("p (s k n) -> p s k n", s=3, k=2)

        in_x = [sem(f"in_x{b}") for b in range(B)]
        in_names = ["const_a", "const_b", "wqkv0", "wqk0", "wo0", "rf", "ctx", "ctxkT", "xmask", "bias0", "clips", "wgu",
                    "wqkv1", "gb", "win", "bin", "lens", "wg", "jbits"]
        loaded = {n: sem("in_" + n) for n in in_names}
        var_ready, std_ready, y_ready, yT_psum, yT_ready = (sem(n) for n in ("var_ready", "std_ready", "y_ready", "yT_psum", "yT_ready"))
        YT0 = (0, 2, None, 4, 6, 8)
        s = {n: sem(n) for n in (
            "dve_chain act_chain pool_chain identbf_ready rfbd_ready wf_psum wf_ready qkv_psum sq_ready v_ready nsq_ready fexp_ready vext_ready "
            "proj_psum turns_ready frac_ready fabs_ready feat_ready kv_psum kv_ready qkvo_psum o_ready oT_psum oT_ready wo_psum "
            "x0_ready kx_ready vx_ready xb_ready sx_psum sx_read nmx_ready lx_ready px_ready pxT_psum pxT_ready ox_psum oxs_ready oxt_psum ox_used x1_ready "
            "clip_exp wq_ready wT_psum wT_ready wdrow_psum wdrow_ready wdb_psum "
            "amax_ready amaxT_psum gsc_ready gscb_psum act_ready xq_ready xqT_psum xqT_ready gu_psum sg_ready hf_ready "
            "hmax_ready hmaxT_psum gsh_ready gshb_psum hq_ready down_psum x2_ready "
            "q1_psum part1_ready resid1_ready part2_ready part3_ready v1_psum vpad_ready "
            "scores_psum tw_ready shifted_pool shifted_dve oT1_ready o_psum t_psum p_ready pv_done wdb_used out1_ready lno_var lno_std x3_ready "
            "len_ready cs_psum hit_ready cnt_psum csq_ready cstd_ready upd_ready dep_psum dep_ready wing_ready onehot_ready e_psum "
            "x4_ready lg_psum lgm_ready lge_ready s_ready s16_ready sbc_psum sbc_ready flag_ready digit_psum "
            "selmask_ready smaskT_psum smask_ready ys_ready ysT_psum ysT_ready ab_psum silu_ready h_ready "
            "w2_psum acc_done out_done").split()}

        experts_in = sem("experts_in")
        heads_loaded = [sem(f"heads_loaded{b}") for b in range(B)]
        heads0_by_pool = sem("heads0_by_pool")
        parts_stored = [[sem(f"parts_stored{b}_{n}") for n in range(3)] for b in range(B)]


        bank = [psum[:, i, :] for i in range(8)]

        def load_heads(queue, b, m, ws=range(2), done=None):
            for w in ws:
                for first, n, q, k in TERM_RUNS:
                    if (q, k + n - 1)[w] != m:
                        continue
                    for par in range(2):
                        if w == 0:
                            src = parts_dram[b, 0, q, par].rearrange("d h n -> d (h n)").unsqueeze(0).to_broadcast([n, DH8, HP * S])
                        else:
                            src = parts_dram[b, 1, k:k + n, par].rearrange("m d h n -> m d (h n)")
                        at = 64 * par + DH8 * first
                        queue.dma_start(heads[at:at + DH8 * n, b, w].rearrange("p h n -> p (h n)"), src).then_inc(done or heads_loaded[b], 16)

        block = ctx.enter_context(nc.Block())

        @block.sync
        def _(sp):
            n_a = CONST["bd4"][1]
            sp.dma_start(x[:, 0:TB, :], x_in[0].rearrange("(t p) d -> p t d", p=P)).then_inc(in_x[0], 16)
            sp.dma_start(x[:, TB:NT, :], x_in[1].rearrange("(t p) d -> p t d", p=P)).then_inc(in_x[1], 16)
            sp.dma_start(const[:, 0:n_a], const_in[:, 0:n_a]).then_inc(loaded["const_a"], 16)
            sp.dma_start(rf[:, :], rf_in).then_inc(loaded["rf"], 16)
            sp.dma_start(wqkv0[:, :], wqkv0_in).then_inc(loaded["wqkv0"], 16)
            sp.dma_start(wqk0[:, :, :], wqk0_in).then_inc(loaded["wqk0"], 16)
            sp.dma_start(const[:, n_a:], const_in[:, n_a:]).then_inc(loaded["const_b"], 16)
            sp.dma_start(wo0[:, :], wo0_in).then_inc(loaded["wo0"], 16)
            sp.dma_start(ctxkT[:, :, :], ctxkT_in).then_inc(loaded["ctxkT"], 16)
            sp.dma_start(ctx_sb[:, :, :], ctx_in.rearrange("b s c -> s b c")).then_inc(loaded["ctx"], 16)
            sp.dma_start(xmask_i[:, :], xmask_in.rearrange("(a n) -> a n", a=1).to_broadcast([P, B * SC])).then_inc(loaded["xmask"], 16)
            sp.dma_start(bias0[:, :], bias0_in.rearrange("(a n) -> a n", a=1).to_broadcast([P, 1])).then_inc(loaded["bias0"], 16)
            sp.dma_start(clips[:, :], clips_in).then_inc(loaded["clips"], 16)
            sp.dma_start(lens_i[:, :], lens_in).then_inc(loaded["lens"], 16)
            sp.dma_start(wgu[:, 0:2 * NFC * P].rearrange("p (c n) -> p c n", n=P),
                         wgu_in.rearrange("(c p) n -> p c n", p=P)).then_inc(loaded["wgu"], 16)
            sp.dma_start(wgu[:, 2 * NFC * P:], wd_in).then_inc(loaded["wgu"], 16)
            sp.dma_start(wqkv1[:, :], wqkv1_in).then_inc(loaded["wqkv1"], 16)

            def rows(v, n, r=P):
                return v.rearrange("(a n) -> a n", a=1).to_broadcast([r, n])
            sp.dma_start(gamma[:, :], rows(gamma_in, D)).then_inc(loaded["gb"], 16)
            sp.dma_start(beta[:, :], rows(beta_in, D)).then_inc(loaded["gb"], 16)
            sp.dma_start(win[:, :], win_in).then_inc(loaded["win"], 16)
            sp.dma_start(gres[:, :], gres_in).then_inc(loaded["win"], 16)
            sp.dma_start(ginit[:, :], rows(ginit_in[0:D], D, SC)).then_inc(loaded["win"], 16)
            sp.dma_start(wg[:, :], wg_in).then_inc(loaded["wg"], 16)
            sp.dma_start(jbits[:, :], jbits_in).then_inc(loaded["jbits"], 16)

            sp.wait_ge(s["hf_ready"], 2 * NFC)
            sp.dma_start(bin_row.rearrange("p (t d) -> p t d", t=TB),
                         bin_in.rearrange("(a b n) -> a b n", a=1, b=1).to_broadcast([1, TB, D])).then_inc(loaded["bin"], 16)
            for b in range(B):
                for n in range(3):
                    sp.wait_ge((s["part1_ready"], s["part2_ready"], s["part3_ready"])[n], 2 * (b + 1))
                    for w in range(2):
                        sp.dma_start(parts_dram[b, w, n].rearrange("a d h n -> h (a d) n"),
                                     part[:, w, n, b * S:(b + 1) * S]).then_inc(parts_stored[b][n], 16)
                for m in range(3):
                    sp.wait_ge(parts_stored[b][m], 2 * 16)
                    load_heads(sp, b, m, [w for w in range(2) if (b, m, w) not in HEADS_BY_POOL])
            sp.dma_start(w1[:, :, :], w1_in.rearrange("e d h -> d e h")).then_inc(experts_in, 16)
            sp.dma_start(w3[:, :, :], w3_in.rearrange("e d h -> d e h")).then_inc(experts_in, 16)
            sp.dma_start(w2[:, :, :, :], w2_in.rearrange("e (c p) d -> p e c d", p=P)).then_inc(experts_in, 16)
            for b in range(B):
                sp.wait_ge(s["acc_done"], 2 * NE - 1 + b)
                sp.dma_start(out[b].rearrange("(t p) d -> p t d", p=P), x[:, TB * b:TB * (b + 1), :]).then_inc(s["out_done"], 16)
            sp.wait_ge(s["out_done"], 32)

        @block.tensor
        def _(pe):
            ident = cst("ident")

            def transpose_y(i, halves=range(B)):
                for b in halves:
                    for t in range(TB * b, TB * b + TB):
                        pe.wait_ge(y_ready, NT * i + t + 1)
                        last = pe.transpose(bank[b][:, (t % TB) * P:(t % TB + 1) * P], y[:, t, :], ident)
                    last.then_inc(yT_psum, 1)

            pe.wait_ge(loaded["const_a"], 16)
            pe.wait_ge(loaded["wqk0"], 16)
            pe.wait_ge(s["rfbd_ready"], 1)
            for w in range(2):
                pe.matmul(bank[4 + w], lhsT=wqk0[:, w, :], rhs=rf_bd[:, :, :], start=True, stop=True).then_inc(s["wf_psum"], 1)
            transpose_y(0)
            pe.wait_ge(loaded["wqkv0"], 16)
            for t in range(NT):
                if t % TB == 0:
                    pe.wait_ge(yT_ready, YT0[0] + t // TB + 1)
                if t >= 2:
                    pe.wait_ge(s["v_ready"], t - 1)
                pe.matmul(bank[2 + t % 2][:, 0:3 * D], lhsT=yT[:, t * P:(t + 1) * P], rhs=wqkv0[:, :],
                          start=True, stop=True).then_inc(s["qkv_psum"], 1)
            pe.wait_ge(s["wf_ready"], 2)

            def project(u):
                if u >= 4:
                    pe.wait_ge(s["frac_ready"], u - 3)
                b, i = divmod(u, 2 * FC)
                if i < TB:
                    t = TB * b + i
                    l, r = yT[:, t * P:(t + 1) * P], wf[:, 1, :]
                else:
                    c = i - TB
                    l, r = wf[:, 0, c * P:(c + 1) * P], yT[:, b * S:(b + 1) * S]
                pe.matmul(bank[4 + u % 4], lhsT=l, rhs=r, start=True, stop=True).then_inc(s["proj_psum"], 1)

            def key_sums(b, c):
                pe.wait_ge(s["feat_ready"], 2 * (2 * FC * b + TB))
                for f in range(2):
                    for t in range(TB * b, TB * b + TB):
                        last = pe.matmul(bank[2 + b][:, (f * FC + c) * 36:(f * FC + c + 1) * 36],
                                         lhsT=kfeat[:, t, f, c * P:(c + 1) * P], rhs=vext0[:, t, 4 * c:4 * c + 4, :],
                                         start=(t == TB * b), stop=(t == TB * b + TB - 1))
                if c == FC - 1:
                    last.then_inc(s["kv_psum"], 1)

            def query_sums(b, c):
                pe.wait_ge(s["kv_ready"], b + 1)
                pe.wait_ge(s["feat_ready"], 2 * (2 * FC * b + TB + c + 1))
                if b:
                    pe.wait_ge(s["o_ready"], 1)
                for t in range(TB * b, TB * b + TB):
                    i = t % TB
                    for f in range(2):
                        last = pe.matmul(bank[i // 2][:, (i % 2) * H16 * W9 + c * 36:(i % 2) * H16 * W9 + (c + 1) * 36],
                                         lhsT=qfeat[:, c, f, t * P:(t + 1) * P],
                                         rhs=kv_bd[:, b, f * FC + c, :, :], start=(f == 0), stop=(f == 1))
                if c == FC - 1:
                    last.then_inc(s["qkvo_psum"], 1)

            def turn_o(b):
                pe.wait_ge(s["o_ready"], b + 1)
                for t in range(TB * b, TB * b + TB):
                    last = pe.transpose(bank[2 + b][:, (t % TB) * P:(t % TB + 1) * P], tmp[:, t, :], ident)
                last.then_inc(s["oT_psum"], 1)

            for u in range(4):
                project(u)
            pe.wait_ge(s["vext_ready"], 2)
            pe.wait_ge(yT_ready, YT0[0] + 2)
            pe.wait_ge(loaded["const_b"], 16)
            pe.wait_ge(s["len_ready"], 1)
            pe.matmul(bank[3][0:SC, S - B:S], lhsT=cst("tri", SC), rhs=lens_f[:, :], start=True, stop=True).then_inc(s["cs_psum"], 1)
            for i in range(16):
                if i + 4 < 16:
                    project(i + 4)
                if 4 <= i < 8:
                    key_sums(0, i - 4)
                elif 8 <= i < 12:
                    query_sums(0, i - 8)
                elif i >= 12:
                    key_sums(1, i - 12)
            turn_o(0)
            pe.wait_ge(s["frac_ready"], 16)
            for c in range(FC):
                query_sums(1, c)
                if c == 0:
                    for b in range(B):
                        pe.wait_ge(s["hit_ready"], b + 1)
                        pe.matmul(bank[6 + b][0:SC, :], lhsT=ones_bf[:, :], rhs=bhit[:, b, :],
                                  start=True, stop=True).then_inc(s["cnt_psum"], 1)
            pe.wait_ge(loaded["wo0"], 16)
            for b in range(B):
                if b:
                    turn_o(1)
                    pe.wait_ge(s["identbf_ready"], 1)
                    pe.wait_ge(s["wq_ready"], 1)
                    pe.wait_ge(s["onehot_ready"], 2)
                    wps = bank[6].bitcast(BF16)
                    for c in range(2 * NFC):
                        last = pe.transpose(wps[:, c * P:(c + 1) * P], wq_bf[:, c * P:(c + 1) * P], ident_bf[:, :])
                    last.then_inc(s["wT_psum"], 1)
                    wps = bank[7].bitcast(BF16)
                    for c in range(NFC):
                        n = P if c < NFC - 1 else FFL
                        at = 2 * NFC * P + c * P
                        last = pe.transpose(wps[0:n, c * P:(c + 1) * P], wq_bf[:, at:at + n], ident_bf[:, :])
                    last.then_inc(s["wT_psum"], 1)
                    pe.transpose(bank[2][0:1, 0:P], wscale[:, 2 * NFC:2 * NFC + 1], ident).then_inc(s["wdrow_psum"], 1)
                pe.wait_ge(s["oT_ready"], b + 1)
                for t in range(TB * b, TB * b + TB):
                    last = pe.matmul(bank[4 + b][:, (t % TB) * D:(t % TB + 1) * D], lhsT=oT[:, t * P:(t + 1) * P], rhs=wo0[:, :],
                                     start=True, stop=True)
                last.then_inc(s["wo_psum"], 1)
            pe.wait_ge(s["wdrow_ready"], 1)
            pe.matmul(bank[2][:, P:2 * P], lhsT=cst("ones", 1), rhs=wdrow[:, :], start=True, stop=True).then_inc(s["wdb_psum"], 1)

            transpose_y(1, (0,))
            pe.wait_ge(s["kx_ready"], 1)
            pe.wait_ge(s["vx_ready"], 2)

            def x_scores(t):
                if t % TB == 0:
                    pe.wait_ge(yT_ready, YT0[1] + t // TB + 1)
                if t >= 2:
                    pe.wait_ge(s["sx_read"], t - 1)
                for g in range(2):
                    last = pe.matmul(bank[2 + 2 * (t % 2) + g][:, 0:4 * SC], lhsT=yT[:, t * P:(t + 1) * P],
                                     rhs=kx_bd[:, t // TB, 4 * g:4 * g + 4, :], start=True, stop=True)
                last.then_inc(s["sx_psum"], 1)

            def x_turn(t):
                pe.wait_ge(s["px_ready"], t + 1)
                if t >= 1:
                    pe.wait_ge(s["pxT_ready"], t)
                for h in range(HX):
                    last = pe.transpose(bank[6 + h // 4][0:SC, (h % 4) * P:(h % 4 + 1) * P], lx[:, t % 3, h, :], ident)
                last.then_inc(s["pxT_psum"], 1)

            def x_values(t):
                pe.wait_ge(s["pxT_ready"], t + 1)
                if t >= 2:
                    pe.wait_ge(s["ox_used"], t - 1)
                for h in range(HX):
                    g, k = divmod(h, 4)
                    last = pe.matmul(bank[t % 2][32 * k:32 * k + 32, g * P:(g + 1) * P], lhsT=vx[:, t // TB, h, :],
                                     rhs=pxT[:, t % 2, h * P:(h + 1) * P], start=True, stop=True, tile_position=(0, 32 * k))
                last.then_inc(s["ox_psum"], 1)

            def x_turn_back(t):
                pe.wait_ge(s["oxs_ready"], t + 1)
                for g in range(2):
                    last = pe.transpose(bank[t % 2][:, (2 + g) * P:(3 + g) * P], oxs[:, t % 2, g * P:(g + 1) * P], ident)
                last.then_inc(s["oxt_psum"], 1)

            pe.wait_ge(s["wdb_used"], 1)
            x_scores(0)
            transpose_y(1, (1,))
            x_scores(1)
            pe.wait_ge(yT_ready, YT0[1] + 2)
            for t in range(NT):
                if t == 0:
                    pe.wait_ge(s["wT_ready"], 2)
                if t == NT - 1:
                    x_values(t - 1)
                x_turn(t)
                if t >= 2:
                    x_turn_back(t - 2)
                if t + 2 < NT:
                    x_scores(t + 2)
                if 1 <= t < NT - 1:
                    x_values(t - 1)
            x_values(NT - 1)
            x_turn_back(NT - 2)
            x_turn_back(NT - 1)

            pe.wait_ge(s["amax_ready"], 1)
            pe.transpose(bank[2][0:1, 0:P], amax[:, 0:1], ident).then_inc(s["amaxT_psum"], 1)
            pe.wait_ge(s["gsc_ready"], 1)
            pe.matmul(bank[3][:, 0:2], lhsT=cst("ones", 1), rhs=gsc[:, 0, :], start=True, stop=True).then_inc(s["gscb_psum"], 1)
            xps = [bank[b].bitcast(BF16) for b in range(B)]
            for b in range(B):
                pe.wait_ge(s["xq_ready"], b + 1)
                for t in range(TB * b, TB * b + TB):
                    last = pe.transpose(xps[b][:, (t % TB) * P:(t % TB + 1) * P], xq[:, t * P:(t + 1) * P], ident_bf[:, :])
                last.then_inc(s["xqT_psum"], 1)
            pe.wait_ge(s["act_ready"], 1)
            for u in range(2 * NFC):
                b, c = divmod(u, NFC)
                pe.wait_ge(s["xqT_ready"], b + 1)
                if u >= 3:
                    pe.wait_ge(s["hf_ready"], u - 2)
                for w in range(2):
                    last = pe.matmul(bank[2 + 2 * (u % 3) + w], lhsT=wguT[:, (w * NFC + c) * P:(w * NFC + c + 1) * P],
                                     rhs=xqT[:, b * S:(b + 1) * S], start=True, stop=True)
                last.then_inc(s["gu_psum"], 1)
            pe.wait_ge(s["hmax_ready"], 1)
            pe.transpose(bank[0][0:1, 0:P], amax[:, 1:2], ident).then_inc(s["hmaxT_psum"], 1)
            pe.wait_ge(s["gsh_ready"], 1)
            pe.matmul(bank[1][:, 0:2], lhsT=cst("ones", 1), rhs=gsc[:, 1, :], start=True, stop=True).then_inc(s["gshb_psum"], 1)
            for b in range(B):
                pe.wait_ge(s["hq_ready"], b + 1)
                for t in range(TB * b, TB * b + TB):
                    for c in range(NFC):
                        n = P if c < NFC - 1 else FFL
                        last = pe.matmul(bank[2 + b][:, (t % TB) * D:(t % TB + 1) * D], lhsT=hq[0:n, c, t * P:(t + 1) * P],
                                         rhs=wdT[0:n, c * P:(c + 1) * P], start=(c == 0), stop=(c == NFC - 1))
                last.then_inc(s["down_psum"], 1)

            pe.wait_ge(loaded["wqkv1"], 16)
            for b in range(B):
                transpose_y(3, (b,))
                pe.wait_ge(yT_ready, YT0[3] + b + 1)
                for w in range(2):
                    pe.matmul(bank[2 + 2 * b + w], lhsT=wqkv1[:, w * D:(w + 1) * D], rhs=yT[:, b * S:(b + 1) * S],
                              start=True, stop=True).then_inc(s["q1_psum"], 1)
            for b in range(B):
                for t in range(TB * b, TB * b + TB):
                    last = pe.matmul(bank[6 + b][:, (t % TB) * D:(t % TB + 1) * D], lhsT=yT[:, t * P:(t + 1) * P],
                                     rhs=wqkv1[:, 2 * D:3 * D], start=True, stop=True)
                last.then_inc(s["v1_psum"], 1)
            pe.wait_ge(s["vpad_ready"], 4)
            pe.wait_ge(s["upd_ready"], 1)
            pe.matmul(bank[1][0:SC, 0:B * D], lhsT=cst("lmat", SC), rhs=upd[:, :, :], start=True, stop=True).then_inc(s["dep_psum"], 1)
            pe.wait_ge(s["dep_ready"], 1)

            def scores(i):
                if i >= 4:
                    pe.wait_ge(s["tw_ready"], i - 2)
                pair, q = i // NPSTEP, (i % NPSTEP) // 2
                b, hp = divmod(pair, HP)
                if i == b * NPSTEP * HP:
                    by_pool = 2 * len(HEADS_BY_POOL) if b == 0 else 0
                    pe.wait_ge(heads_loaded[b], (2 * 2 * len(TERM_RUNS) - by_pool) * 16)
                    if b == 0:
                        pe.wait_ge(heads0_by_pool, by_pool * 16)
                for a in range(2):
                    rows = slice(64 * a, 64 * a + KS)
                    pe.matmul(bank[(i + a) % 4], lhsT=heads[rows, b, 0, hp, q * P:(q + 1) * P],
                              rhs=heads[rows, b, 1, hp, :], start=True, stop=True).then_inc(s["scores_psum"], 1)

            def turn(i):
                by_pool = i % NPSTEP in POOL_STEPS
                pe.wait_ge(s["shifted_pool"] if by_pool else s["shifted_dve"], shifted_before(i, by_pool) + 1)
                if i >= 2:
                    pe.wait_ge(s["p_ready"], i - 1)
                for k in range(4):
                    last = pe.transpose(bank[4 + i % 2][:, k * P:(k + 1) * P], tw[:, i % 8, k * P:(k + 1) * P], ident)
                last.then_inc(s["t_psum"], 1)

            def values(pair, a):
                b, hp = divmod(pair, HP)
                pe.wait_ge(s["p_ready"], NPSTEP * pair + NPSTEP - 1 + a)
                if a == 0 and pair >= 2:
                    pe.wait_ge(s["out1_ready"], pair - 1)
                for k in range(4):
                    last = pe.matmul(bank[6 + pair % 2][32 * k:32 * k + 32, :], lhsT=vpad[:, b * TB + k, 2 * hp + a, :],
                                     rhs=pT[:, pair % 2, a, k, :], start=(a == 0), stop=(a == 1), tile_position=(0, 32 * k))
                last.then_inc(s["pv_done"], 1)

            def fold(pair):
                pe.wait_ge(s["oT1_ready"], pair + 1)
                for q in range(4):
                    last = pe.matmul(bank[6 + pair % 2][:, q * W18:(q + 1) * W18], lhsT=oT1[:, pair % 2, q * P:(q + 1) * P],
                                     rhs=cst("fold"), start=True, stop=True)
                last.then_inc(s["o_psum"], 1)

            scores(0)
            scores(2)
            for i in range(0, NPSTEP * NPAIR, 2):
                pair, q = i // NPSTEP, (i % NPSTEP) // 2
                if i + 4 < NPSTEP * NPAIR:
                    scores(i + 4)
                turn(i)
                turn(i + 1)
                if pair >= 1 and q in (0, 2):
                    values(pair - 1, q // 2)
                if pair >= 2 and q == 1:
                    fold(pair - 2)
            values(NPAIR - 1, 0)
            fold(NPAIR - 2)
            values(NPAIR - 1, 1)
            fold(NPAIR - 1)

            pe.wait_ge(s["wing_ready"], 1)
            pe.wait_ge(loaded["bin"], 16)
            pe.wait_ge(s["tw_ready"], NPSTEP * NPAIR)
            for b in range(B):
                pe.matmul(bank[2 + b], lhsT=cst("ones", 1), rhs=bin_row, start=True, stop=False)
                for t in range(TB * b, TB * b + TB):
                    pe.matmul(bank[2 + b][:, (t % TB) * D:(t % TB + 1) * D], lhsT=onehot[:, b, (t % TB) * P:(t % TB + 1) * P],
                              rhs=depool[:, b, :], start=False, stop=False)
            for b in range(B):
                transpose_y(4, (b,))
                pe.wait_ge(yT_ready, YT0[4] + b + 1)
                for t in range(TB * b, TB * b + TB):
                    last = pe.matmul(bank[2 + b][:, (t % TB) * D:(t % TB + 1) * D], lhsT=yT[:, t * P:(t + 1) * P], rhs=win[:, :],
                                     start=False, stop=(t % TB == TB - 1))
                last.then_inc(s["e_psum"], 1)

            pe.wait_ge(loaded["wg"], 16)
            for t in range(NT):
                if t % TB == 0:
                    b = t // TB
                    transpose_y(5, (b,))
                    pe.wait_ge(yT_ready, YT0[5] + b + 1)
                    if b == 0:
                        pe.wait_ge(s["x4_ready"], 1)
                last = pe.matmul(bank[2][:, t * NE:(t + 1) * NE], lhsT=yT[:, t * P:(t + 1) * P], rhs=wg[:, :],
                                 start=True, stop=True)
            last.then_inc(s["lg_psum"], 1)
            pe.wait_ge(s["s16_ready"], 1)
            for b in range(B):
                for t in range(TB * b, TB * b + TB):
                    last = pe.transpose(bank[5 + b][:, (t % TB) * P:(t % TB + 1) * P], sc16[:, t, :], ident)
                last.then_inc(s["sbc_psum"], 1)

            def turn_ys(e):
                pe.wait_ge(s["ys_ready"], e + 1)
                for b in range(B):
                    if e >= 1:
                        pe.wait_ge(s["ysT_ready"], 2 * e - 1 + b)
                    for t in range(TB * b, TB * b + TB):
                        last = pe.transpose(bank[b][:, (t % TB) * P:(t % TB + 1) * P], ys[:, e % 2, t, :], ident)
                    last.then_inc(s["ysT_psum"], 1)

            def hidden(e, u):
                c, b = divmod(u, 2)
                g = 4 * e + u
                pe.wait_ge(s["ysT_ready"], 2 * e + b + 1)
                if g >= 2:
                    pe.wait_ge(s["h_ready"], g - 1)
                for w, ww in enumerate((w1, w3)):
                    last = pe.matmul(bank[2 + 2 * (u % 2) + w], lhsT=ww[:, e, c * P:(c + 1) * P],
                                     rhs=ysT[:, e % 2, b * S:(b + 1) * S], start=True, stop=True)
                last.then_inc(s["ab_psum"], 1)

            def down(e):
                pe.wait_ge(s["h_ready"], 4 * e + 4)
                if e >= 1:
                    pe.wait_ge(s["acc_done"], 2 * e)
                for b in range(B):
                    for t in range(TB * b, TB * b + TB):
                        for c in range(2):
                            last = pe.matmul(bank[6 + b][:, (t % TB) * D:(t % TB + 1) * D], lhsT=hmoe[:, e % 3, c, t * P:(t + 1) * P],
                                             rhs=w2[:, e, c, :], start=(c == 0), stop=(c == 1))
                    last.then_inc(s["w2_psum"], 1)

            turn_ys(0)
            pe.wait_ge(experts_in, 48)
            pe.wait_ge(s["sbc_ready"], 2)
            hidden(0, 0)
            for r in range(len(SEL_SHIFTS)):
                pe.wait_ge(s["flag_ready"], r + 1)
                pe.matmul(bank[7][:, r:r + 1], lhsT=group_bf[:, :], rhs=flag[:, :], start=True, stop=True).then_inc(s["digit_psum"], 1)
                e, u = divmod(r + 1, 4)
                if u == 2:
                    turn_ys(e + 1)
                hidden(e, u)
            for u in range(1, 4):
                hidden(2, u)
            pe.wait_ge(s["selmask_ready"], 1)
            for b in range(B):
                pe.wait_ge(s["ysT_ready"], 2 * 2 + b + 1)
                for t in range(TB * b, TB * b + TB):
                    last = pe.transpose(bank[b][:, (t % TB) * P:(t % TB + 1) * P], selmask[:, t * P:(t + 1) * P], ident)
            last.then_inc(s["smaskT_psum"], 1)
            down(0)
            pe.wait_ge(s["smask_ready"], 1)
            turn_ys(3)
            for e in range(3, NE):
                hidden(e, 0)
                hidden(e, 1)
                down(1 if e == 3 else e - 1)
                if e + 1 < NE:
                    turn_ys(e + 1)
                hidden(e, 2)
                hidden(e, 3)
                if e == 3:
                    down(2)
            down(NE - 1)

        @block.scalar
        def _(act):
            links = [0]

            def link(ins):
                links[0] += 1
                ins.then_inc(s["act_chain"], 1)
                act.wait_ge(s["act_chain"], links[0])

            def copy(o, i):
                return act.activation(o, i, ACT.Copy)

            def copy_yT(i, b):
                act.wait_ge(yT_psum, YT0[i] + b + 1)
                copy(yT[:, b * S:(b + 1) * S], bank[b]).then_inc(yT_ready, 1)

            def deviation(i, b, scale=1.0, bias="eps"):
                h = slice(TB * b, TB * (b + 1))
                act.wait_ge(var_ready, 2 * i + b + 1)
                act.activation(std[:, h], mv[:, h, 1], ACT.Sqrt, scale=scale, bias=cst(bias)).then_inc(std_ready, 1)

            def norm(i, turn=True, scale=1.0, bias="eps", apart=False):

                if i == 0:
                    act.wait_ge(loaded["const_a"], 16)
                for b in range(B):
                    deviation(i, b, scale, bias)
                    if apart:
                        copy_yT(i, b)
                if turn and not apart:
                    for b in range(B):
                        copy_yT(i, b)

            for w in range(2):
                act.wait_ge(s["wf_psum"], w + 1)
                copy(wf[:, w, :], bank[4 + w]).then_inc(s["wf_ready"], 1)
            norm(0)
            for t in range(NT):
                act.wait_ge(s["qkv_psum"], t + 1)
                if t >= 2:
                    act.wait_ge(s["nsq_ready"], t - 1)
                act.activation(sq[:, t % 2, :], bank[2 + t % 2][:, 0:2 * D], ACT.Square).then_inc(s["sq_ready"], 1)
                copy(v_tok[:, t, :], bank[2 + t % 2][:, 2 * D:3 * D]).then_inc(s["v_ready"], 1)
            act.wait_ge(s["nsq_ready"], NT)
            act.activation(fscale[:, :, :], nsq[:, :, :], ACT.Exp, scale=-0.5).then_inc(s["fexp_ready"], 1)
            act.wait_ge(loaded["clips"], 16)
            act.activation(clipe[:, :], clips[:, :], ACT.Exp, scale=-1.0).then_inc(s["clip_exp"], 1)
            for u in range(16):
                act.wait_ge(s["fabs_ready"], u + 1)
                b, i = divmod(u, 2 * FC)
                if i < TB:
                    o = [kfeat[:, TB * b + i, f, :] for f in range(2)]
                else:
                    o = [qfeat[:, i - TB, f, b * S:(b + 1) * S] for f in range(2)]
                act.activation(o[0], frac[:, u % 3, :], ACT.Sin, scale=TWO_PI).then_inc(s["feat_ready"], 1)
                act.activation(o[1], fabs[:, u % 3, :], ACT.Sin, scale=-TWO_PI, bias=cst("halfpi")).then_inc(s["feat_ready"], 1)
            for b in range(B):
                act.wait_ge(s["oT_psum"], b + 1)
                copy(oT[:, b * S:(b + 1) * S], bank[2 + b]).then_inc(s["oT_ready"], 1)

            norm(1, apart=True)
            act.wait_ge(s["wT_psum"], 1)
            copy(wguT[:, :], bank[6].bitcast(BF16)[:, 0:2 * NFC * P]).then_inc(s["wT_ready"], 1)
            act.wait_ge(s["wT_psum"], 2)
            wps = bank[7].bitcast(BF16)
            copy(wdT[:, 0:(NFC - 1) * P], wps[:, 0:(NFC - 1) * P])
            copy(wdT[0:FFL, (NFC - 1) * P:NFC * P], wps[0:FFL, (NFC - 1) * P:NFC * P]).then_inc(s["wT_ready"], 1)

            def copy_sums(t):
                act.wait_ge(s["ox_psum"], t + 1)
                if t >= 2:
                    act.wait_ge(s["oxt_psum"], t - 1)
                copy(oxs[:, t % 2, :], bank[t % 2][:, 0:2 * P]).then_inc(s["oxs_ready"], 1)

            for t in range(NT):
                act.wait_ge(s["lx_ready"], t + 1)
                act.activation(lx[:, t % 3, :, :], lx[:, t % 3, :, :], ACT.Exp).then_inc(s["px_ready"], 1)
                if t >= 2:
                    copy_sums(t - 2)
                act.wait_ge(s["pxT_psum"], t + 1)
                if t >= 2:
                    act.wait_ge(s["ox_psum"], t - 1)
                copy(pxT[:, t % 2, :].rearrange("p (a n) -> p a n", a=2), psum[0:SC, 6:8, :]).then_inc(s["pxT_ready"], 1)
            copy_sums(NT - 2)
            copy_sums(NT - 1)

            norm(2, turn=False)
            for b in range(B):
                act.wait_ge(s["xqT_psum"], b + 1)
                copy(xqT[:, b * S:(b + 1) * S], bank[b].bitcast(BF16)[:, 0:S]).then_inc(s["xqT_ready"], 1)
            act.wait_ge(s["act_ready"], 2)
            for u in range(2 * NFC):
                b, c = divmod(u, NFC)
                act.wait_ge(s["gu_psum"], u + 1)
                if u >= 4:
                    act.wait_ge(s["hf_ready"], u - 3)
                act.activation(sg[:, u % 4, :], bank[2 + 2 * (u % 3)], ACT.Silu, scale=iscale[:, c:c + 1]).then_inc(s["sg_ready"], 1)

            act.wait_ge(loaded["ctx"], 16)
            act.wait_ge(s["hf_ready"], 2 * NFC)
            for b in range(B):
                act.activation(csq[:, :], ctx_sb[:, b, :], ACT.Square, accum_out=csum[:, b:b + 1]).then_inc(s["csq_ready"], 1)
                act.wait_ge(s["csq_ready"], b + 1)
            act.activation(csum[:, :], csum[:, :], ACT.Sqrt, scale=1.0 / CTX, bias=cst("eps", SC)).then_inc(s["cstd_ready"], 1)
            for b in range(B):
                deviation(3, b)
                if b == 0:
                    copy_yT(3, 0)
            for b in range(B):
                h = slice(b * S, (b + 1) * S)
                for w in range(2):
                    act.wait_ge(s["q1_psum"], 2 * b + w + 1)
                    copy(part[:, w, 0, h], bank[2 + 2 * b + w]).then_inc(s["part1_ready"], 1)
                if b == 0:
                    copy_yT(3, 1)
                for w in range(2):
                    act.wait_ge(s["resid1_ready"], 2 * b + w + 1)
                    copy(part[:, w, 1, h], resid[:, w, h]).then_inc(s["part2_ready"], 1)
            act.wait_ge(s["vpad_ready"], 2)
            for b in range(B):
                act.wait_ge(s["v1_psum"], b + 1)
                v = bank[6 + b].rearrange("p (t h a d) -> p (t h) a d", t=TB, h=HP, a=2)
                dst = vpad[:, b * TB:(b + 1) * TB, :, :].rearrange("p t (h a) c -> p (t h) a c", a=2)
                copy(dst[:, :, 0, 0:DH8], v[:, :, 0, :])
                copy(dst[:, :, 1, W9:W9 + DH8], v[:, :, 1, :]).then_inc(s["vpad_ready"], 1)

            def lno_deviation(b):
                act.wait_ge(s["lno_var"], TB + b)
                act.activation(std[:, TB * b:TB * (b + 1)], mv[:, TB * b:TB * (b + 1), 1], ACT.Sqrt,
                               bias=cst("eps")).then_inc(s["lno_std"], 1)

            for i in range(NPSTEP * (NPAIR + 1) + 2):
                pair, j = divmod(i, NPSTEP)
                if i == NPSTEP * (NPAIR + 1):
                    lno_deviation(0)
                if pair < NPAIR:
                    act.wait_ge(s["t_psum"], i + 1)
                    if pair >= 2:
                        act.wait_ge(s["pv_done"], 2 * (pair - 2) + 1 + i % 2)
                    act.activation(pT[:, pair % 2, i % 2, :, (j // 2) * P:(j // 2 + 1) * P],
                                   bank[4 + i % 2].rearrange("p (k n) -> p k n", k=4), ACT.Exp).then_inc(s["p_ready"], 1)
                if pair >= 2 and j == 1:
                    act.wait_ge(s["pv_done"], 2 * (pair - 1))
                    copy(oT1[:, pair % 2, :], bank[6 + pair % 2]).then_inc(s["oT1_ready"], 1)
            lno_deviation(1)

            norm(4, scale=1.0 + EPS, bias="eps2", apart=True)

            norm(5, apart=True)
            act.wait_ge(s["lgm_ready"], 1)
            act.activation(lg[:, :, :], lg[:, :, :], ACT.Exp).then_inc(s["lge_ready"], 1)
            act.wait_ge(s["sbc_psum"], 1)
            copy(sbc[:, 0:S], bank[5]).then_inc(s["sbc_ready"], 1)

            def copy_ysT(e):
                for b in range(B):
                    act.wait_ge(s["ysT_psum"], 2 * e + b + 1)
                    copy(ysT[:, e % 2, b * S:(b + 1) * S], bank[b]).then_inc(s["ysT_ready"], 1)
            copy_ysT(0)
            for g in range(4 * NE):
                e, u = divmod(g, 4)
                if g == 12:
                    copy_ysT(3)
                if u == 2 and e != 2 and e + 1 < NE:
                    copy_ysT(e + 1)
                act.wait_ge(s["ab_psum"], g + 1)
                if g >= 4:
                    act.wait_ge(s["h_ready"], g - 3)
                act.activation(sg[:, u, :], bank[2 + 2 * (u % 2)], ACT.Silu).then_inc(s["silu_ready"], 1)

        @block.gpsimd
        def _(pool):
            links = [0]

            def link(ins):
                links[0] += 1
                ins.then_inc(s["pool_chain"], 1)
                pool.wait_ge(s["pool_chain"], links[0])

            pool.wait_ge(loaded["const_a"], 16)
            pool.wait_ge(loaded["ctxkT"], 16)
            for b in range(B):
                ins = pool.tensor_tensor(kx_bd[:, b, :, :], ctxkT[:, b, :].unsqueeze(1).to_broadcast([P, HX, SC]),
                                         cst("bd8").unsqueeze(2).to_broadcast([P, HX, SC]), ALU.mult)
            ins.then_inc(s["kx_ready"], 1)
            pool.wait_ge(loaded["ctx"], 16)
            pool.memset(vx[:, :, :, :], 0.0).then_inc(s["vx_ready"], 1)
            pool.wait_ge(s["vx_ready"], 1)
            pool.memset(vx[:, :, :, DX:W17], 1.0)
            pool.tensor_copy(vx[:, :, :, 0:DX], ctx_sb[:, :, D:2 * D].rearrange("p b (h d) -> p b h d", h=HX)).then_inc(s["vx_ready"], 1)
            pool.memset(vpad[:, :, :, :], 0.0).then_inc(s["vpad_ready"], 1)
            pool.wait_ge(s["vpad_ready"], 1)
            ones = vpad[:, :, :, :].rearrange("p t (h a) c -> p (t h) a c", a=2)
            pool.memset(ones[:, :, 0, DH8:W9], 1.0)
            pool.memset(ones[:, :, 1, W9 + DH8:W18], 1.0).then_inc(s["vpad_ready"], 1)
            for t in range(NT):
                pool.wait_ge(s["nmx_ready"], t + 1)
                pool.tensor_tensor(lx[:, t % 3, :, :], lx[:, t % 3, :, :], nmx[:, t % 3, :].unsqueeze(2).to_broadcast([P, HX, SC]),
                                   ALU.add).then_inc(s["lx_ready"], 1)
            for b, m, w in HEADS_BY_POOL:
                pool.wait_ge(parts_stored[b][m], 2 * 16)
                load_heads(pool, b, m, (w,), heads0_by_pool)
            for i in range(NPSTEP * NPAIR):
                if i % NPSTEP not in POOL_STEPS:
                    continue
                pool.wait_ge(s["tw_ready"], i + 1)
                pool.tensor_scalar(tw[:, i % 8, :], tw[:, i % 8, :], tmax[:, i % 8:i % 8 + 1], None,
                                   ALU.subtract).then_inc(s["shifted_pool"], 1)
            pool.wait_ge(s["s_ready"], 1)
            for e in range(NE):
                if e >= 2:
                    pool.wait_ge(s["ysT_psum"], 2 * (e - 1))
                pool.tensor_tensor(ys[:, e % 2, :, :], y[:, :, :], sc8[:, :, e:e + 1].to_broadcast([P, NT, D]),
                                   ALU.mult).then_inc(s["ys_ready"], 1)

        @block.vector
        def _(dve):
            links = [0]

            def link(ins):
                links[0] += 1
                ins.then_inc(s["dve_chain"], 1)
                dve.wait_ge(s["dve_chain"], links[0])

            def stats_of(src, b):
                for t in range(TB * b, TB * b + TB):
                    last = dve.bn_stats(stats[:, t, :], src[:, t, :])
                return last

            def moments(b):
                for t in range(TB * b, TB * b + TB):
                    last = dve.bn_aggr(mv[:, t, :], stats[:, t, :])
                return last

            def norm_stats(b):
                link(stats_of(x, b))
                moments(b).then_inc(var_ready, 1)

            def norm_rows(i, b):
                h = slice(TB * b, TB * (b + 1))
                dve.wait_ge(std_ready, 2 * i + b + 1)
                link(dve.reciprocal(rstd[:, h], std[:, h]))
                for t in range(TB * b, TB * b + TB):
                    dve.tensor_scalar(y[:, t, :], x[:, t, :], mv[:, t, 0:1], rstd[:, t:t + 1], ALU.subtract,
                                      ALU.mult).then_inc(y_ready, 1)

            def quantise(dst, src, inv):
                if inv is not None:
                    link(dve.tensor_scalar(src, src, inv, QMAX, ALU.mult, ALU.min))
                else:
                    link(dve.tensor_scalar(src, src, QMAX, None, ALU.min))
                link(dve.tensor_scalar(src, src, -QMAX - 1.0, MAGIC, ALU.max, ALU.add))
                return dve.tensor_scalar(dst, src, MAGIC, None, ALU.subtract)

            dve.wait_ge(loaded["const_a"], 16)
            dve.wait_ge(loaded["rf"], 16)
            dve.scalar_tensor_tensor(rf_bd[:, :, :], rf[:, :].unsqueeze(1).to_broadcast([P, H16, M_RF]), 1.0 / (2 * math.pi),
                                     cst("bd16").unsqueeze(2).to_broadcast([P, H16, M_RF]), ALU.mult, ALU.mult).then_inc(s["rfbd_ready"], 1)
            dve.tensor_copy(ident_bf[:, :], cst("ident")).then_inc(s["identbf_ready"], 1)
            for b in range(B):
                dve.wait_ge(in_x[b], 16)
                norm_stats(b)
            for b in range(B):
                norm_rows(0, b)
            for t in range(NT):
                dve.wait_ge(s["sq_ready"], t + 1)
                dve.tensor_reduce(nsq[:, t, :], sq[:, t % 2, :].rearrange("p (h d) -> p h d", d=DH8), AX.X, ALU.add).then_inc(s["nsq_ready"], 1)
            dve.wait_ge(s["fexp_ready"], 1)
            link(dve.tensor_scalar(fscale[:, :, :], fscale[:, :, :], M_RF ** -0.5, None, ALU.mult))
            dve.wait_ge(s["v_ready"], NT)
            k_sc = fscale[:, :, H16:2 * H16]
            dve.tensor_tensor(vext0[:, :, :, 0:DH8], v_tok[:, :, :].rearrange("p t (h d) -> p t h d", h=H16),
                              k_sc.unsqueeze(3).to_broadcast([P, NT, H16, DH8]), ALU.mult).then_inc(s["vext_ready"], 1)
            dve.tensor_copy(vext0[:, :, :, DH8:W9], k_sc.unsqueeze(3)).then_inc(s["vext_ready"], 1)

            def kv(b):
                dve.wait_ge(s["kv_psum"], b + 1)
                dve.tensor_tensor(kv_bd[:, b, :, :, :], bank[2 + b][:, 0:2 * FC * 36].rearrange("p (c g d) -> p c g d", g=4, d=W9),
                                  cst("bd4").unsqueeze(1).unsqueeze(3).to_broadcast([P, 2 * FC, 4, W9]), ALU.mult).then_inc(s["kv_ready"], 1)

            def o_parts(b):
                dve.wait_ge(s["qkvo_psum"], b + 1)
                q_sc = fscale[:, TB * b:TB * (b + 1), 0:H16]
                sums = psum[:, 0:2, 0:2 * H16 * W9].rearrange("p a (g d) -> p a g d", d=W9)
                for a in range(2):
                    last = dve.tensor_tensor(zden[:, 2 * a:2 * a + 2, :], sums[:, a, :, DH8].rearrange("p (t h) -> p t h", t=2),
                                             q_sc[:, 2 * a:2 * a + 2, :], ALU.mult)
                link(last)
                link(dve.tensor_scalar(zden[:, :, :], zden[:, :, :], 1e-6, None, ALU.max))
                link(dve.reciprocal(zrec[:, :, :], zden[:, :, :]))
                link(dve.tensor_tensor(zfac[:, :, :], zrec[:, :, :], q_sc, ALU.mult))
                for a in range(2):
                    ins = dve.tensor_tensor(tmp[:, TB * b + 2 * a:TB * b + 2 * a + 2, :].rearrange("p t (h d) -> p (t h) d", h=H16),
                                            sums[:, a, :, 0:DH8],
                                            zfac[:, 2 * a:2 * a + 2, :].rearrange("p t h -> p (t h)").unsqueeze(2).to_broadcast([P, 2 * H16, DH8]),
                                            ALU.mult)
                ins.then_inc(s["o_ready"], 1)

            def whole_turns(u):
                dve.wait_ge(s["proj_psum"], u + 1)
                if u >= 2:
                    dve.wait_ge(s["frac_ready"], u - 1)
                dve.tensor_scalar(turns[:, u % 2, :], bank[4 + u % 4], MAGIC, MAGIC, ALU.add, ALU.subtract).then_inc(s["turns_ready"], 1)

            dve.wait_ge(loaded["lens"], 16)
            dve.wait_ge(loaded["const_b"], 16)
            dve.tensor_copy(ones_bf[:, :], cst("ones", SC)[:, 0:SC])
            dve.tensor_copy(lens_f[:, :], lens_i[:, :]).then_inc(s["len_ready"], 1)
            whole_turns(0)
            dve.wait_ge(s["cs_psum"], 1)
            dve.tensor_scalar(bidx[:, 0, :], bank[3][0:SC, S - B:S], -1.0, None, ALU.add)
            link(dve.tensor_scalar(bidx[:, 1, :], bank[3][0:SC, S - B:S], S - 1.0, None, ALU.add))
            for u in range(16):
                if u >= 3:
                    dve.wait_ge(s["feat_ready"], 2 * (u - 2))
                dve.wait_ge(s["turns_ready"], u + 1)
                dve.tensor_tensor(frac[:, u % 3, :], bank[4 + u % 4], turns[:, u % 2, :], ALU.subtract).then_inc(s["frac_ready"], 1)
                if u + 1 < 16:
                    whole_turns(u + 1)
                dve.wait_ge(s["frac_ready"], u + 1)
                dve.tensor_scalar(fabs[:, u % 3, :].bitcast(I32), frac[:, u % 3, :].bitcast(I32), 0x7FFFFFFF, None,
                                  ALU.bitwise_and).then_inc(s["fabs_ready"], 1)
                if u == 9:
                    kv(0)
                elif u == 13:
                    o_parts(0)
            for b in range(B):
                link(dve.tensor_scalar((bmask, bcum)[b][:, :], cst("iota_l", SC), bidx[:, 0, b:b + 1], None, ALU.is_equal))
                dve.scalar_tensor_tensor(bhit[:, b, :], cst("iota_l", SC), bidx[:, 1, b:b + 1], (bmask, bcum)[b][:, :], ALU.is_equal,
                                         ALU.add).then_inc(s["hit_ready"], 1)
            link(dve.memset(zeros[:, :], 0.0))
            kv(1)

            nw = 2 * NFC * P
            dve.wait_ge(loaded["wgu"], 32)
            dve.tensor_reduce(wmax[:, 0:2 * NFC], wgu[:, 0:nw].rearrange("p (c n) -> p c n", n=P), AX.X, ALU.max, apply_absolute_value=True)
            link(dve.tensor_reduce(wmax[:, 2 * NFC:], wgu[:, nw:], AX.X, ALU.max, apply_absolute_value=True))
            link(dve.tensor_scalar(wscale[:, :], wmax[:, :], 1.0 / QMAX, None, ALU.mult))
            link(dve.reciprocal(winv[:, :], wscale[:, :]))
            dve.tensor_tensor(wgu[:, 0:nw].rearrange("p (c n) -> p c n", n=P), wgu[:, 0:nw].rearrange("p (c n) -> p c n", n=P),
                              winv[:, 0:2 * NFC].unsqueeze(2).to_broadcast([P, 2 * NFC, P]), ALU.mult)
            link(dve.tensor_scalar(wgu[:, nw:], wgu[:, nw:], winv[:, 2 * NFC:], None, ALU.mult))
            quantise(wq_bf[:, :], wgu[:, :], None).then_inc(s["wq_ready"], 1)

            dve.wait_ge(loaded["xmask"], 16)
            dve.wait_ge(loaded["bias0"], 16)
            link(dve.tensor_copy(xmask_f[:, :], xmask_i[:, :]))
            link(dve.tensor_scalar(xmask_f[:, :], xmask_f[:, :], 1.0, 1e30, ALU.subtract, ALU.mult))
            link(dve.tensor_scalar(xbias[:, :, :].rearrange("p b n -> p (b n)"), xmask_f[:, :], bias0[:, 0:1], None, ALU.add))
            dve.wait_ge(loaded["win"], 48)
            for b in range(B):
                dve.wait_ge(s["cnt_psum"], b + 1)
                link(dve.tensor_scalar(bmask[:, :], bank[6 + b][0:SC, :], 1.0, None, ALU.min))
                link(dve.tensor_tensor_scan(bcum[:, :], bmask[:, :], zeros[:, :], 0.0, ALU.add, ALU.add))
                link(dve.tensor_scalar(bcum[:, :], bcum[:, :], -1.0, 0.0, ALU.add, ALU.max))
                link(dve.tensor_scalar(bcum[:, :], bcum[:, :], SC - 1.0, None, ALU.min))
                dve.tensor_scalar(onehot[:, b, :], bcum[:, :], cst("iota_p", SC), None, ALU.is_equal).then_inc(s["onehot_ready"], 1)
            o_parts(1)

            def add_psum(b, first_bank, done):
                xs = x[:, TB * b:TB * (b + 1), :]
                dve.tensor_tensor(xs, xs, bank[first_bank + b].rearrange("p (t d) -> p t d", t=TB), ALU.add).then_inc(done, 1)
            dve.wait_ge(s["wo_psum"], 1)
            add_psum(0, 4, s["x0_ready"])
            dve.wait_ge(s["x0_ready"], 1)
            norm_stats(0)
            dve.wait_ge(s["wdrow_psum"], 1)
            dve.tensor_copy(wdrow[:, :], bank[2][0:1, 0:P]).then_inc(s["wdrow_ready"], 1)
            norm_rows(1, 0)
            dve.wait_ge(s["wo_psum"], 2)
            add_psum(1, 4, s["x0_ready"])
            dve.wait_ge(s["x0_ready"], 2)
            dve.wait_ge(s["wdb_psum"], 1)
            dve.tensor_copy(wdscale[:, :], bank[2][:, P:2 * P]).then_inc(s["wdb_used"], 1)
            norm_stats(1)

            norm_rows(1, 1)

            def x_out(t):
                dve.wait_ge(s["oxt_psum"], t + 1)
                o = bank[t % 2][:, 2 * P:4 * P].rearrange("p (h d) -> p h d", d=32)
                link(dve.reciprocal(xrec[:, :].unsqueeze(2), o[:, :, DX:W17]))
                dve.tensor_tensor(tmp[:, t, :].rearrange("p (h d) -> p h d", h=HX), o[:, :, 0:DX],
                                  xrec[:, :].unsqueeze(2).to_broadcast([P, HX, DX]), ALU.mult).then_inc(s["ox_used"], 1)
                dve.wait_ge(s["ox_used"], t + 1)
                dve.tensor_tensor(x[:, t, :], x[:, t, :], tmp[:, t, :], ALU.add).then_inc(s["x1_ready"], 1)
                dve.wait_ge(s["x1_ready"], t + 1)
                link(dve.bn_stats(stats[:, t, :], x[:, t, :]))
                ins = dve.bn_aggr(mv[:, t, :], stats[:, t, :])
                if t == NT - 1:
                    ins.then_inc(var_ready, 2)

            for t in range(NT):
                dve.wait_ge(s["sx_psum"], t + 1)
                if t >= 3:
                    dve.wait_ge(s["pxT_psum"], t - 2)
                l = lx[:, t % 3, :, :]
                b0 = 2 + 2 * (t % 2)
                dve.tensor_tensor(l.rearrange("p (g h) n -> p g h n", g=2),
                                  psum[:, b0:b0 + 2, 0:4 * SC].rearrange("p g (h n) -> p g h n", n=SC),
                                  xbias[:, t // TB, :].unsqueeze(1).unsqueeze(1).to_broadcast([P, 2, 4, SC]), ALU.add).then_inc(s["sx_read"], 1)
                dve.wait_ge(s["sx_read"], t + 1)
                dve.tensor_reduce(nmx[:, t % 3, :], l, AX.X, ALU.max, negate=True).then_inc(s["nmx_ready"], 1)
                if t >= 3:
                    x_out(t - 3)
            x_out(NT - 3)
            dve.wait_ge(s["clip_exp"], 1)
            link(dve.tensor_scalar(clipf[:, :], clipe[:, :], 1.0, None, ALU.add))
            link(dve.reciprocal(clipf[:, :], clipf[:, :]))
            x_out(NT - 2)
            x_out(NT - 1)

            for b in range(B):
                norm_rows(2, b)

            def scale_of(k, src_bank, ready):
                link(dve.tensor_reduce(gmax[:, k:k + 1], bank[src_bank][0:1, 0:P], AX.X, ALU.max))
                link(dve.tensor_scalar(gsc[:, k, 0:1], gmax[:, k:k + 1], clipf[:, k:k + 1], 1.0 / QMAX, ALU.mult, ALU.mult))
                dve.reciprocal(gsc[:, k, 1:2], gsc[:, k, 0:1]).then_inc(ready, 1)
            dve.wait_ge(y_ready, 3 * NT)
            dve.tensor_reduce(amax[:, 0:1], y[:, :, :], AX.XY, ALU.max, apply_absolute_value=True).then_inc(s["amax_ready"], 1)
            dve.wait_ge(s["amaxT_psum"], 1)
            scale_of(0, 2, s["gsc_ready"])
            dve.wait_ge(s["gscb_psum"], 1)
            dve.tensor_copy(act_sc[:, 0, :], bank[3][:, 0:2]).then_inc(s["act_ready"], 1)
            dve.wait_ge(s["act_ready"], 1)
            dve.tensor_scalar(iscale[:, :], wscale[:, 0:2 * NFC], act_sc[:, 0, 0:1], None, ALU.mult).then_inc(s["act_ready"], 1)
            for b in range(B):
                quantise(xq[:, b * S:(b + 1) * S], y[:, TB * b:TB * (b + 1), :].rearrange("p t d -> p (t d)"),
                         act_sc[:, 0, 1:2]).then_inc(s["xq_ready"], 1)
            dve.wait_ge(s["act_ready"], 2)
            for u in range(2 * NFC):
                b, c = divmod(u, NFC)
                dve.wait_ge(s["sg_ready"], u + 1)
                h = hf[:, c, b * S:(b + 1) * S]
                dve.scalar_tensor_tensor(h, bank[3 + 2 * (u % 3)], iscale[:, NFC + c:NFC + c + 1], sg[:, u % 4, :], ALU.mult,
                                         ALU.mult).then_inc(s["hf_ready"], 1)
                dve.wait_ge(s["hf_ready"], u + 1)
                last = dve.tensor_reduce(hmax[:, u:u + 1], h, AX.X, ALU.max, apply_absolute_value=True)
            link(last)
            dve.tensor_reduce(amax[:, 1:2], hmax[:, :], AX.X, ALU.max).then_inc(s["hmax_ready"], 1)
            dve.wait_ge(s["hmaxT_psum"], 1)
            scale_of(1, 0, s["gsh_ready"])
            dve.wait_ge(s["gshb_psum"], 1)
            link(dve.tensor_copy(act_sc[:, 1, :], bank[1][:, 0:2]))
            for b in range(B):
                quantise(hq[:, :, b * S:(b + 1) * S], hf[:, :, b * S:(b + 1) * S], act_sc[:, 1, 1:2]).then_inc(s["hq_ready"], 1)
            for b in range(B):
                dve.wait_ge(s["down_psum"], b + 1)
                ts_ = tmp[:, TB * b:TB * (b + 1), :]
                xs = x[:, TB * b:TB * (b + 1), :]
                link(dve.scalar_tensor_tensor(ts_, bank[2 + b].rearrange("p (t d) -> p t d", t=TB), act_sc[:, 1, 0:1],
                                              wdscale[:, :].unsqueeze(1).to_broadcast([P, TB, D]), ALU.mult, ALU.mult))
                if b == 1:
                    norm_rows(3, 0)
                dve.tensor_tensor(xs, xs, ts_, ALU.add).then_inc(s["x2_ready"], 1)
                dve.wait_ge(s["x2_ready"], b + 1)
                norm_stats(b)

            norm_rows(3, 1)
            for b in range(B):
                h = slice(b * S, (b + 1) * S)
                for w in range(2):
                    dve.wait_ge(s["part1_ready"], 2 * b + w + 1)
                    dve.tensor_tensor(resid[:, w, h], bank[2 + 2 * b + w], part[:, w, 0, h], ALU.subtract).then_inc(s["resid1_ready"], 1)
                for w in range(2):
                    dve.wait_ge(s["part2_ready"], 2 * b + w + 1)
                    dve.tensor_tensor(part[:, w, 2, h], resid[:, w, h], part[:, w, 1, h], ALU.subtract).then_inc(s["part3_ready"], 1)

            dve.wait_ge(s["cstd_ready"], 1)
            link(dve.reciprocal(csum[:, :], csum[:, :]))
            for b in range(B):
                link(dve.tensor_scalar(upd[:, b, :], ctx_sb[:, b, 0:D], csum[:, b:b + 1], BCOEF, ALU.mult, ALU.mult))
                last = dve.tensor_tensor(upd[:, b, :], upd[:, b, :], ginit[:, :], ALU.mult)
            last.then_inc(s["upd_ready"], 1)
            dve.wait_ge(s["dep_psum"], 1)
            dve.tensor_copy(depool[:, :, :], bank[1][0:SC, 0:B * D].rearrange("p (b d) -> p b d", b=B)).then_inc(s["dep_ready"], 1)
            dve.tensor_scalar(win[:, :], win[:, :], gres[:, 0:1], None, ALU.mult).then_inc(s["wing_ready"], 1)

            def divide(pair):
                b, hp = divmod(pair, HP)
                dve.wait_ge(s["o_psum"], pair + 1)
                o = bank[6 + pair % 2][:, 0:TB * W18].rearrange("p (t a d) -> p t a d", t=TB, a=2)
                den = nsq[:, TB * b:TB * (b + 1), 2 * hp:2 * hp + 2]
                link(dve.reciprocal(den.unsqueeze(3), o[:, :, :, DH8:W9]))
                dve.tensor_tensor(tmp[:, TB * b:TB * (b + 1), 2 * DH8 * hp:2 * DH8 * (hp + 1)].rearrange("p t (a d) -> p t a d", a=2),
                                  o[:, :, :, 0:DH8], den.unsqueeze(3).to_broadcast([P, TB, 2, DH8]), ALU.mult).then_inc(s["out1_ready"], 1)

            def times_gamma(t):
                return dve.scalar_tensor_tensor(tmp[:, t, :], tmp[:, t, :], mv[:, t, 0:1], gamma[:, :], ALU.subtract, ALU.mult)

            def add_normed(b):
                h = slice(TB * b, TB * (b + 1))
                for t in range(TB * b, TB * b + TB):
                    last = dve.scalar_tensor_tensor(tmp[:, t, :], tmp[:, t, :], rstd[:, t:t + 1], beta[:, :], ALU.mult, ALU.add)
                link(last)
                dve.tensor_tensor(x[:, h, :], x[:, h, :], tmp[:, h, :], ALU.add).then_inc(s["x3_ready"], 1)

            def lno_rstd(b):
                dve.wait_ge(s["lno_std"], b + 1)
                link(dve.reciprocal(rstd[:, TB * b:TB * (b + 1)], std[:, TB * b:TB * (b + 1)]))

            for i in range(NPSTEP * NPAIR + 1):
                pair, j = divmod(i, NPSTEP)
                if 2 <= pair < NPAIR and j == 7:
                    divide(pair - 2)
                t = pair - HP - 2
                if 0 <= t < TB and j == 3:
                    dve.wait_ge(s["out1_ready"], HP)
                    link(dve.bn_stats(stats[:, t, :], tmp[:, t, :]))
                    dve.bn_aggr(mv[:, t, :], stats[:, t, :]).then_inc(s["lno_var"], 1)
                if 0 <= t < TB and j == 5:
                    dve.wait_ge(s["lno_var"], t + 1)
                    if t == 0:
                        dve.wait_ge(loaded["gb"], 32)
                    times_gamma(t)
                if i < NPSTEP * NPAIR:
                    dve.wait_ge(s["scores_psum"], i + 1)
                    if i >= 8:
                        dve.wait_ge(s["t_psum"], i - 7)
                    at = (S - P) - ((i % NPSTEP) // 2) * P
                    dve.tensor_tensor_reduce(out=tw[:, i % 8, :], in0=bank[i % 4], in1=cst("dist")[:, at:at + S], scale=1.0,
                                             scalar=-3.0e38, op0=ALU.mult, op1=ALU.max,
                                             accum_out=tmax[:, i % 8:i % 8 + 1]).then_inc(s["tw_ready"], 1)
                if i >= 1 and (i - 1) % NPSTEP not in POOL_STEPS:
                    o = (i - 1) % 8
                    dve.wait_ge(s["tw_ready"], i)
                    dve.tensor_scalar(tw[:, o, :], tw[:, o, :], tmax[:, o:o + 1], None, ALU.subtract).then_inc(s["shifted_dve"], 1)
            divide(NPAIR - 2)
            lno_rstd(0)
            add_normed(0)
            divide(NPAIR - 1)
            dve.wait_ge(s["out1_ready"], NPAIR)
            link(stats_of(tmp, 1))
            moments(1).then_inc(s["lno_var"], 1)
            dve.wait_ge(s["x3_ready"], 1)
            norm_stats(0)
            lno_rstd(1)
            for t in range(TB, NT):
                last = times_gamma(t)
            link(last)
            norm_rows(4, 0)
            add_normed(1)
            dve.wait_ge(s["x3_ready"], 2)
            norm_stats(1)

            norm_rows(4, 1)
            for b in range(B):
                dve.wait_ge(s["e_psum"], b + 1)
                add_psum(b, 2, s["x4_ready"])
                dve.wait_ge(s["x4_ready"], b + 1)
                norm_stats(b)
                norm_rows(5, b)

            dve.tensor_copy(group_bf[:, :], cst("group"))
            dve.wait_ge(s["lg_psum"], 1)
            lgp = bank[2][:, 0:NT * NE].rearrange("p (t e) -> p t e", e=NE)
            link(dve.tensor_reduce(smx[:, :], lgp, AX.X, ALU.max))
            dve.tensor_tensor(lg[:, :, :], lgp, smx[:, :].unsqueeze(2).to_broadcast([P, NT, NE]), ALU.subtract).then_inc(s["lgm_ready"], 1)
            dve.wait_ge(s["lge_ready"], 1)
            link(dve.tensor_reduce(smx[:, :], lg[:, :, :], AX.X, ALU.add))
            link(dve.reciprocal(smx[:, :], smx[:, :]))
            dve.tensor_tensor(sc8[:, :, :], lg[:, :, :], smx[:, :].unsqueeze(2).to_broadcast([P, NT, NE]), ALU.mult).then_inc(s["s_ready"], 1)
            dve.wait_ge(s["s_ready"], 1)
            dve.tensor_copy(sc16[:, :, :].rearrange("p t (e j) -> p (t e) j", j=SEL_J),
                            sc8[:, :, :].rearrange("p t e -> p (t e)").unsqueeze(2).to_broadcast([P, NT * NE, SEL_J])).then_inc(s["s16_ready"], 1)
            dve.wait_ge(s["sbc_psum"], 2)
            dve.tensor_copy(sbc[:, S:2 * S], bank[6]).then_inc(s["sbc_ready"], 1)
            dve.wait_ge(s["sbc_ready"], 2)
            dve.wait_ge(loaded["jbits"], 16)
            link(dve.memset(thr[:, :], 0))

            def h_product(g):
                e, u = divmod(g, 4)
                c, b = divmod(u, 2)
                dve.wait_ge(s["silu_ready"], g + 1)
                if u == 0 and e >= 3:
                    dve.wait_ge(s["w2_psum"], 2 * (e - 2))
                dve.tensor_tensor(hmoe[:, e % 3, c, b * S:(b + 1) * S], bank[3 + 2 * (u % 2)], sg[:, u, :], ALU.mult).then_inc(s["h_ready"], 1)

            def add_expert(e):
                for b in range(B):
                    dve.wait_ge(s["w2_psum"], 2 * e + b + 1)
                    if b == 0 and e >= 1:
                        dve.wait_ge(s["acc_done"], 2 * e)
                    for t in range(TB * b, TB * b + TB):
                        ins = dve.scalar_tensor_tensor(x[:, t, :], bank[6 + b][:, (t % TB) * D:(t % TB + 1) * D], smask[:, t, e:e + 1],
                                                       x[:, t, :], ALU.mult, ALU.add)
                    ins.then_inc(s["acc_done"], 1)

            for r, sh in enumerate(SEL_SHIFTS):
                link(dve.tensor_tensor(cand[:, :], thr[:, :], jbits[:, r:r + 1], ALU.bitwise_or))
                link(dve.tensor_scalar(selw[:, 0, :], sbc[:, :], cand[:, :].bitcast(F32), None, ALU.is_ge, ALU.add, accum_out=cnt[:, 0:1]))
                dve.tensor_scalar(flag[:, :], cnt[:, 0:1], float(CAP), 2.0 ** sh, ALU.is_ge, ALU.mult).then_inc(s["flag_ready"], 1)
                h_product(r)
                dve.wait_ge(s["digit_psum"], r + 1)
                link(dve.tensor_scalar(digit[:, :], bank[7][:, r:r + 1], -2.0 ** max(sh, 0), None, ALU.add))
                link(dve.tensor_tensor(thr[:, :], thr[:, :], digit[:, :], ALU.bitwise_or))
            tf = thr[:, :].bitcast(F32)
            link(dve.tensor_scalar(selw[:, 0, :], sbc[:, :], tf, None, ALU.is_gt, ALU.add, accum_out=cnt[:, 1:2]))
            dve.tensor_scalar(need[:, :], cnt[:, 1:2], -1.0, float(CAP), ALU.mult, ALU.add)
            h_product(8)
            link(dve.tensor_scalar(selw[:, 1, :], sbc[:, :], tf, None, ALU.is_equal))
            link(dve.tensor_tensor_scan(selw[:, 2, :], selw[:, 1, :], selw[:, 1, :], 0.0, ALU.add, ALU.max))
            h_product(9)
            link(dve.scalar_tensor_tensor(selw[:, 1, :], selw[:, 2, :], need[:, 0:1], selw[:, 1, :], ALU.is_le, ALU.mult))
            dve.tensor_tensor(selmask[:, :], selw[:, 0, :], selw[:, 1, :], ALU.add).then_inc(s["selmask_ready"], 1)
            h_product(10)
            h_product(11)
            dve.wait_ge(s["smaskT_psum"], 1)
            dve.tensor_copy(smask[:, :, :].rearrange("p (a t) e -> p a t e", a=2),
                            psum[:, 0:2, :].rearrange("p a (t e j) -> p a t e j", e=NE, j=SEL_J)[:, :, :, :, 0]).then_inc(s["smask_ready"], 1)
            dve.wait_ge(s["smask_ready"], 1)
            add_expert(0)
            for e in range(3, NE):
                h_product(4 * e)
                h_product(4 * e + 1)
                add_expert(1 if e == 3 else e - 1)
                h_product(4 * e + 2)
                h_product(4 * e + 3)
                if e == 3:
                    add_expert(2)
            add_expert(NE - 1)


def kernel(**inputs):
    a = {k: np.asarray(v) for k, v in inputs.items()}
    import concourse.bacc as bacc
    from concourse.bass_utils import run_bass_kernel_spmd

    def pad_rows(w):
        return np.concatenate([w, w[:NFC * P - FF]], axis=0)
    jb = np.zeros((P, len(SEL_SHIFTS)), np.int32)
    for r, sh in enumerate(SEL_SHIFTS):
        j = np.arange(P) % SEL_J
        jb[:, r] = j << sh if sh >= 0 else j >> -sh
    data = {
        "x": a["x"],
        "ctx": a["ctx_2048"],
        "ctxkT": a["ctx_2048"][:, :, :D].transpose(2, 0, 1),
        "xmask": a["mask_BxS2_ik0"].reshape(-1),
        "lens": a["mask_BxS2_if0"].T,
        "wqkv0": np.concatenate([a["L0_attn_wq"].T, a["L0_attn_wk"].T, a["L0_attn_wv"].T], axis=1),
        "wqk0": np.stack([a["L0_attn_wq"], a["L0_attn_wk"]], axis=1),
        "wo0": a["L0_attn_wo"].T,
        "rf": np.tile(a["L0_attn_rf"].T, (H16, 1)),
        "bias0": a["L0_xattn_b"],
        "clips": np.stack([a["L0_ffn_clip_x"], a["L0_ffn_clip_down"]], axis=1),
        "wgu": np.concatenate([pad_rows(a["L0_ffn_w_gate"]), pad_rows(a["L0_ffn_w_up"])], axis=0),
        "wd": a["L0_ffn_w_down"],
        "wqkv1": np.concatenate([a["L1_attn_Wq"].T, a["L1_attn_Wk"].T, a["L1_attn_Wv"].T], axis=1),
        "gamma": a["L1_attn_ln_gamma"],
        "beta": a["L1_attn_ln_beta"],
        "win": a["L1_xattn_W_in"].T,
        "bin": a["L1_xattn_b_in"],
        "gres": a["L1_xattn_g_res"][:, None],
        "ginit": a["L1_xattn_g_init"],
        "wg": a["L1_ffn_wg"],
        "w1": a["L1_ffn_w1"],
        "w3": a["L1_ffn_w3"],
        "w2": a["L1_ffn_w2"],
        "const": constants(),
        "jbits": jb,
    }
    nc = bacc.Bacc("TRN2", target_bir_lowering=False, num_devices=1)
    arrays, args = {}, []
    for name, v in data.items():
        v = np.ascontiguousarray(v)
        arrays["in_" + name] = v
        args.append(nc.dram_tensor("in_" + name, v.shape, mybir.dt.from_np(v.dtype), kind="ExternalInput").ap())
    res = nc.dram_tensor("out_x", (B, S, D), F32, kind="ExternalOutput").ap()
    parts = nc.dram_tensor("qk_parts", (B, 2, 3, 2, DH8, HP, S), BF16, kind="Internal").ap()
    build(nc, *args, res, parts)
    r = run_bass_kernel_spmd(nc, [arrays], core_ids=[0])
    return r.results[0]["out_x"]
```
